# Optimizing a Trainium2 kernel written in Bass

```python
import numpy as np
import jax
import jax.numpy as jnp

def _softmax(x, axis=-1):
    return jax.nn.softmax(x, axis=axis)

def _gelu(x):
    return jax.nn.gelu(x, approximate=True)

def _silu(x):
    return jax.nn.silu(x)

def _sigmoid(x):
    return jax.nn.sigmoid(x)

def _layernorm(x, axis=-1, eps=1e-05):
    m = jnp.mean(x, axis=axis, keepdims=True)
    v = jnp.var(x, axis=axis, keepdims=True)
    return (x - m) / jnp.sqrt(v + eps)

def _scatter_add(tgt, idx, src, axis=0):
    return tgt.at[idx].add(src)

def _segment_sum(src, seg, n):
    return jax.ops.segment_sum(src, seg, n)
kernel_name = 'mk_xattn_seq_d1_seqx_r2_59d396'

def setup_inputs(seed: int=0):
    np.random.seed(seed)
    _w = jnp.asarray

    def _rec_inputs():
        import jax
        import jax.numpy as jnp
        _rk = jax.random.key(seed)
        x = -0.0001548 + 1 * jax.random.normal(jax.random.fold_in(_rk, 1), (16, 100, 640), jnp.float32)
        _lenS = 100 - jax.random.randint(jax.random.fold_in(_rk, 7), (16,), 0, max(1, 100 // 4) + 1, jnp.int32)
        _lenS2 = 722 - jax.random.randint(jax.random.fold_in(_rk, 8), (16,), 0, max(1, 722 // 4) + 1, jnp.int32)
        _ctx_768P = jax.random.normal(jax.random.fold_in(_rk, 11), (16, 16, 384), jnp.float32)
        _ctx_768c = jax.random.dirichlet(jax.random.fold_in(_rk, 511), 0.3 * jnp.ones((16,), jnp.float32), (16, 722))
        _ctx_768t = jnp.einsum('bsk,bkd->bsd', _ctx_768c, _ctx_768P)
        _ctx_768t = _ctx_768t * jax.lax.rsqrt(jnp.mean(jnp.square(_ctx_768t)) + 1e-12) * 0.953939
        ctx_768 = 0.00141353 + 0.998943 * (_ctx_768t + 0.3 * jax.random.normal(jax.random.fold_in(_rk, 611), (16, 722, 384), jnp.float32))
        return (x, ctx_768)
    x, ctx_768 = _rec_inputs()

    def _L0_xattn_setup():
        import jax, jax.numpy as jnp
        import numpy as np
        HEADS = 8
        NUM_TOKENS = 4
        CROSS_ATTENTION_DIM = 384

        def _mha(q, k, v, heads=HEADS):
            B, Sq, H = q.shape
            Sk = k.shape[1]
            d = H // heads
            qh = q.reshape(B, Sq, heads, d).transpose(0, 2, 1, 3)
            kh = k.reshape(B, Sk, heads, d).transpose(0, 2, 1, 3)
            vh = v.reshape(B, Sk, heads, d).transpose(0, 2, 1, 3)
            scores = jnp.einsum('bhqd,bhkd->bhqk', qh, kh) * jnp.asarray(d, q.dtype) ** (-0.5)
            probs = jax.nn.softmax(scores, axis=-1)
            out = jnp.einsum('bhqk,bhkd->bhqd', probs, vh)
            return out.transpose(0, 2, 1, 3).reshape(B, Sq, H)
        key = jax.random.key(seed)
        ks = jax.random.split(key, 10)
        B, S, H, CAD, T = (4, 512, 640, CROSS_ATTENTION_DIM, NUM_TOKENS)
        sc = 0.02
        return {'hidden_states': jax.random.normal(ks[0], (B, S, H), jnp.float32), 'encoder_hidden_states': jax.random.normal(ks[1], (B, 77 + T, CAD), jnp.float32), 'Wq': jax.random.normal(ks[2], (H, H), jnp.float32) * sc, 'Wk': jax.random.normal(ks[3], (CAD, H), jnp.float32) * sc, 'Wv': jax.random.normal(ks[4], (CAD, H), jnp.float32) * sc, 'Wq_ca': jax.random.normal(ks[5], (T, H), jnp.float32) * sc, 'Wk_ca': jax.random.normal(ks[6], (CAD, H), jnp.float32) * sc, 'Wv_ca': jax.random.normal(ks[7], (CAD, H), jnp.float32) * sc, 'Wout': jax.random.normal(ks[8], (H, H), jnp.float32) * sc, 'b_out': jnp.zeros((H,), jnp.float32)}
    _L0_xattn_all = _L0_xattn_setup()
    _L0_xattn_in = {k: v for k, v in _L0_xattn_all.items() if k in ('Wq', 'Wk', 'Wv', 'Wq_ca', 'Wk_ca', 'Wv_ca', 'Wout', 'b_out')}
    del _L0_xattn_all
    return {'x': x, 'ctx_768': ctx_768, 'L0_xattn_Wq': _L0_xattn_in['Wq'], 'L0_xattn_Wk': _L0_xattn_in['Wk'], 'L0_xattn_Wv': _L0_xattn_in['Wv'], 'L0_xattn_Wq_ca': _L0_xattn_in['Wq_ca'], 'L0_xattn_Wk_ca': _L0_xattn_in['Wk_ca'], 'L0_xattn_Wv_ca': _L0_xattn_in['Wv_ca'], 'L0_xattn_Wout': _L0_xattn_in['Wout'], 'L0_xattn_b_out': _L0_xattn_in['b_out']}

def reference(x, ctx_768, L0_xattn_Wq, L0_xattn_Wk, L0_xattn_Wv, L0_xattn_Wq_ca, L0_xattn_Wk_ca, L0_xattn_Wv_ca, L0_xattn_Wout, L0_xattn_b_out):
    import jax
    import jax.numpy as jnp

    def _L0_xattn_ref(hidden_states, encoder_hidden_states, Wq, Wk, Wv, Wq_ca, Wk_ca, Wv_ca, Wout, b_out):
        import jax, jax.numpy as jnp
        import numpy as np
        HEADS = 8
        NUM_TOKENS = 4
        CROSS_ATTENTION_DIM = 384

        def _mha(q, k, v, heads=HEADS):
            B, Sq, H = q.shape
            Sk = k.shape[1]
            d = H // heads
            qh = q.reshape(B, Sq, heads, d).transpose(0, 2, 1, 3)
            kh = k.reshape(B, Sk, heads, d).transpose(0, 2, 1, 3)
            vh = v.reshape(B, Sk, heads, d).transpose(0, 2, 1, 3)
            scores = jnp.einsum('bhqd,bhkd->bhqk', qh, kh) * jnp.asarray(d, q.dtype) ** (-0.5)
            probs = jax.nn.softmax(scores, axis=-1)
            out = jnp.einsum('bhqk,bhkd->bhqd', probs, vh)
            return out.transpose(0, 2, 1, 3).reshape(B, Sq, H)
        residual = hidden_states
        unet_size = residual.shape[1]
        end_pos = encoder_hidden_states.shape[1] - NUM_TOKENS
        enc = encoder_hidden_states[:, :end_pos, :]
        ca = encoder_hidden_states[:, end_pos:, :]
        query = hidden_states @ Wq
        keyt = enc @ Wk
        valt = enc @ Wv
        hs = _mha(query, keyt, valt)
        ca_q1 = jnp.einsum('btc,th->bch', ca, Wq_ca)
        indices = np.linspace(0, CROSS_ATTENTION_DIM - 1, unet_size).astype(np.int64)
        ca_q1 = ca_q1[:, indices, :]
        ca_hs1 = _mha(ca_q1, residual, residual)
        ca_q2 = ca_hs1 @ Wq
        ca_k2 = ca @ Wk_ca
        ca_v2 = ca @ Wv_ca
        ca_hs2 = _mha(ca_q2, ca_k2, ca_v2)
        out = hs + ca_hs2
        out = out @ Wout + b_out
        out = out + residual
        return out
    x = _L0_xattn_ref(x, ctx_768, L0_xattn_Wq, L0_xattn_Wk, L0_xattn_Wv, L0_xattn_Wq_ca, L0_xattn_Wk_ca, L0_xattn_Wv_ca, L0_xattn_Wout, L0_xattn_b_out)
    return x

_drawn_inputs = setup_inputs


def setup_inputs(seed=0):
    import zlib

    import numpy as np

    out = dict(_drawn_inputs(seed))
    spreads = {'L0_xattn_b_out': (0.0, 0.1)}
    factors = {'L0_xattn_Wq': 8.0, 'L0_xattn_Wk': 8.0, 'L0_xattn_Wq_ca': 8.0, 'L0_xattn_Wk_ca': 8.0}
    for name, (base, spread) in spreads.items():
        noise = np.random.default_rng([zlib.crc32(name.encode()), seed]).standard_normal(out[name].shape)
        drawn = base * np.exp(spread * noise) if base else spread * noise
        out[name] = jnp.asarray(drawn.astype(out[name].dtype))
    for name, factor in factors.items():
        out[name] = (out[name] * factor).astype(out[name].dtype)
    return out
```

```python
from contextlib import ExitStack

import concourse.bass as bass
from concourse import mybir

F32 = mybir.dt.float32
F32R = mybir.dt.float32r
ALU = mybir.AluOpType
ACT = mybir.ActivationFunctionType
AX = mybir.AxisListType

B, S, H = 16, 100, 640
HEADS = 8
D = H // HEADS
C = 384
T = 4
KEYS = 722 - T
NT = B * S
R = HEADS * S
HT = HEADS * T
SCALE = float(D) ** -0.5

CT = C // 128
FT = H // 128
KT = 6
KP = (KEYS + KT - 1) // KT
KPAD = KT * KP
HALF = KPAD // 2
MT = (R + 127) // 128
RH = R // 2
GT = 4 * S
STK = 3 * D // 2
EX = STK - D


def rows(m):
    return min(128, R - 128 * m)


def raw(ap):
    return ap.bitcast(F32)


def wait_apart(eng, sem, value, passed):
    eng.wait_ge(sem, value)
    eng.sem_inc(passed, 1)


def products(a, b):
    return ((a[0], b[0]), (a[0], b[1]), (a[1], b[0]))


def build(nc, x, xT, encT, encN, caT, asel, Wq, WqT, WkT, Wv, WqcaBD, Wkca, Wvca, Wout, bout, out):
    q_d = nc.dram_tensor("q_split", [2, H, NT], F32R).ap()
    g_d = nc.dram_tensor("g_split", [2, HT, NT], F32R).ap()
    wk_d = nc.dram_tensor("wk_split", [2, H, C], F32R).ap()
    wo_d = nc.dram_tensor("wo_split", [2, 128, FT * H], F32R).ap()
    v2_d = nc.dram_tensor("v2_split", [2, B, T, H], F32R).ap()
    m_d = nc.dram_tensor("m_split", [2, B, D, HEADS * HT], F32R).ap()
    hs_d = nc.dram_tensor("hs_split", [2, H, NT], F32R).ap()
    with ExitStack() as keep:
        Wv_s = [keep.enter_context(nc.sbuf_tensor(f"Wv_{p}", [128, CT, H], F32R)) for p in "hl"]
        ident = keep.enter_context(nc.sbuf_tensor("ident", [128, 128], F32))
        headmask = keep.enter_context(nc.sbuf_tensor("headmask", [HT, HEADS], F32))
        wbig = keep.enter_context(nc.sbuf_tensor("wbig", [128, 2, FT * H], F32R))
        prepare_weights(nc, wbig, Wv_s, ident, headmask, caT, WqT, WkT, Wv, Wkca, Wvca, Wout,
                        wk_d, wo_d, v2_d, m_d)
        project_queries(nc, xT, Wq, WqcaBD, q_d, g_d)
        attend(nc, Wv_s, ident, headmask, wbig, x, encT, encN, asel, q_d, g_d, wk_d, wo_d, v2_d, m_d, hs_d)
        project_out(nc, wbig, x, bout, hs_d, out)


def prepare_weights(nc, wbig, Wv_s, ident, headmask, caT, WqT, WkT, Wv, Wkca, Wvca, Wout,
                    wk_d, wo_d, v2_d, m_d):
    with ExitStack() as ctx:
        def sb(name, shape, dt=F32):
            return ctx.enter_context(nc.sbuf_tensor(name, shape, dt))

        def sem(name):
            return ctx.enter_context(nc.semaphore(name))

        shapes = {
            "caT": ([128, CT, B * T], caT.rearrange("(c p) n -> p c n", p=128)),
            "Wkca": ([128, CT, H], Wkca.rearrange("(c p) n -> p c n", p=128)),
            "WqT": ([D, HEADS, H], WqT.rearrange("(h d) n -> d h n", d=D)),
            "Wvca": ([128, CT, H], Wvca.rearrange("(c p) n -> p c n", p=128)),
            "WkT": ([128, FT, C], WkT.rearrange("(c p) n -> p c n", p=128)),
            "Wv": ([128, CT, H], Wv.rearrange("(c p) n -> p c n", p=128)),
            "Wout": ([128, FT, H], Wout.rearrange("(c p) n -> p c n", p=128)),
        }
        order = list(shapes)
        RING = 2
        size = max(s[1] * s[2] for s, _ in shapes.values())
        raws = [sb(f"raw{j}", [128, size]) for j in range(RING)]
        split = {}
        for n in order:
            s = shapes[n][0]
            if n == "Wv":
                split[n] = [w[:, :, :] for w in Wv_s]
            elif n == "WkT":
                split[n] = [w.rearrange("p a b -> p (a b)").rearrange("p (a b) -> p a b", a=FT)
                            for w in split["Wkca"]]
            elif n == "Wout":
                split[n] = [wbig[:, p, :].rearrange("p (a b) -> p a b", a=FT) for p in range(2)]
            else:
                split[n] = [sb(f"{n}_{p}", s, F32R)[:, :, :] for p in "hl"]
        k2T = [sb(f"k2T_{p}", [D, HEADS, B * T], F32R) for p in "hl"]
        v2 = [sb(f"v2_{p}", [B * T, H], F32R) for p in "hl"]
        M = [sb(f"M_{p}", [D, B, HEADS, HT], F32R) for p in "hl"]

        psum = [ctx.enter_context(nc.psum_tensor(f"psw{j}", [128, 512], F32)) for j in range(4)]
        s_raw = [sem(f"s_raw{j}") for j in range(RING)]
        s_hi, s_lo = sem("s_hi"), sem("s_lo")
        s_const = sem("s_const")
        s_k2, s_k2hi, s_k2lo = sem("s_k2"), sem("s_k2hi"), sem("s_k2lo")
        s_v2, s_v2hi, s_v2lo = sem("s_v2"), sem("s_v2hi"), sem("s_v2lo")
        s_m, s_mhi, s_mlo = sem("s_m"), sem("s_mhi"), sem("s_mlo")
        s_st = sem("s_st")
        STORES = 8

        def rawview(n):
            s = shapes[n][0]
            return raws[order.index(n) % RING][0:s[0], 0:s[1] * s[2]].rearrange("p (a b) -> p a b", a=s[1])

        with nc.Block() as block:
            @block.sync
            def _(sp):
                for k, n in enumerate(order):
                    if k >= RING:
                        sp.wait_ge(s_lo, k - RING + 1)
                    sp.dma_start(rawview(n), shapes[n][1]).then_inc(s_raw[k % RING], 16)
                sp.wait_ge(s_v2lo, 2)
                for p in range(2):
                    sp.dma_start(raw(v2_d[p].rearrange("b t n -> (b t) n")), raw(v2[p][:, :])).then_inc(s_st, 16)
                sp.wait_ge(s_lo, order.index("WkT") + 1)
                for p in range(2):
                    sp.dma_start(raw(wk_d[p].rearrange("(c p) n -> p c n", p=128)),
                                 raw(split["WkT"][p])).then_inc(s_st, 16)
                sp.wait_ge(s_lo, order.index("Wout") + 1)
                for p in range(2):
                    sp.dma_start(raw(wo_d[p]),
                                 raw(split["Wout"][p].rearrange("p a b -> p (a b)"))).then_inc(s_st, 16)
                sp.wait_ge(s_mlo, HEADS)
                for p in range(2):
                    sp.dma_start(raw(m_d[p].rearrange("b d n -> d b n")),
                                 raw(M[p][:, :, :, :].rearrange("d b a n -> d b (a n)"))).then_inc(s_st, 16)
                sp.wait_ge(s_st, 16 * STORES)

            @block.gpsimd
            def _(pool):
                nc.gpsimd.memset(ident[:, :], 0.0).then_inc(s_const, 1)
                nc.gpsimd.memset(headmask[:, :], 1.0).then_inc(s_const, 1)
                pool.wait_ge(s_const, 2)
                nc.gpsimd.affine_select(out=ident[:, :], in_=ident[:, :], compare_op=ALU.not_equal, fill=1.0,
                                        base=0, pattern=[[-1, 128]], channel_multiplier=1).then_inc(s_const, 1)
                nc.gpsimd.affine_select(out=headmask[:, :], in_=headmask[:, :], compare_op=ALU.is_ge, fill=0.0,
                                        base=0, pattern=[[-T, HEADS]], channel_multiplier=1).then_inc(s_const, 1)
                pool.wait_ge(s_const, 4)
                nc.gpsimd.affine_select(out=headmask[:, :], in_=headmask[:, :], compare_op=ALU.is_ge, fill=0.0,
                                        base=T - 1, pattern=[[T, HEADS]], channel_multiplier=-1).then_inc(s_const, 1)

            def m_view(p, h1):
                return M[p][:, :, h1, :].rearrange("d b (h t) -> d h b t", h=HEADS)

            def ps_m(h1):
                return psum[h1 % 4][0:D, :].rearrange("d (h b t) -> d h b t", h=HEADS, b=B)

            @block.scalar
            def _(act):
                def high(k):
                    n = order[k]
                    act.wait_ge(s_raw[k % RING], 16 * (k // RING + 1))
                    nc.scalar.activation(split[n][0], rawview(n), ACT.Copy).then_inc(s_hi, 1)

                for k in range(3):
                    high(k)
                act.wait_ge(s_k2, 1)
                nc.scalar.activation(k2T[0][:, :, :], psum[0][0:D, :].rearrange("d (h n) -> d h n", h=HEADS),
                                     ACT.Copy, scale=SCALE).then_inc(s_k2hi, 1)
                high(3)
                for j in range(2):
                    act.wait_ge(s_v2, j + 1)
                    nc.scalar.activation(v2[0][:, j * 320:(j + 1) * 320], psum[2 + j][0:B * T, 0:320],
                                         ACT.Copy).then_inc(s_v2hi, 1)
                for k in range(4, len(order)):
                    high(k)
                for h1 in range(HEADS):
                    act.wait_ge(s_m, h1 + 1)
                    nc.scalar.activation(m_view(0, h1), ps_m(h1), ACT.Copy).then_inc(s_mhi, 1)

            @block.vector
            def _(dve):
                def low(k):
                    n = order[k]
                    dve.wait_ge(s_hi, k + 1)
                    nc.vector.tensor_tensor(split[n][1], rawview(n), split[n][0], ALU.subtract).then_inc(s_lo, 1)

                for k in range(3):
                    low(k)
                dve.wait_ge(s_k2hi, 1)
                nc.vector.scalar_tensor_tensor(out=k2T[1][:, :, :].rearrange("d h n -> d (h n)"), in0=psum[0][0:D, :],
                                               scalar=SCALE, in1=k2T[0][:, :, :].rearrange("d h n -> d (h n)"),
                                               op0=ALU.mult, op1=ALU.subtract).then_inc(s_k2lo, 1)
                low(3)
                for j in range(2):
                    cols = slice(j * 320, (j + 1) * 320)
                    dve.wait_ge(s_v2hi, j + 1)
                    nc.vector.tensor_tensor(v2[1][:, cols], psum[2 + j][0:B * T, 0:320], v2[0][:, cols],
                                            ALU.subtract).then_inc(s_v2lo, 1)
                for k in range(4, len(order)):
                    low(k)
                for h1 in range(HEADS):
                    dve.wait_ge(s_mhi, h1 + 1)
                    nc.vector.tensor_tensor(m_view(1, h1), ps_m(h1), m_view(0, h1), ALU.subtract).then_inc(s_mlo, 1)

            @block.tensor
            def _(pe):
                pe.wait_ge(s_lo, order.index("Wkca") + 1)
                for h in range(HEADS):
                    n = 0
                    for c in range(CT):
                        for w, a in products(split["Wkca"], split["caT"]):
                            mm = pe.matmul(psum[0][0:D, h * B * T:(h + 1) * B * T], w[:, c, h * D:(h + 1) * D],
                                           a[:, c, :], start=(n == 0), stop=(n == 3 * CT - 1))
                            n += 1
                mm.then_inc(s_k2, 1)
                pe.wait_ge(s_lo, order.index("Wvca") + 1)
                for j in range(2):
                    n = 0
                    for c in range(CT):
                        for a, w in products(split["caT"], split["Wvca"]):
                            mm = pe.matmul(psum[2 + j][0:B * T, 0:320], a[:, c, :], w[:, c, j * 320:(j + 1) * 320],
                                           start=(n == 0), stop=(n == 3 * CT - 1))
                            n += 1
                    mm.then_inc(s_v2, 1)
                pe.wait_ge(s_k2lo, 1)
                pe.wait_ge(s_v2lo, 2)
                for h1 in range(HEADS):
                    if h1 >= 4:
                        pe.wait_ge(s_mlo, h1 - 3)
                    for h in range(HEADS):
                        for n, (w, k) in enumerate(products(split["WqT"], k2T)):
                            mm = pe.matmul(psum[h1 % 4][0:D, h * B * T:(h + 1) * B * T],
                                           w[:, h, h1 * D:(h1 + 1) * D], k[:, h, :], start=(n == 0), stop=(n == 2))
                    mm.then_inc(s_m, 1)


def project_queries(nc, xT, Wq, WqcaBD, q_d, g_d):
    with ExitStack() as ctx:
        def sb(name, shape, dt=F32):
            return ctx.enter_context(nc.sbuf_tensor(name, shape, dt))

        def sem(name):
            return ctx.enter_context(nc.semaphore(name))

        GROUPS = NT // GT
        wraw, graw = sb("wq_raw", [128, FT, H]), sb("wg_raw", [128, FT, HT])
        wq = [sb(f"wq_{p}", [128, FT, H], F32R) for p in "hl"]
        wg = [sb(f"wg_{p}", [128, FT, HT], F32R) for p in "hl"]
        xraw = sb("xT_raw", [128, FT, GT])
        xs = [sb(f"xT_{p}", [128, FT, GT], F32R) for p in "hl"]
        qs = [sb(f"q_{p}", [128, FT, GT], F32R) for p in "hl"]
        gs = [sb(f"g_{p}", [HT, GT], F32R) for p in "hl"]
        NP = FT + 1
        ps = [ctx.enter_context(nc.psum_tensor(f"psq{j}", [128, 512], F32)) for j in range(NP)]
        s_w, s_whi, s_wlo, s_xr = sem("s_w"), sem("s_whi"), sem("s_wlo"), sem("s_xr")
        s_xhi, s_xlo, s_q, s_qhi, s_qlo, s_qst = (sem(n) for n in ("s_xhi", "s_xlo", "s_q", "s_qhi", "s_qlo", "s_qst"))
        s_pass = sem("s_pass")
        STORES = 4
        x_view = xT.rearrange("(c p) n -> p c n", p=128)

        with nc.Block() as block:
            @block.sync
            def _(sp):
                sp.dma_start(wraw[:, :, :], Wq.rearrange("(c p) n -> p c n", p=128)).then_inc(s_w, 16)
                sp.dma_start(graw[:, :, :], WqcaBD.rearrange("(c p) n -> p c n", p=128)).then_inc(s_w, 16)
                sp.dma_start(xraw[:, :, :], x_view[:, :, 0:GT]).then_inc(s_xr, 16)

                def store(g):
                    wait_apart(sp, s_qlo, NP * g + NP, s_pass)
                    for p in range(2):
                        sp.dma_start(raw(q_d[p].rearrange("(c p) n -> p c n", p=128)[:, :, bass.ds(g * GT, GT)]),
                                     raw(qs[p][:, :, :])).then_inc(s_qst, 16)
                        sp.dma_start(raw(g_d[p][:, bass.ds(g * GT, GT)]), raw(gs[p][:, :])).then_inc(s_qst, 16)

                with sp.Fori(0, GROUPS - 1) as g:
                    wait_apart(sp, s_xlo, FT * g + FT, s_pass)
                    sp.dma_start(xraw[:, :, :], x_view[:, :, bass.ds(g * GT + GT, GT)]).then_inc(s_xr, 16)
                    store(g)
                store(GROUPS - 1)
                sp.wait_ge(s_qst, 16 * STORES * GROUPS)

            @block.scalar
            def _(act):
                act.wait_ge(s_w, 32)
                nc.scalar.activation(wq[0][:, :, :], wraw[:, :, :], ACT.Copy).then_inc(s_whi, 1)
                nc.scalar.activation(wg[0][:, :, :], graw[:, :, :], ACT.Copy).then_inc(s_whi, 1)

                def group(g, first):
                    act.wait_ge(s_xr, 16 * g + 16)
                    if not first:
                        act.wait_ge(s_q, NP * g)
                    for c in range(FT):
                        nc.scalar.activation(xs[0][:, c, :], xraw[:, c, :], ACT.Copy).then_inc(s_xhi, 1)
                    if not first:
                        act.wait_ge(s_qst, 16 * STORES * g)
                    for j in range(FT):
                        act.wait_ge(s_q, NP * g + j + 1)
                        nc.scalar.activation(qs[0][:, j, :], ps[j][:, 0:GT], ACT.Copy, scale=SCALE).then_inc(s_qhi, 1)
                    act.wait_ge(s_q, NP * g + NP)
                    nc.scalar.activation(gs[0][:, :], ps[FT][0:HT, 0:GT], ACT.Copy, scale=SCALE).then_inc(s_qhi, 1)

                group(0, True)
                with act.Fori(1, GROUPS) as g:
                    group(g, False)

            @block.vector
            def _(dve):
                dve.wait_ge(s_whi, 2)
                nc.vector.tensor_tensor(wq[1][:, :, :], wraw[:, :, :], wq[0][:, :, :], ALU.subtract).then_inc(s_wlo, 1)
                nc.vector.tensor_tensor(wg[1][:, :, :], graw[:, :, :], wg[0][:, :, :], ALU.subtract).then_inc(s_wlo, 1)
                with dve.Fori(0, GROUPS) as g:
                    for c in range(FT):
                        dve.wait_ge(s_xhi, FT * g + c + 1)
                        nc.vector.tensor_tensor(xs[1][:, c, :], xraw[:, c, :], xs[0][:, c, :],
                                                ALU.subtract).then_inc(s_xlo, 1)
                    for j in range(NP):
                        dve.wait_ge(s_qhi, NP * g + j + 1)
                        o = [qs[p][:, j, :] if j < FT else gs[p][:, :] for p in range(2)]
                        src = ps[j][0:(128 if j < FT else HT), 0:GT]
                        nc.vector.scalar_tensor_tensor(out=o[1], in0=src, scalar=SCALE, in1=o[0],
                                                       op0=ALU.mult, op1=ALU.subtract).then_inc(s_qlo, 1)

            @block.tensor
            def _(pe):
                pe.wait_ge(s_wlo, 2)

                def group(g, first):
                    for j in range(NP):
                        if not first:
                            pe.wait_ge(s_qlo, NP * g - NP + j + 1)
                        n = 0
                        M = 128 if j < FT else HT
                        for c in range(FT):
                            if j == 0:
                                pe.wait_ge(s_xlo, FT * g + c + 1)
                            w = [wq[p][:, c, j * 128:(j + 1) * 128] if j < FT else wg[p][:, c, :] for p in range(2)]
                            for a, b in products(w, xs):
                                mm = pe.matmul(ps[j][0:M, 0:GT], a, b[:, c, :], start=(n == 0), stop=(n == 3 * FT - 1))
                                n += 1
                        mm.then_inc(s_q, 1)

                group(0, True)
                with pe.Fori(1, GROUPS) as g:
                    group(g, False)


def attend(nc, Wv_s, ident, headmask, wbig, x, encT, encN, asel, q_d, g_d, wk_d, wo_d, v2_d, m_d, hs_d):
    with ExitStack() as ctx:
        def sb(name, shape, dt=F32):
            return ctx.enter_context(nc.sbuf_tensor(name, shape, dt))

        def pair(name, shape):
            return [sb(f"{name}_{p}", shape, F32R) for p in "hl"]

        def sem(name):
            return ctx.enter_context(nc.semaphore(name))

        PRING = 3
        enc_raw = sb("enc_raw", [128, max(CT * KEYS, KT * C)])
        rawT = enc_raw[:, 0:CT * KEYS].rearrange("p (c k) -> p c k", c=CT)
        rawN = enc_raw[0:KP, 0:KT * C].rearrange("p (k c) -> p k c", k=KT)
        eT, eN = pair("encT", [128, CT, KEYS]), pair("encN", [KP, KT, C])
        qk = pair("qk", [128, CT, R])
        P = [sb(f"probs{j}", [128, KPAD]) for j in range(PRING)]
        PT = pair("PT", [KP, KT, R])
        UT = pair("UT", [128, CT, RH])
        qst = pair("qstack", [STK, HEADS, S])
        hs = pair("hs", [D, 2, RH])
        negmax, total, inv = sb("negmax", [128, MT]), sb("total", [128, MT]), sb("inv", [128, MT])
        xr, xs = sb("x_raw", [S, H]), pair("x", [S, H])
        ar, As = sb("a_raw", [HT, S]), pair("a", [HT, S])
        g = pair("g_in", [HT, S])
        gbd = pair("gbd", [HT, HEADS, S])
        v2 = pair("v2bd", [HT, H])
        Ms = pair("Min", [D, HEADS, HT])
        P1 = sb("P1", [S, HEADS, S])
        P1T = pair("P1T", [S, HEADS, S])
        P2 = sb("P2", [S, HEADS, T])
        P2T = pair("P2T", [HT, S])
        st1 = sb("st1", [S, 3, HEADS])
        st2 = sb("st2", [S, 3, HEADS])
        hs1T = [UT[p][0:D, 0:2, :] for p in range(2)]
        wk = wbig[0:STK, :, 0:HEADS * C].rearrange("p a (h c) -> p a h c", h=HEADS)

        psS = [ctx.enter_context(nc.psum_tensor(f"psS{j}", [128, 2, 512], F32)) for j in range(2)]
        psT = ctx.enter_context(nc.psum_tensor("psT", [128, 2, 512], F32))
        psB = ctx.enter_context(nc.psum_tensor("psB", [128, 2, 512], F32))

        names = """rawT rawN qin gin ain xin v2in min wkin hsout woin
            scores pt u qkp hsp b2s b2t b2pv b2c b2t2
            exp pthi uhi qkhi hshi b2exp p1hi hs1hi b2exp2 p2hi
            negmax inv norm ptlo ulo qklo hslo b2max b2sub b2sum b2inv b2norm p1lo hs1lo
            c2max c2sub c2sum c2inv c2norm p2lo ready passed_sp passed_pool
            encThi encT encNhi encN gbd ahi a xhi xlo v2bd""".split()
        s = {n: sem("s_" + n) for n in names}

        def tile_in(m):
            return psS[m % 2][0:rows(m), :, 0:HALF]

        def tile_exp(m):
            whole = psS[m % 2][0:rows(m), :, :]
            w = KEYS // 2
            step = list(list(d) for d in whole.ap)
            return bass.AP(whole.tensor, whole.offset, [step[0], [512 + HALF - w, 2], [1, w]])

        def qk_bank(j):
            return psS[(j % 4) // 2][:, j % 2, 0:RH]

        def heads4(ap):
            return ap.rearrange("p a (h j) -> p a h j", h=4)

        with nc.Block() as block:
            @block.sync
            def _(sp):
                def load_ahead(b, first=False):
                    def free(name, n):
                        if not first:
                            wait_apart(sp, s[name], n, s["passed_sp"])
                    free("qkp", 6 * b)
                    for p in range(2):
                        q3 = q_d[p].rearrange("(h d) n -> d h n", d=D)[:, :, bass.ds(b * S, S)]
                        sp.dma_start(raw(qst[p][0:D, :, :]), raw(q3)).then_inc(s["qin"], 16)
                        qh = q_d[0].rearrange("(h d) n -> d h n", d=D)[p * EX:(p + 1) * EX, :, bass.ds(b * S, S)]
                        sp.dma_start(raw(qst[p][D:STK, :, :]), raw(qh)).then_inc(s["qin"], 16)
                    free("encN", b)
                    sp.dma_start(rawT[:, :, :], encT[bass.ds(b, 1)].rearrange("o (c p) k -> p (o c) k", p=128))\
                      .then_inc(s["rawT"], 16)
                    free("gbd", 2 * b)
                    for p in range(2):
                        sp.dma_start(raw(g[p][:, :]), raw(g_d[p][:, bass.ds(b * S, S)])).then_inc(s["gin"], 16)
                    free("a", b)
                    sp.dma_start(ar[:, :], asel[bass.ds(b, 1)].rearrange("o p j -> (o p) j")).then_inc(s["ain"], 16)
                    free("xlo", b)
                    sp.dma_start(xr[:, :], x[bass.ds(b, 1)].rearrange("o p j -> (o p) j")).then_inc(s["xin"], 16)
                    free("b2c", b)
                    for p in range(2):
                        sp.dma_start(raw(Ms[p][:, :, :].rearrange("d a n -> d (a n)")),
                                     raw(m_d[p][bass.ds(b, 1)].rearrange("o d n -> (o d) n"))).then_inc(s["min"], 16)
                    wait_apart(sp, s["encT"], b + 1, s["passed_sp"])
                    sp.dma_start(rawN[:, :, :], encN[bass.ds(b, 1)].rearrange("o (k p) c -> p (o k) c", p=KP))\
                      .then_inc(s["rawN"], 16)

                def load_v2(b):
                    for p in range(2):
                        src = v2_d[p][bass.ds(b, 1)].rearrange("o t n -> (o t) n")
                        for h in range(HEADS):
                            sp.dma_start(raw(v2[p][h * T:(h + 1) * T, :]), raw(src)).then_inc(s["v2in"], 16)

                def store_hs(b, half):
                    wait_apart(sp, s["hslo"], 2 * b + half + 2, s["passed_sp"])
                    for p in range(2):
                        dst = hs_d[p].rearrange("(a h d) n -> a d h n", a=2, d=D)[half][:, :, bass.ds(b * S, S)]
                        sp.dma_start(raw(dst), raw(hs[p][:, half, :].rearrange("d (h n) -> d h n", h=4)))\
                          .then_inc(s["hsout"], 16)

                for p in range(2):
                    sp.dma_start(raw(wk[0:D, p]), raw(wk_d[0].rearrange("(h d) c -> d h c", d=D)))\
                      .then_inc(s["wkin"], 16)
                    sp.dma_start(raw(wk[D:STK, p]),
                                 raw(wk_d[1].rearrange("(h d) c -> d h c", d=D)[p * EX:(p + 1) * EX]))\
                      .then_inc(s["wkin"], 16)
                load_ahead(0, first=True)
                load_v2(0)
                with sp.Fori(0, B - 1) as i:
                    load_ahead(i + 1)
                    store_hs(i, 0)
                    wait_apart(sp, s["hsp"], 2 * i + 2, s["passed_sp"])
                    load_v2(i + 1)
                    store_hs(i, 1)
                for p in range(2):
                    sp.dma_start(raw(wbig[:, p, :]), raw(wo_d[p])).then_inc(s["woin"], 16)
                store_hs(B - 1, 0)
                store_hs(B - 1, 1)
                sp.wait_ge(s["hsout"], 1 + 16 * 4 * B)
                sp.wait_ge(s["woin"], 32)

            @block.gpsimd
            def _(pool):
                def split_inputs(b, first=False):
                    pool.wait_ge(s["gin"], 32 * b + 32)
                    if not first:
                        pool.wait_ge(s["b2s"], b)
                    for p in range(2):
                        nc.gpsimd.tensor_tensor(
                            gbd[p][:, :, :], g[p][:, :].rearrange("p (o j) -> p o j", o=1).to_broadcast([HT, HEADS, S]),
                            headmask[:, :].rearrange("p (h o) -> p h o", o=1).to_broadcast([HT, HEADS, S]),
                            ALU.mult).then_inc(s["gbd"], 1)
                    wait_apart(pool, s["ain"], 16 * b + 16, s["passed_pool"])
                    nc.gpsimd.tensor_copy(As[0][:, :], ar[:, :]).then_inc(s["ahi"], 1)
                    pool.wait_ge(s["ahi"], b + 1)
                    nc.gpsimd.tensor_tensor(As[1][:, :], ar[:, :], As[0][:, :], ALU.subtract).then_inc(s["a"], 1)
                    pool.wait_ge(s["xin"], 16 * b + 16)
                    if not first:
                        wait_apart(pool, s["b2pv"], b, s["passed_pool"])
                    nc.gpsimd.tensor_copy(xs[0][:, :], xr[:, :]).then_inc(s["xhi"], 1)
                    pool.wait_ge(s["xhi"], b + 1)
                    nc.gpsimd.tensor_tensor(xs[1][:, :], xr[:, :], xs[0][:, :], ALU.subtract).then_inc(s["xlo"], 1)
                    pool.wait_ge(s["rawT"], 16 * b + 16)
                    if not first:
                        wait_apart(pool, s["scores"], MT * b, s["passed_pool"])
                    nc.gpsimd.tensor_copy(eT[0][:, :, :], rawT[:, :, :]).then_inc(s["encThi"], 1)
                    pool.wait_ge(s["encThi"], b + 1)
                    nc.gpsimd.tensor_tensor(eT[1][:, :, :], rawT[:, :, :], eT[0][:, :, :], ALU.subtract)\
                      .then_inc(s["encT"], 1)
                    pool.wait_ge(s["rawN"], 16 * b + 16)
                    if not first:
                        wait_apart(pool, s["u"], 2 * CT * b, s["passed_pool"])
                    nc.gpsimd.tensor_copy(eN[0][:, :, :], rawN[:, :, :]).then_inc(s["encNhi"], 1)
                    pool.wait_ge(s["encNhi"], b + 1)
                    nc.gpsimd.tensor_tensor(eN[1][:, :, :], rawN[:, :, :], eN[0][:, :, :], ALU.subtract)\
                      .then_inc(s["encN"], 1)
                    pool.wait_ge(s["v2in"], 16 * 2 * HEADS * (b + 1))
                    for p in range(2):
                        v = v2[p][:, :].rearrange("p (h d) -> p h d", h=HEADS)
                        nc.gpsimd.tensor_tensor(
                            v, v, headmask[:, :].rearrange("p (h o) -> p h o", o=1).to_broadcast([HT, HEADS, D]),
                            ALU.mult).then_inc(s["v2bd"], 1)

                split_inputs(0, first=True)
                with pool.Fori(1, B) as b:
                    split_inputs(b)

            @block.tensor
            def _(pe):
                def scores(i, m):
                    n = rows(m)
                    if m == 0:
                        pe.wait_ge(s["qklo"], 6 * i + 6)
                        pe.wait_ge(s["encT"], i + 1)
                    if m >= 2:
                        pe.wait_ge(s["exp"], MT * i + m - 1)
                    for half in range(2):
                        k0 = half * (KEYS - HALF)
                        j = 0
                        for c in range(CT):
                            for a, e in products(qk, eT):
                                mm = pe.matmul(psS[m % 2][0:n, half, 0:HALF], a[:, c, m * 128:m * 128 + n],
                                               e[:, c, k0:k0 + HALF], start=(j == 0), stop=(j == 3 * CT - 1))
                                j += 1
                    mm.then_inc(s["scores"], 1)

                def turn(i, m):
                    pe.wait_ge(s["norm"], MT * i + m + 1)
                    if m == 0:
                        pe.wait_ge(s["hslo"], 2 * i + 1)
                    else:
                        pe.wait_ge(s["ptlo"], MT * i + m)
                    for k in range(KT):
                        mm = pe.transpose(psT[0:KP, k // 3, (k % 3) * 128:(k % 3 + 1) * 128],
                                          P[m % PRING][:, k * KP:(k + 1) * KP], ident[:, :])
                    mm.then_inc(s["pt"], 1)

                def context(i, u):
                    half, c = divmod(u, CT)
                    if u == 0:
                        pe.wait_ge(s["encN"], i + 1)
                        pe.wait_ge(s["ptlo"], MT * i + (RH + 127) // 128)
                        pe.wait_ge(s["p2lo"], i + 1)
                    if u == CT:
                        pe.wait_ge(s["ptlo"], MT * i + MT)
                    if u >= 2:
                        pe.wait_ge(s["ulo"], 2 * CT * i + u - 1)
                    j = 0
                    for k in range(KT):
                        for e, a in products(eN, PT):
                            mm = pe.matmul(psB[:, u % 2, 0:RH], e[:, k, c * 128:(c + 1) * 128],
                                           a[:, k, half * RH:(half + 1) * RH], start=(j == 0), stop=(j == 3 * KT - 1))
                            j += 1
                    mm.then_inc(s["u"], 1)

                def queries(b, j, first=False):
                    half, c = divmod(j, CT)
                    if j == 0:
                        pe.wait_ge(s["qin"], 64 * b + 64)
                        if first:
                            pe.wait_ge(s["wkin"], 64)
                        else:
                            pe.wait_ge(s["exp"], MT * b)
                    if j >= 4:
                        pe.wait_ge(s["qklo"], 6 * b + j - 3)
                    for h in range(4):
                        for p in range(2):
                            mm = pe.matmul(qk_bank(j)[:, h * S:(h + 1) * S],
                                           wk[:, p, 4 * half + h, c * 128:(c + 1) * 128],
                                           qst[p][:, 4 * half + h, :], start=(p == 0), stop=(p == 1))
                    mm.then_inc(s["qkp"], 1)

                def values(i, half):
                    pe.wait_ge(s["ulo"], 2 * CT * i + CT * (half + 1))
                    if half == 0:
                        pe.wait_ge(s["ptlo"], MT * i + MT)
                        pe.wait_ge(s["v2bd"], 2 * i + 2)
                    for h in range(4):
                        hh = slice((4 * half + h) * D, (4 * half + h + 1) * D)
                        o = psT[0:D, half, h * S:(h + 1) * S]
                        j = 0
                        for c in range(CT):
                            for w, a in products(Wv_s, UT):
                                pe.matmul(o, w[:, c, hh], a[:, c, h * S:(h + 1) * S], start=(j == 0), stop=False)
                                j += 1
                        for j, (w, a) in enumerate(products(v2, P2T)):
                            mm = pe.matmul(o, w[:, hh], a[:, :], start=False, stop=(j == 2))
                    mm.then_inc(s["hsp"], 1)

                def b2_scores(i):
                    pe.wait_ge(s["gbd"], 2 * i + 2)
                    pe.wait_ge(s["a"], i + 1)
                    for half in range(2):
                        for j, (a, e) in enumerate(products(As, gbd)):
                            mm = pe.matmul(psB[0:S, half, 0:RH], a[:, :],
                                           e[:, 4 * half:4 * half + 4, :].rearrange("p h j -> p (h j)"),
                                           start=(j == 0), stop=(j == 2))
                    mm.then_inc(s["b2s"], 1)

                def b2_turn(i):
                    pe.wait_ge(s["b2norm"], i + 1)
                    for h in range(HEADS):
                        mm = pe.transpose(psB[0:S, h // 4, (h % 4) * S:(h % 4 + 1) * S], P1[:, h, :], ident[0:S, 0:S])
                    mm.then_inc(s["b2t"], 1)

                def b2_values(i):
                    pe.wait_ge(s["p1lo"], i + 1)
                    pe.wait_ge(s["xlo"], i + 1)
                    for h in range(HEADS):
                        for j, (w, a) in enumerate(products(xs, P1T)):
                            mm = pe.matmul(psB[0:D, h // 4, (h % 4) * S:(h % 4 + 1) * S],
                                           w[:, h * D:(h + 1) * D], a[:, h, :], start=(j == 0), stop=(j == 2))
                    mm.then_inc(s["b2pv"], 1)

                def b2_scores2(i):
                    pe.wait_ge(s["hs1lo"], i + 1)
                    pe.wait_ge(s["min"], 32 * i + 32)
                    for h in range(HEADS):
                        for j, (a, w) in enumerate(products([t[:, h // 4, (h % 4) * S:(h % 4 + 1) * S] for t in hs1T],
                                                            [t[:, h, :] for t in Ms])):
                            mm = pe.matmul(psB[0:S, 0, 0:HT], a, w, start=(h == 0 and j == 0),
                                           stop=(h == HEADS - 1 and j == 2))
                    mm.then_inc(s["b2c"], 1)

                def b2_turn2(i):
                    pe.wait_ge(s["c2norm"], i + 1)
                    pe.transpose(psB[0:HT, 0, 0:S], P2[:, :, :].rearrange("p h t -> p (h t)"),
                                 ident[0:S, 0:S]).then_inc(s["b2t2"], 1)

                def batch(i, last=False):
                    ahead = (lambda j: None) if last else (lambda j: queries(i + 1, j))
                    scores(i, 0)
                    b2_scores(i)
                    scores(i, 1)
                    scores(i, 2)
                    turn(i, 0)
                    b2_turn(i)
                    scores(i, 3)
                    turn(i, 1)
                    b2_values(i)
                    scores(i, 4)
                    turn(i, 2)
                    b2_scores2(i)
                    scores(i, 5)
                    turn(i, 3)
                    scores(i, 6)
                    turn(i, 4)
                    b2_turn2(i)
                    turn(i, 5)
                    context(i, 0)
                    turn(i, 6)
                    ahead(0)
                    context(i, 1)
                    ahead(1)
                    context(i, 2)
                    ahead(2)
                    context(i, 3)
                    values(i, 0)
                    ahead(3)
                    context(i, 4)
                    ahead(4)
                    context(i, 5)
                    ahead(5)
                    values(i, 1)

                for j in range(2 * CT):
                    queries(0, j, first=True)
                with pe.Fori(0, B - 1) as i:
                    batch(i)
                batch(B - 1, last=True)

            @block.scalar
            def _(act):
                def expo(i, m):
                    n = rows(m)
                    act.wait_ge(s["negmax"], MT * i + m + 1)
                    if m >= PRING:
                        act.wait_ge(s["pt"], MT * i + m - PRING + 1)
                    nc.scalar.activation(P[m % PRING][0:n, 0:KEYS].rearrange("p (a k) -> p a k", a=2), tile_exp(m),
                                         ACT.Exp, bias=negmax[0:n, m:m + 1],
                                         accum_out=total[0:n, m:m + 1]).then_inc(s["exp"], 1)

                def pt_high(i, m):
                    n = rows(m)
                    act.wait_ge(s["pt"], MT * i + m + 1)
                    nc.scalar.activation(
                        PT[0][:, :, m * 128:m * 128 + n].rearrange("p (a k) n -> p a k n", a=2),
                        psT[0:KP, :, 0:384].rearrange("p a (k n) -> p a k n", k=3)[:, :, :, 0:n],
                        ACT.Copy).then_inc(s["pthi"], 1)

                def u_high(i, u):
                    act.wait_ge(s["u"], 2 * CT * i + u + 1)
                    if u == CT:
                        act.wait_ge(s["hsp"], 2 * i + 1)
                    nc.scalar.activation(UT[0][:, u % CT, :], psB[:, u % 2, 0:RH], ACT.Copy).then_inc(s["uhi"], 1)

                def qk_high(b, j):
                    half, c = divmod(j, CT)
                    act.wait_ge(s["qkp"], 6 * b + j + 1)
                    nc.scalar.activation(qk[0][:, c, half * RH:(half + 1) * RH], qk_bank(j),
                                         ACT.Copy).then_inc(s["qkhi"], 1)

                def hs_high(i, half):
                    act.wait_ge(s["hsp"], 2 * i + half + 1)
                    act.wait_ge(s["hsout"], 64 * i + 1)
                    nc.scalar.activation(hs[0][:, half, :], psT[0:D, half, 0:RH], ACT.Copy).then_inc(s["hshi"], 1)

                def b2_exp(i):
                    act.wait_ge(s["b2sub"], i + 1)
                    nc.scalar.activation(P1[:, :, :], P1[:, :, :], ACT.Exp).then_inc(s["b2exp"], 1)

                def b2_pt_high(i):
                    act.wait_ge(s["b2t"], i + 1)
                    nc.scalar.activation(P1T[0][:, :, :].rearrange("p (a h) j -> p a (h j)", a=2),
                                         psB[0:S, :, 0:RH], ACT.Copy).then_inc(s["p1hi"], 1)

                def b2_hs_high(i):
                    act.wait_ge(s["b2pv"], i + 1)
                    nc.scalar.activation(hs1T[0], psB[0:D, :, 0:RH], ACT.Copy).then_inc(s["hs1hi"], 1)

                def b2_exp2(i):
                    act.wait_ge(s["c2sub"], i + 1)
                    nc.scalar.activation(P2[:, :, :], P2[:, :, :], ACT.Exp).then_inc(s["b2exp2"], 1)

                def b2_pt2_high(i):
                    act.wait_ge(s["b2t2"], i + 1)
                    nc.scalar.activation(P2T[0][:, :], psB[0:HT, 0, 0:S], ACT.Copy).then_inc(s["p2hi"], 1)

                def batch(i, last=False):
                    ahead = (lambda j: None) if last else (lambda j: qk_high(i + 1, j))
                    expo(i, 0)
                    expo(i, 1)
                    b2_exp(i)
                    expo(i, 2)
                    pt_high(i, 0)
                    b2_pt_high(i)
                    expo(i, 3)
                    pt_high(i, 1)
                    b2_hs_high(i)
                    expo(i, 4)
                    pt_high(i, 2)
                    b2_exp2(i)
                    expo(i, 5)
                    pt_high(i, 3)
                    expo(i, 6)
                    pt_high(i, 4)
                    b2_pt2_high(i)
                    pt_high(i, 5)
                    u_high(i, 0)
                    pt_high(i, 6)
                    ahead(0)
                    u_high(i, 1)
                    ahead(1)
                    u_high(i, 2)
                    ahead(2)
                    u_high(i, 3)
                    hs_high(i, 0)
                    ahead(3)
                    u_high(i, 4)
                    ahead(4)
                    u_high(i, 5)
                    ahead(5)
                    hs_high(i, 1)

                nc.scalar.activation(st2[:, 2, :], ident[0:S, 0:HEADS], ACT.Copy).then_inc(s["hsout"], 1)
                for j in range(2 * CT):
                    qk_high(0, j)
                with act.Fori(0, B - 1) as i:
                    batch(i)
                batch(B - 1, last=True)

            @block.vector
            def _(dve):
                def rowmax(i, m):
                    n = rows(m)
                    dve.wait_ge(s["scores"], MT * i + m + 1)
                    nc.vector.tensor_reduce(negmax[0:n, m:m + 1], tile_in(m), AX.XY, ALU.max,
                                            negate=True).then_inc(s["negmax"], 1)

                def norm(i, m):
                    n = rows(m)
                    dve.wait_ge(s["exp"], MT * i + m + 1)
                    nc.vector.reciprocal(inv[0:n, m:m + 1], total[0:n, m:m + 1]).then_inc(s["inv"], 1)
                    dve.wait_ge(s["inv"], MT * i + m + 1)
                    nc.vector.tensor_scalar(P[m % PRING][0:n, 0:KEYS], P[m % PRING][0:n, 0:KEYS], inv[0:n, m:m + 1],
                                            None, ALU.mult).then_inc(s["norm"], 1)

                def pt_low(i, m):
                    n = rows(m)
                    dve.wait_ge(s["pthi"], MT * i + m + 1)
                    o = [PT[p][:, :, m * 128:m * 128 + n].rearrange("p (a k) n -> p a k n", a=2) for p in range(2)]
                    nc.vector.tensor_tensor(
                        o[1], psT[0:KP, :, 0:384].rearrange("p a (k n) -> p a k n", k=3)[:, :, :, 0:n], o[0],
                        ALU.subtract).then_inc(s["ptlo"], 1)

                def u_low(i, u):
                    dve.wait_ge(s["uhi"], 2 * CT * i + u + 1)
                    nc.vector.tensor_tensor(UT[1][:, u % CT, :], psB[:, u % 2, 0:RH], UT[0][:, u % CT, :],
                                            ALU.subtract).then_inc(s["ulo"], 1)

                def qk_low(b, j):
                    half, c = divmod(j, CT)
                    cols = slice(half * RH, (half + 1) * RH)
                    dve.wait_ge(s["qkhi"], 6 * b + j + 1)
                    nc.vector.tensor_tensor(qk[1][:, c, cols], qk_bank(j), qk[0][:, c, cols],
                                            ALU.subtract).then_inc(s["qklo"], 1)

                def hs_low(i, half):
                    dve.wait_ge(s["hshi"], 2 * i + half + 1)
                    nc.vector.tensor_tensor(hs[1][:, half, :], psT[0:D, half, 0:RH], hs[0][:, half, :],
                                            ALU.subtract).then_inc(s["hslo"], 1)

                def b2_less_max(i):
                    dve.wait_ge(s["b2s"], i + 1)
                    v = heads4(psB[0:S, :, 0:RH])
                    nc.vector.tensor_reduce(st1[:, 0, :].rearrange("p (a h) -> p a h", a=2), v, AX.X, ALU.max,
                                            negate=True).then_inc(s["b2max"], 1)
                    dve.wait_ge(s["b2max"], i + 1)
                    nc.vector.tensor_tensor(
                        P1[:, :, :].rearrange("p (a h) j -> p a h j", a=2), v,
                        st1[:, 0, :].rearrange("p (a h o) -> p a h o", a=2, o=1).to_broadcast([S, 2, 4, S]),
                        ALU.add).then_inc(s["b2sub"], 1)

                def b2_norm(i):
                    dve.wait_ge(s["b2exp"], i + 1)
                    nc.vector.tensor_reduce(st1[:, 1, :], P1[:, :, :], AX.X, ALU.add).then_inc(s["b2sum"], 1)
                    dve.wait_ge(s["b2sum"], i + 1)
                    nc.vector.reciprocal(st1[:, 2, :], st1[:, 1, :]).then_inc(s["b2inv"], 1)
                    dve.wait_ge(s["b2inv"], i + 1)
                    nc.vector.tensor_tensor(
                        P1[:, :, :], P1[:, :, :],
                        st1[:, 2, :].rearrange("p (h o) -> p h o", o=1).to_broadcast([S, HEADS, S]),
                        ALU.mult).then_inc(s["b2norm"], 1)

                def b2_pt_low(i):
                    dve.wait_ge(s["p1hi"], i + 1)
                    o = [P1T[p][:, :, :].rearrange("p (a h) j -> p a (h j)", a=2) for p in range(2)]
                    nc.vector.tensor_tensor(o[1], psB[0:S, :, 0:RH], o[0], ALU.subtract).then_inc(s["p1lo"], 1)

                def b2_hs_low(i):
                    dve.wait_ge(s["hs1hi"], i + 1)
                    nc.vector.tensor_tensor(hs1T[1], psB[0:D, :, 0:RH], hs1T[0], ALU.subtract).then_inc(s["hs1lo"], 1)

                def b2_less_max2(i):
                    dve.wait_ge(s["b2c"], i + 1)
                    v = psB[0:S, 0, 0:HT].rearrange("p (h t) -> p h t", h=HEADS)
                    nc.vector.tensor_reduce(st2[:, 0, :], v, AX.X, ALU.max, negate=True).then_inc(s["c2max"], 1)
                    dve.wait_ge(s["c2max"], i + 1)
                    nc.vector.tensor_tensor(
                        P2[:, :, :], v, st2[:, 0, :].rearrange("p (h o) -> p h o", o=1).to_broadcast([S, HEADS, T]),
                        ALU.add).then_inc(s["c2sub"], 1)

                def b2_norm2(i):
                    dve.wait_ge(s["b2exp2"], i + 1)
                    nc.vector.tensor_reduce(st2[:, 1, :], P2[:, :, :], AX.X, ALU.add).then_inc(s["c2sum"], 1)
                    dve.wait_ge(s["c2sum"], i + 1)
                    nc.vector.reciprocal(st2[:, 2, :], st2[:, 1, :]).then_inc(s["c2inv"], 1)
                    dve.wait_ge(s["c2inv"], i + 1)
                    nc.vector.tensor_tensor(
                        P2[:, :, :], P2[:, :, :],
                        st2[:, 2, :].rearrange("p (h o) -> p h o", o=1).to_broadcast([S, HEADS, T]),
                        ALU.mult).then_inc(s["c2norm"], 1)

                def b2_pt2_low(i):
                    dve.wait_ge(s["p2hi"], i + 1)
                    nc.vector.tensor_tensor(P2T[1][:, :], psB[0:HT, 0, 0:S], P2T[0][:, :],
                                            ALU.subtract).then_inc(s["p2lo"], 1)

                def batch(i, last=False):
                    ahead = (lambda j: None) if last else (lambda j: qk_low(i + 1, j))
                    rowmax(i, 0)
                    norm(i, 0)
                    b2_less_max(i)
                    rowmax(i, 1)
                    norm(i, 1)
                    b2_norm(i)
                    rowmax(i, 2)
                    pt_low(i, 0)
                    norm(i, 2)
                    b2_pt_low(i)
                    rowmax(i, 3)
                    pt_low(i, 1)
                    norm(i, 3)
                    b2_hs_low(i)
                    rowmax(i, 4)
                    pt_low(i, 2)
                    norm(i, 4)
                    b2_less_max2(i)
                    rowmax(i, 5)
                    pt_low(i, 3)
                    norm(i, 5)
                    b2_norm2(i)
                    rowmax(i, 6)
                    pt_low(i, 4)
                    norm(i, 6)
                    b2_pt2_low(i)
                    pt_low(i, 5)
                    u_low(i, 0)
                    pt_low(i, 6)
                    ahead(0)
                    u_low(i, 1)
                    ahead(1)
                    u_low(i, 2)
                    ahead(2)
                    u_low(i, 3)
                    hs_low(i, 0)
                    ahead(3)
                    u_low(i, 4)
                    ahead(4)
                    u_low(i, 5)
                    ahead(5)
                    hs_low(i, 1)

                for j in range(PRING):
                    nc.vector.memset(P[j][:, KEYS:KPAD], 0.0).then_inc(s["hslo" if j == 0 else "ready"], 1)
                for j in range(2 * CT):
                    qk_low(0, j)
                with dve.Fori(0, B - 1) as i:
                    batch(i)
                batch(B - 1, last=True)


def project_out(nc, wbig, x, bout, hs_d, out):
    with ExitStack() as ctx:
        def sb(name, shape, dt=F32):
            return ctx.enter_context(nc.sbuf_tensor(name, shape, dt))

        FULL, REST = divmod(NT, 128)
        HW = H // 2
        wo = [wbig[:, p, :].rearrange("p (c n) -> p c n", c=FT) for p in range(2)]
        hsT = [[sb(f"hsT{j}_{p}", [128, FT, 128], F32R) for p in "hl"] for j in range(2)]
        xin = [sb(f"x_in{j}", [128, H]) for j in range(2)]
        res = [sb(f"res{j}", [128, H]) for j in range(2)]
        bias = sb("bias", [128, H])
        ps = [ctx.enter_context(nc.psum_tensor(f"pso{j}", [128, 2, 512], F32)) for j in range(2)]
        s_b = ctx.enter_context(nc.semaphore("s_bias"))
        s_pass = ctx.enter_context(nc.semaphore("s_passed_out"))
        s_in = [ctx.enter_context(nc.semaphore(f"s_in{j}")) for j in range(2)]
        s_mm, s_sum, s_res = (ctx.enter_context(nc.semaphore(n)) for n in ("s_mm", "s_sum", "s_res"))
        s_st = [ctx.enter_context(nc.semaphore(f"s_store{j}")) for j in range(2)]
        x2, out2 = x.rearrange("b s n -> (b s) n"), out.rearrange("b s n -> (b s) n")

        with nc.Block() as block:
            @block.sync
            def _(sp):
                def load(r, j, n=128):
                    t0 = (2 * r + j) * 128
                    for p in range(2):
                        sp.dma_start(raw(hsT[j][p][:, :, 0:n]),
                                     raw(hs_d[p].rearrange("(c p) n -> p c n", p=128)[:, :, bass.ds(t0, n)]))\
                          .then_inc(s_in[j], 16)
                    sp.dma_start(xin[j][0:n, :], x2[bass.ds(t0, n), :]).then_inc(s_in[j], 16)

                load(0, 0)
                sp.dma_start(bias[:, :], bout.rearrange("(o n) -> o n", o=1).to_broadcast([128, H])).then_inc(s_b, 16)
                load(0, 1)
                with sp.Fori(1, FULL // 2) as r:
                    for j in range(2):
                        wait_apart(sp, s_res, 2 * r + j - 1, s_pass)
                        load(r, j)
                sp.wait_ge(s_res, FULL - 1)
                load(FULL // 2, 0, REST)

            @block.tensor
            def _(pe):
                def tile(r, j, n=128, first=False):
                    pe.wait_ge(s_in[j], 48 * r + 48)
                    if not first:
                        pe.wait_ge(s_sum, 2 * r + j - 1)
                    for half in range(2):
                        k = 0
                        for c in range(FT):
                            for a, w in products(hsT[j], wo):
                                mm = pe.matmul(ps[j][0:n, half, 0:HW], a[:, c, 0:n], w[:, c, half * HW:(half + 1) * HW],
                                               start=(k == 0), stop=(k == 3 * FT - 1))
                                k += 1
                    mm.then_inc(s_mm, 1)

                tile(0, 0, first=True)
                tile(0, 1, first=True)
                with pe.Fori(1, FULL // 2) as r:
                    tile(r, 0)
                    tile(r, 1)
                tile(FULL // 2, 0, REST)

            @block.vector
            def _(dve):
                def tile(r, j, n=128, first=False):
                    dve.wait_ge(s_mm, 2 * r + j + 1)
                    if not first:
                        dve.wait_ge(s_st[j], 16 * r)
                    v = [t[0:n, :].rearrange("p (a k) -> p a k", a=2) for t in (res[j], bias, xin[j])]
                    nc.vector.tensor_tensor(v[0], ps[j][0:n, :, 0:HW], v[1], ALU.add).then_inc(s_sum, 1)
                    dve.wait_ge(s_sum, 2 * r + j + 1)
                    nc.vector.tensor_tensor(v[0], v[0], v[2], ALU.add).then_inc(s_res, 1)

                dve.wait_ge(s_b, 16)
                tile(0, 0, first=True)
                tile(0, 1, first=True)
                with dve.Fori(1, FULL // 2) as r:
                    tile(r, 0)
                    tile(r, 1)
                tile(FULL // 2, 0, REST)

            @block.scalar
            def _(act):
                def store(r, j, n=128):
                    act.wait_ge(s_res, 2 * r + j + 1)
                    act.dma_start(out2[bass.ds((2 * r + j) * 128, n), :], res[j][0:n, :]).then_inc(s_st[j], 16)

                with act.Fori(0, FULL // 2) as r:
                    store(r, 0)
                    store(r, 1)
                store(FULL // 2, 0, REST)
                act.wait_ge(s_st[0], 16 * (FULL // 2 + 1))
                act.wait_ge(s_st[1], 16 * (FULL // 2))


def kernel(x, ctx_768, L0_xattn_Wq, L0_xattn_Wk, L0_xattn_Wv, L0_xattn_Wq_ca, L0_xattn_Wk_ca, L0_xattn_Wv_ca,
           L0_xattn_Wout, L0_xattn_b_out):
    import numpy as _np
    import concourse.bacc as _bacc
    from concourse import mybir as _mybir
    from concourse.bass_utils import run_bass_kernel_spmd as _run

    x = _np.asarray(x)
    ctx = _np.asarray(ctx_768)
    Wq, Wk = _np.asarray(L0_xattn_Wq), _np.asarray(L0_xattn_Wk)
    Wq_ca = _np.asarray(L0_xattn_Wq_ca)
    enc, ca = ctx[:, :KEYS], ctx[:, KEYS:]
    encN = _np.zeros((B, KPAD, C), x.dtype)
    encN[:, :KEYS] = enc
    picked = _np.linspace(0, C - 1, S).astype(_np.int64)
    wg = _np.zeros((H, HT), x.dtype)
    for h in range(HEADS):
        wg[h * D:(h + 1) * D, h * T:(h + 1) * T] = Wq_ca[:, h * D:(h + 1) * D].T
    laid = {
        "x": x,
        "xT": x.reshape(NT, H).T,
        "encT": enc.transpose(0, 2, 1),
        "encN": encN,
        "caT": ca.reshape(B * T, C).T,
        "asel": _np.tile(ca[:, :, picked], (1, HEADS, 1)),
        "Wq": Wq,
        "WqT": Wq.T,
        "WkT": Wk.T,
        "Wv": L0_xattn_Wv,
        "WqcaBD": wg,
        "Wkca": L0_xattn_Wk_ca,
        "Wvca": L0_xattn_Wv_ca,
        "Wout": L0_xattn_Wout,
        "bout": L0_xattn_b_out,
    }
    nc = _bacc.Bacc("TRN2", target_bir_lowering=False, num_devices=1)
    arrays, args = {}, []
    for name, a in laid.items():
        a = _np.ascontiguousarray(a)
        arrays[f"in_{name}_dram"] = a
        args.append(nc.dram_tensor(f"in_{name}_dram", a.shape, _mybir.dt.from_np(a.dtype), kind="ExternalInput").ap())
    args.append(nc.dram_tensor("out_0_dram", (B, S, H), F32, kind="ExternalOutput").ap())
    build(nc, *args)
    r = _run(nc, [arrays], core_ids=[0])
    return r.results[0]["out_0_dram"]
```

```python
from contextlib import ExitStack

import concourse.bass as bass
from concourse import mybir

F32 = mybir.dt.float32
F32R = mybir.dt.float32r
ALU = mybir.AluOpType
ACT = mybir.ActivationFunctionType
AX = mybir.AxisListType

B, S, H = 16, 100, 640
HEADS = 8
D = H // HEADS
C = 384
T = 4
KEYS = 722 - T
NT = B * S
R = HEADS * S
HT = HEADS * T
ST = 3 * HT
SCALE = float(D) ** -0.5

CT = C // 128
FT = H // 128
KT = 6
KP = (KEYS + KT - 1) // KT
KPAD = KT * KP
HALF = KPAD // 2
RH = R // 2
GT = 4 * S
STK = 3 * D // 2
EX = STK - D
SLOTS = 4


def pieces(f):
    found = []
    for h in range(HEADS):
        lo, hi = max(128 * f, D * h), min(128 * (f + 1), D * (h + 1))
        if lo < hi:
            found.append((h, lo - D * h, lo - 128 * f, hi - lo))
    return found


def low_pieces(r0, n):
    found = []
    for p in range(2):
        lo, hi = max(r0, EX * p), min(r0 + n, EX * (p + 1))
        if lo < hi:
            found.append((p, lo, hi - lo))
    return found


LIFTS = [sum(1 + len(low_pieces(r0, n)) for _, r0, _, n in pieces(f)) for f in range(FT)]


def raw(ap):
    return ap.bitcast(F32)


def wait_apart(eng, sem, value, passed):
    eng.wait_ge(sem, value)
    eng.sem_inc(passed, 1)


def products(a, b):
    return ((a[0], b[0]), (a[0], b[1]), (a[1], b[0]))


def build(nc, x, xT, encT, encN, caT, asel, Wq, WqT, Wk, Wv, WqcaBD, Wkca, Wvca, Wout, bout, out):
    q_d = nc.dram_tensor("q_split", [2, H, NT], F32R).ap()
    g_d = nc.dram_tensor("g_split", [2, HT, NT], F32R).ap()
    v2_d = nc.dram_tensor("v2_split", [2, B, T, H], F32R).ap()
    m_d = nc.dram_tensor("m_split", [2, B, D, HEADS, HT], F32R).ap()
    hs_d = nc.dram_tensor("hs_all", [H, NT], F32).ap()
    with ExitStack() as keep:
        Wv_s = [keep.enter_context(nc.sbuf_tensor(f"Wv_{p}", [128, CT, H], F32R)) for p in "hl"]
        ident = keep.enter_context(nc.sbuf_tensor("ident", [128, 128], F32))
        headmask = keep.enter_context(nc.sbuf_tensor("headmask", [ST, HEADS], F32))
        wk_keep = keep.enter_context(nc.sbuf_tensor("Wk_keep", [128, 2 * CT * H], F32R))
        eT_keep = keep.enter_context(nc.sbuf_tensor("encT_keep", [128, 2 * CT * KEYS], F32R))
        Wk_s = [wk_keep[:, p * CT * H:(p + 1) * CT * H].rearrange("p (c n) -> p c n", c=CT) for p in range(2)]
        Wo_s = [t[:, 0:FT * H].rearrange("p (c n) -> p c n", c=FT) for t in (wk_keep, eT_keep)]
        eT_s = [eT_keep[:, p * CT * KEYS:(p + 1) * CT * KEYS].rearrange("p (c k) -> p c k", c=CT) for p in range(2)]
        prepare(nc, Wk_s, Wv_s, eT_s, ident, headmask, xT, encT, caT, Wq, WqT, Wk, Wv, WqcaBD, Wkca, Wvca,
                q_d, g_d, v2_d, m_d)
        attend(nc, Wk_s, Wv_s, Wo_s, eT_s, ident, headmask, x, encT, encN, asel, Wout, q_d, g_d, v2_d, m_d, hs_d)
        project_out(nc, Wo_s, x, bout, hs_d, out)


def prepare(nc, Wk_s, Wv_s, eT_s, ident, headmask, xT, encT, caT, Wq, WqT, Wk, Wv, WqcaBD, Wkca, Wvca,
            q_d, g_d, v2_d, m_d):
    with ExitStack() as ctx:
        def sb(name, shape, dt=F32):
            return ctx.enter_context(nc.sbuf_tensor(name, shape, dt))

        def pair(name, shape):
            return [sb(f"{name}_{p}", shape, F32R) for p in "hl"]

        def sem(name):
            return ctx.enter_context(nc.semaphore(name))

        GROUPS = NT // GT
        NP = FT + 1
        RING = 3
        wq, wg = pair("wq", [128, FT, H]), pair("wg", [128, FT, HT])
        ca_s, wkca, wvca = pair("caT", [128, CT, B * T]), pair("Wkca", [128, CT, H]), pair("Wvca", [128, CT, H])
        cuts = {"Wq0": slice(0, 3), "Wq1": slice(3, FT)}

        def tiled(w):
            return w.rearrange("(c p) n -> p c n", p=128)

        items = {
            "Wq0": (tiled(Wq)[:, cuts["Wq0"]], [w[:, cuts["Wq0"], :] for w in wq]),
            "Wq1": (tiled(Wq)[:, cuts["Wq1"]], [w[:, cuts["Wq1"], :] for w in wq]),
            "Wg": (tiled(WqcaBD), [w[:, :, :] for w in wg]),
            "caT": (tiled(caT), [w[:, :, :] for w in ca_s]),
            "Wkca": (tiled(Wkca), [w[:, :, :] for w in wkca]),
            "Wvca": (tiled(Wvca), [w[:, :, :] for w in wvca]),
            "Wk": (tiled(Wk), Wk_s),
            "Wv": (tiled(Wv), [w[:, :, :] for w in Wv_s]),
            "enc": (tiled(encT[0]), eT_s),
        }
        order = list(items)
        done = {n: k + 1 for k, n in enumerate(order)}
        raws = [sb(f"raw{j}", [128, CT * KEYS]) for j in range(RING)]
        xraw, xs = sb("xT_raw", [128, FT, GT]), pair("xT", [128, FT, GT])
        qs, gs = pair("q", [128, FT, GT]), pair("g", [HT, GT])
        hraw = [sb(f"WqT_raw{j}", [D, H]) for j in range(2)]
        wqT = [pair(f"WqT{j}", [D, H]) for j in range(2)]
        M = [pair(f"M{j}", [D, B, HEADS, T]) for j in range(2)]
        k2T, v2 = pair("k2T", [D, HEADS, B * T]), pair("v2", [B * T, H])
        credit = sb("credit", [1, 1])

        ps = [ctx.enter_context(nc.psum_tensor(f"psq{j}", [128, 512], F32)) for j in range(NP)]
        psw = [ctx.enter_context(nc.psum_tensor(f"psw{j}", [128, 512], F32)) for j in range(2)]
        s_raw = [sem(f"s_raw{j}") for j in range(RING)]
        s_hraw = [sem(f"s_WqT_raw{j}") for j in range(2)]
        s_const, s_pass = sem("s_const"), sem("s_pass")
        s_hi, s_lo = sem("s_hi"), sem("s_lo")
        s_hhi, s_hlo = sem("s_WqT_hi"), sem("s_WqT_lo")
        s_xr, s_xhi, s_xlo = sem("s_xr"), sem("s_xhi"), sem("s_xlo")
        s_q, s_qhi, s_qlo, s_qst = sem("s_q"), sem("s_qhi"), sem("s_qlo"), sem("s_qst")
        s_k2, s_k2hi, s_k2lo = sem("s_k2"), sem("s_k2hi"), sem("s_k2lo")
        s_v2, s_v2hi, s_v2lo, s_v2st = sem("s_v2"), sem("s_v2hi"), sem("s_v2lo"), sem("s_v2st")
        s_m, s_mhi, s_mlo, s_mst = sem("s_m"), sem("s_mhi"), sem("s_mlo"), sem("s_mst")
        STORES = 4
        x_view = tiled(xT)

        def rawview(n):
            dst = items[n][1][0]
            _, a, b = dst.shape
            return raws[order.index(n) % RING][:, 0:a * b].rearrange("p (a b) -> p a b", a=a)

        with nc.Block() as block:
            @block.sync
            def _(sp):
                def load(n):
                    k = order.index(n)
                    if k >= RING:
                        sp.wait_ge(s_lo, k - RING + 1)
                    sp.dma_start(rawview(n), items[n][0]).then_inc(s_raw[k % RING], 16)

                def load_x(g):
                    sp.dma_start(xraw[:, :, :], x_view[:, :, bass.ds(g * GT, GT)]).then_inc(s_xr, 16)

                def load_head(h, j):
                    sp.dma_start(hraw[j][:, :], WqT[bass.ds(h * D, D), :]).then_inc(s_hraw[j], 16)

                def store_q(g):
                    wait_apart(sp, s_qlo, NP * g + NP, s_pass)
                    for p in range(2):
                        sp.dma_start(raw(tiled(q_d[p])[:, :, bass.ds(g * GT, GT)]),
                                     raw(qs[p][:, :, :])).then_inc(s_qst, 16)
                        sp.dma_start(raw(g_d[p][:, bass.ds(g * GT, GT)]), raw(gs[p][:, :])).then_inc(s_qst, 16)

                def store_m(h, j):
                    wait_apart(sp, s_mlo, h + 1, s_pass)
                    for p in range(2):
                        dst = m_d[p][:, :, bass.ds(h, 1), :].rearrange("b d o n -> d b (o n)")
                        sp.dma_start(raw(dst), raw(M[j][p][:, :, :, :].rearrange("d b a t -> d b (a t)")))\
                          .then_inc(s_mst, 16)

                load("Wq0")
                load_x(0)
                load("Wq1")
                load("Wg")
                load_head(0, 0)
                load_head(1, 1)
                for n in ("caT", "Wkca", "Wvca"):
                    load(n)
                sp.wait_ge(s_xlo, FT)
                load_x(1)
                load("Wk")
                load("Wv")
                store_q(0)
                sp.wait_ge(s_v2lo, 2)
                for p in range(2):
                    sp.dma_start(raw(v2_d[p].rearrange("b t n -> (b t) n")), raw(v2[p][:, :])).then_inc(s_v2st, 16)
                load("enc")

                def group(g, last=False):
                    if not last:
                        wait_apart(sp, s_xlo, FT * g + FT, s_pass)
                        load_x(g + 1)
                    for j in range(2):
                        wait_apart(sp, s_hlo, 2 * g - 1 + j, s_pass)
                        load_head(2 * g + j, j)
                    store_q(g)
                    for j in range(2):
                        store_m(2 * g - 2 + j, j)

                with sp.Fori(1, GROUPS - 1) as g:
                    group(g)
                group(GROUPS - 1, last=True)
                for j in range(2):
                    store_m(HEADS - 2 + j, j)
                sp.wait_ge(s_qst, 16 * STORES * GROUPS)
                sp.wait_ge(s_v2st, 32)
                sp.wait_ge(s_mst, 1 + 32 * HEADS)

            @block.gpsimd
            def _(pool):
                nc.gpsimd.memset(credit[:, :], 0.0).then_inc(s_mst, 1)
                nc.gpsimd.memset(ident[:, :], 0.0).then_inc(s_const, 1)
                nc.gpsimd.memset(headmask[:, :], 1.0).then_inc(s_const, 1)
                pool.wait_ge(s_const, 2)
                nc.gpsimd.affine_select(out=ident[:, :], in_=ident[:, :], compare_op=ALU.not_equal, fill=1.0,
                                        base=0, pattern=[[-1, 128]], channel_multiplier=1).then_inc(s_const, 1)
                done = 3
                for k in range(3):
                    block = headmask[k * HT:(k + 1) * HT, :]
                    for op in (dict(base=0, pattern=[[-T, HEADS]], channel_multiplier=1),
                               dict(base=T - 1, pattern=[[T, HEADS]], channel_multiplier=-1)):
                        pool.wait_ge(s_const, done)
                        nc.gpsimd.affine_select(out=block, in_=block, compare_op=ALU.is_ge, fill=0.0,
                                                **op).then_inc(s_const, 1)
                        done += 1

            def m_view(j, p):
                return M[j][p][:, :, :, :].rearrange("d b a t -> d a b t")

            def ps_m(j):
                return psw[j][0:D, :].rearrange("d (a b t) -> d a b t", a=HEADS, b=B)

            def output(j, p):
                return qs[p][:, j, :] if j < FT else gs[p][:, :]

            def ps_output(j):
                return ps[j][0:(128 if j < FT else HT), 0:GT]

            @block.scalar
            def _(act):
                def high(n):
                    k = order.index(n)
                    act.wait_ge(s_raw[k % RING], 16 * (k // RING + 1))
                    nc.scalar.activation(items[n][1][0], rawview(n), ACT.Copy).then_inc(s_hi, 1)

                def x_high(g, cs=range(FT), first=False):
                    act.wait_ge(s_xr, 16 * g + 16)
                    if not first:
                        act.wait_ge(s_q, NP * g)
                    for c in cs:
                        nc.scalar.activation(xs[0][:, c, :], xraw[:, c, :], ACT.Copy).then_inc(s_xhi, 1)

                def q_high(g, first=False):
                    if not first:
                        act.wait_ge(s_qst, 16 * STORES * g)
                    for j in range(NP):
                        act.wait_ge(s_q, NP * g + j + 1)
                        nc.scalar.activation(output(j, 0), ps_output(j), ACT.Copy, scale=SCALE).then_inc(s_qhi, 1)

                def head_high(h, g, j, first=False):
                    act.wait_ge(s_hraw[j], 16 * g + 16)
                    if not first:
                        act.wait_ge(s_m, h - 1)
                    nc.scalar.activation(wqT[j][0][:, :], hraw[j][:, :], ACT.Copy).then_inc(s_hhi, 1)

                def m_high(h, g, j):
                    act.wait_ge(s_m, h + 1)
                    act.wait_ge(s_mst, 1 + 64 * (g - 1))
                    nc.scalar.activation(m_view(j, 0), ps_m(j), ACT.Copy).then_inc(s_mhi, 1)

                high("Wq0")
                x_high(0, range(0, 3), first=True)
                high("Wq1")
                x_high(0, range(3, FT), first=True)
                for n in ("Wg", "caT", "Wkca", "Wvca"):
                    high(n)
                q_high(0, first=True)
                x_high(1)
                act.wait_ge(s_k2, 1)
                nc.scalar.activation(k2T[0][:, :, :], psw[0][0:D, :].rearrange("d (h n) -> d h n", h=HEADS),
                                     ACT.Copy, scale=SCALE).then_inc(s_k2hi, 1)
                for j in range(2):
                    act.wait_ge(s_v2, j + 1)
                    nc.scalar.activation(v2[0][:, j * 320:(j + 1) * 320], psw[1 - j][0:B * T, 0:320],
                                         ACT.Copy).then_inc(s_v2hi, 1)
                high("Wk")
                high("Wv")
                head_high(0, 0, 0, first=True)
                head_high(1, 0, 1, first=True)

                def group(g, last=False):
                    q_high(g)
                    if last:
                        high("enc")
                    else:
                        x_high(g + 1)
                    for j in range(2):
                        m_high(2 * g - 2 + j, g, j)
                        head_high(2 * g + j, g, j)

                with act.Fori(1, GROUPS - 1) as g:
                    group(g)
                group(GROUPS - 1, last=True)
                for j in range(2):
                    m_high(HEADS - 2 + j, GROUPS, j)

            @block.vector
            def _(dve):
                def low(n):
                    dve.wait_ge(s_hi, done[n])
                    nc.vector.tensor_tensor(items[n][1][1], rawview(n), items[n][1][0], ALU.subtract).then_inc(s_lo, 1)

                def x_low(g, cs=range(FT)):
                    for c in cs:
                        dve.wait_ge(s_xhi, FT * g + c + 1)
                        nc.vector.tensor_tensor(xs[1][:, c, :], xraw[:, c, :], xs[0][:, c, :],
                                                ALU.subtract).then_inc(s_xlo, 1)

                def q_low(g):
                    for j in range(NP):
                        dve.wait_ge(s_qhi, NP * g + j + 1)
                        nc.vector.scalar_tensor_tensor(out=output(j, 1), in0=ps_output(j), scalar=SCALE,
                                                       in1=output(j, 0), op0=ALU.mult,
                                                       op1=ALU.subtract).then_inc(s_qlo, 1)

                def head_low(h, j):
                    dve.wait_ge(s_hhi, h + 1)
                    nc.vector.tensor_tensor(wqT[j][1][:, :], hraw[j][:, :], wqT[j][0][:, :],
                                            ALU.subtract).then_inc(s_hlo, 1)

                def m_low(h, j):
                    dve.wait_ge(s_mhi, h + 1)
                    nc.vector.tensor_tensor(m_view(j, 1), ps_m(j), m_view(j, 0), ALU.subtract).then_inc(s_mlo, 1)

                low("Wq0")
                x_low(0, range(0, 3))
                low("Wq1")
                x_low(0, range(3, FT))
                for n in ("Wg", "caT", "Wkca", "Wvca"):
                    low(n)
                q_low(0)
                x_low(1)
                dve.wait_ge(s_k2hi, 1)
                nc.vector.scalar_tensor_tensor(out=k2T[1][:, :, :].rearrange("d h n -> d (h n)"), in0=psw[0][0:D, :],
                                               scalar=SCALE, in1=k2T[0][:, :, :].rearrange("d h n -> d (h n)"),
                                               op0=ALU.mult, op1=ALU.subtract).then_inc(s_k2lo, 1)
                for j in range(2):
                    cols = slice(j * 320, (j + 1) * 320)
                    dve.wait_ge(s_v2hi, j + 1)
                    nc.vector.tensor_tensor(v2[1][:, cols], psw[1 - j][0:B * T, 0:320], v2[0][:, cols],
                                            ALU.subtract).then_inc(s_v2lo, 1)
                low("Wk")
                low("Wv")
                head_low(0, 0)
                head_low(1, 1)

                def group(g, last=False):
                    q_low(g)
                    if last:
                        low("enc")
                    else:
                        x_low(g + 1)
                    for j in range(2):
                        m_low(2 * g - 2 + j, j)
                        head_low(2 * g + j, j)

                with dve.Fori(1, GROUPS - 1) as g:
                    group(g)
                group(GROUPS - 1, last=True)
                for j in range(2):
                    m_low(HEADS - 2 + j, j)

            @block.tensor
            def _(pe):
                def queries(g, first=False):
                    for j in range(NP):
                        if not first:
                            pe.wait_ge(s_qlo, NP * g - NP + j + 1)
                        elif j == FT:
                            pe.wait_ge(s_lo, done["Wg"])
                        n = 0
                        for c in range(FT):
                            if j == 0:
                                if first:
                                    pe.wait_ge(s_lo, done["Wq0" if c < 3 else "Wq1"])
                                pe.wait_ge(s_xlo, FT * g + c + 1)
                            w = [wq[p][:, c, j * 128:(j + 1) * 128] if j < FT else wg[p][:, c, :] for p in range(2)]
                            for a, b in products(w, xs):
                                mm = pe.matmul(ps_output(j), a, b[:, c, :], start=(n == 0), stop=(n == 3 * FT - 1))
                                n += 1
                        mm.then_inc(s_q, 1)

                def m_head(h, j, first=False):
                    pe.wait_ge(s_hlo, h + 1)
                    if first:
                        pe.wait_ge(s_v2lo, 2)
                    else:
                        pe.wait_ge(s_mlo, h - 1)
                    for h1 in range(HEADS):
                        for n, (w, k) in enumerate(products(wqT[j], k2T)):
                            mm = pe.matmul(psw[j][0:D, h1 * B * T:(h1 + 1) * B * T], w[:, h1 * D:(h1 + 1) * D],
                                           k[:, bass.ds(h, 1), :].rearrange("d o n -> d (o n)"),
                                           start=(n == 0), stop=(n == 2))
                    mm.then_inc(s_m, 1)

                queries(0, first=True)
                pe.wait_ge(s_lo, done["Wkca"])
                for h in range(HEADS):
                    n = 0
                    for c in range(CT):
                        for w, a in products(wkca, ca_s):
                            mm = pe.matmul(psw[0][0:D, h * B * T:(h + 1) * B * T], w[:, c, h * D:(h + 1) * D],
                                           a[:, c, :], start=(n == 0), stop=(n == 3 * CT - 1))
                            n += 1
                mm.then_inc(s_k2, 1)
                pe.wait_ge(s_lo, done["Wvca"])
                for j in range(2):
                    if j == 1:
                        pe.wait_ge(s_k2lo, 1)
                    n = 0
                    for c in range(CT):
                        for a, w in products(ca_s, wvca):
                            mm = pe.matmul(psw[1 - j][0:B * T, 0:320], a[:, c, :], w[:, c, j * 320:(j + 1) * 320],
                                           start=(n == 0), stop=(n == 3 * CT - 1))
                            n += 1
                    mm.then_inc(s_v2, 1)
                queries(1)
                m_head(0, 0, first=True)
                m_head(1, 1, first=True)
                with pe.Fori(2, GROUPS) as g:
                    queries(g)
                    for j in range(2):
                        m_head(2 * g - 2 + j, j)
                for j in range(2):
                    m_head(HEADS - 2 + j, j)



def attend(nc, Wk_s, Wv_s, Wo_s, eT_s, ident, headmask, x, encT, encN, asel, Wout, q_d, g_d, v2_d, m_d, hs_d):
    with ExitStack() as ctx:
        def sb(name, shape, dt=F32):
            return ctx.enter_context(nc.sbuf_tensor(name, shape, dt))

        def pair(name, shape):
            return [sb(f"{name}_{p}", shape, F32R) for p in "hl"]

        def sem(name):
            return ctx.enter_context(nc.semaphore(name))

        PRING = 3
        PARTS = CT
        KQ = KT // PARTS
        encT_raw, enc_raw = sb("encT_raw", [128, CT * KEYS]), sb("enc_raw", [128, KT * C])
        rawT = encT_raw[:, :].rearrange("p (c k) -> p c k", c=CT)
        rawN = enc_raw[0:KP, :].rearrange("p (k c) -> p k c", k=KT)
        eT = eT_s
        eN = pair("encN", [KP, KT, C])
        kT = [pair(f"kT{j}", [128, KEYS]) for j in range(2)]
        kst = sb("kstack", [STK, 2, SLOTS, KEYS], F32R)
        P = [sb(f"probs{j}", [S, KPAD]) for j in range(PRING)]
        PT = pair("PT", [KP, KT, R])
        UT = sb("UT", [128, CT, 4, 2, S], F32R)
        qst = pair("qstack", [STK, HEADS, S])
        hs = sb("hs", [D, RH])
        negmax, total, inv = sb("negmax", [S, HEADS]), sb("total", [S, HEADS]), sb("inv", [S, HEADS])
        xr, xs = sb("x_raw", [S, H]), pair("x", [S, H])
        ar, As = sb("a_raw", [ST, S]), sb("a", [ST, S], F32R)
        g = sb("g_in", [ST, S], F32R)
        gbd = sb("gbd", [ST, HEADS, S], F32R)
        v2 = sb("v2bd", [ST, H], F32R)
        Ms = sb("Min", [D, 2, HEADS, HEADS, T], F32R)
        P1 = sb("P1", [S, HEADS, S])
        P1T = pair("P1T", [S, HEADS, S])
        P2 = sb("P2", [S, HEADS, T])
        P2x3 = sb("P2x3", [S, 3, HEADS, T])
        P2T = sb("P2T", [ST, S], F32R)
        st1 = sb("st1", [S, 3, HEADS])
        st2 = sb("st2", [S, 3, HEADS])
        hs1T = [[PT[p][0:D, 0:4, (7 - half) * S:(8 - half) * S] for half in range(2)] for p in range(2)]

        psS = [ctx.enter_context(nc.psum_tensor(f"psS{j}", [128, 2, 512], F32)) for j in range(2)]
        psT = ctx.enter_context(nc.psum_tensor("psT", [128, 2, 512], F32))
        psB = ctx.enter_context(nc.psum_tensor("psB", [128, 2, 512], F32))

        names = """c2copy c2add hscopy rawT rawN qin gin ain xin v2in min hsout woin0 woin1
            scores pt u kp hsp b2s b2t b2pv b2c b2t2
            exp pthi uhi khi b2exp p1hi hs1hi b2exp2 p2hi
            negmax inv norm ptlo ulo klo hs b2max b2sub b2sum b2inv b2norm p1lo hs1lo
            c2max c2sub c2sum c2inv c2norm p2lo ready wohi wolo passed_sp passed_pool
            encThi encT encNhi encN gbd ahi a xhi xlo v2bd""".split()
        s = {n: sem("s_" + n) for n in names}
        s_lift = [sem(f"s_lift{f}") for f in range(FT)]

        score_slot = [0, 1, 1, 0, 0, 1, 0, 0]
        k_slot = [1, 1, 0, 0, 1]

        def tile_in(h):
            return psS[score_slot[h]][0:S, :, 0:HALF]

        def without_overlap(t, n):
            whole = t[0:n, :, :]
            w = KEYS // 2
            step = list(list(d) for d in whole.ap)
            return bass.AP(whole.tensor, whole.offset, [step[0], [512 + HALF - w, 2], [1, w]])

        def wo_part(k):
            return slice(0, 3) if k == 0 else slice(3, FT)

        def wo_raw(k):
            n = len(range(*wo_part(k).indices(FT)))
            return (encT_raw, enc_raw)[k][:, 0:n * H].rearrange("p (c n) -> p c n", c=n)

        def hs_parts():
            return psT[0:D, :, 0:4 * S].rearrange("d b (h a n) -> d b h a n", h=2, a=2)

        def heads4(ap):
            return ap.rearrange("p (h n) -> p h n", h=4)

        def halves(ap):
            return ap.rearrange("p (a k) -> p a k", a=2)

        with nc.Block() as block:
            @block.sync
            def _(sp):
                def free(name, n, first):
                    if not first:
                        wait_apart(sp, s[name], n, s["passed_sp"])

                def load_q(b, first=False):
                    free("scores", HEADS * b, first)
                    for p in range(2):
                        q3 = q_d[p].rearrange("(h d) n -> d h n", d=D)[:, :, bass.ds(b * S, S)]
                        sp.dma_start(raw(qst[p][0:D, :, :]), raw(q3)).then_inc(s["qin"], 16)
                        qh = q_d[0].rearrange("(h d) n -> d h n", d=D)[p * EX:(p + 1) * EX, :, bass.ds(b * S, S)]
                        sp.dma_start(raw(qst[p][D:STK, :, :]), raw(qh)).then_inc(s["qin"], 16)

                def load_encT(b, first=False):
                    free("encT", PARTS * (b - 1), first)
                    sp.dma_start(rawT[:, :, :], encT[bass.ds(b, 1)].rearrange("o (c p) k -> p (o c) k", p=128))\
                      .then_inc(s["rawT"], 16)

                def load_ga(b, first=False):
                    free("gbd", b, first)
                    for k, p in enumerate((0, 1, 0)):
                        sp.dma_start(raw(g[k * HT:(k + 1) * HT, :]), raw(g_d[p][:, bass.ds(b * S, S)]))\
                          .then_inc(s["gin"], 16)
                    free("a", b, first)
                    sp.dma_start(ar[:, :], asel[bass.ds(b, 1)].rearrange("o p j -> (o p) j")).then_inc(s["ain"], 16)

                def load_x(b, first=False):
                    free("xlo", b, first)
                    sp.dma_start(xr[:, :], x[bass.ds(b, 1)].rearrange("o p j -> (o p) j")).then_inc(s["xin"], 16)

                def load_m(b, first=False):
                    free("b2c", b, first)
                    for p in range(2):
                        sp.dma_start(raw(Ms[:, p, :, :, :].rearrange("d h a t -> d h (a t)")),
                                     raw(m_d[p][bass.ds(b, 1)].rearrange("o d h n -> (o d) h n"))).then_inc(s["min"], 16)

                def load_enc(b, first=False):
                    free("encN", PARTS * b, first)
                    sp.dma_start(rawN[:, :, :], encN[bass.ds(b, 1)].rearrange("o (k p) c -> p (o k) c", p=KP))\
                      .then_inc(s["rawN"], 16)

                def lift(b, f, heads=range(HEADS), first=False):
                    wait_apart(sp, s["klo"], FT * b + f + 1, s["passed_sp"])
                    for h, r0, a0, n in pieces(f):
                        if h not in heads:
                            continue
                        if h >= SLOTS or not first:
                            wait_apart(sp, s["scores"], HEADS * b + h + 1 - SLOTS, s["passed_sp"])
                        j = h % SLOTS
                        high = kT[f % 2][0][a0:a0 + n, :].rearrange("p (o k) -> p o k", o=1)
                        sp.dma_start(raw(kst[r0:r0 + n, :, j, :]), raw(high.to_broadcast([n, 2, KEYS])))\
                          .then_inc(s_lift[f], 16)
                        for p, r, m in low_pieces(r0, n):
                            sp.dma_start(raw(kst[D + r - EX * p:D + r - EX * p + m, p, j, :]),
                                         raw(kT[f % 2][1][a0 + r - r0:a0 + r - r0 + m, :])).then_inc(s_lift[f], 16)

                def load_v2(b):
                    for k, p in enumerate((0, 0, 1)):
                        src = v2_d[p][bass.ds(b, 1)].to_broadcast([HEADS, T, H])
                        sp.dma_start(raw(v2[k * HT:(k + 1) * HT, :]), raw(src)).then_inc(s["v2in"], 16)

                def store_hs(b, half):
                    wait_apart(sp, s["hs"], 2 * b + half + 2, s["passed_sp"])
                    dst = hs_d.rearrange("(a h d) n -> a d h n", a=2, d=D)[half][:, :, bass.ds(b * S, S)]
                    sp.dma_start(dst, hs[:, :].rearrange("d (h n) -> d h n", h=4)).then_inc(s["hsout"], 16)

                load_ga(0, first=True)
                load_x(0, first=True)
                load_q(0, first=True)
                load_m(0, first=True)
                lift(0, 0, first=True)
                lift(0, 1, first=True)
                lift(0, 2, heads=(3,), first=True)

                def batch(i, first=False, last=False):
                    if not last:
                        load_encT(i + 1, first)
                    lift(i, 2, heads=(4,))
                    if not first:
                        store_hs(i - 1, 0)
                    lift(i, 3)
                    load_enc(i, first)
                    lift(i, 4)
                    if not last:
                        load_ga(i + 1)
                    if not first:
                        wait_apart(sp, s["hsp"], 2 * i, s["passed_sp"])
                    load_v2(i)
                    if not first:
                        store_hs(i - 1, 1)
                    if not last:
                        lift(i + 1, 0)
                        load_x(i + 1)
                        load_m(i + 1)
                        load_q(i + 1)
                        lift(i + 1, 1)
                        lift(i + 1, 2, heads=(3,))

                batch(0, first=True)
                with sp.Fori(1, B - 1) as i:
                    batch(i)
                batch(B - 1, last=True)
                for k in range(2):
                    sp.wait_ge(s["encN" if k else "encT"], PARTS * (B if k else B - 1))
                    sp.dma_start(wo_raw(k), Wout.rearrange("(c p) n -> p c n", p=128)[:, wo_part(k), :])\
                      .then_inc(s[f"woin{k}"], 16)
                store_hs(B - 1, 0)
                store_hs(B - 1, 1)
                sp.wait_ge(s["hsout"], 1 + 16 * 2 * B)

            @block.gpsimd
            def _(pool):
                def spread_g(b, first=False):
                    pool.wait_ge(s["gin"], 48 * b + 48)
                    if not first:
                        pool.wait_ge(s["b2s"], 2 * b)
                    nc.gpsimd.tensor_tensor(
                        gbd[:, :, :], g[:, :].rearrange("p (o j) -> p o j", o=1).to_broadcast([ST, HEADS, S]),
                        headmask[:, :].rearrange("p (h o) -> p h o", o=1).to_broadcast([ST, HEADS, S]),
                        ALU.mult).then_inc(s["gbd"], 1)
                    pool.wait_ge(s["gbd"], b + 1)
                    wait_apart(pool, s["ain"], 16 * b + 16, s["passed_pool"])
                    nc.gpsimd.tensor_copy(As[:, :], ar[:, :]).then_inc(s["ahi"], 1)
                    pool.wait_ge(s["ahi"], b + 1)
                    low = slice(2 * HT, ST)
                    nc.gpsimd.tensor_tensor(As[low, :], ar[low, :], As[low, :], ALU.subtract).then_inc(s["a"], 1)
                    pool.wait_ge(s["a"], b + 1)

                def split_x(b, first=False):
                    wait_apart(pool, s["xin"], 16 * b + 16, s["passed_pool"])
                    if not first:
                        wait_apart(pool, s["b2pv"], 2 * b, s["passed_pool"])
                    nc.gpsimd.tensor_copy(xs[0][:, :], xr[:, :]).then_inc(s["xhi"], 1)
                    pool.wait_ge(s["xhi"], b + 1)
                    nc.gpsimd.tensor_tensor(xs[1][:, :], xr[:, :], xs[0][:, :], ALU.subtract).then_inc(s["xlo"], 1)
                    pool.wait_ge(s["xlo"], b + 1)

                def encT_low(b):
                    for c in range(PARTS):
                        pool.wait_ge(s["encThi"], PARTS * (b - 1) + c + 1)
                        nc.gpsimd.tensor_tensor(eT[1][:, c, :], rawT[:, c, :], eT[0][:, c, :],
                                                ALU.subtract).then_inc(s["encT"], 1)
                        pool.wait_ge(s["encT"], PARTS * (b - 1) + c + 1)

                def enc_low(b):
                    for c in range(PARTS):
                        ks = slice(c * KQ, (c + 1) * KQ)
                        pool.wait_ge(s["encNhi"], PARTS * b + c + 1)
                        nc.gpsimd.tensor_tensor(eN[1][:, ks, :], rawN[:, ks, :], eN[0][:, ks, :],
                                                ALU.subtract).then_inc(s["encN"], 1)
                        pool.wait_ge(s["encN"], PARTS * b + c + 1)

                def spread_v2(b):
                    pool.wait_ge(s["v2in"], 48 * b + 48)
                    v = v2[:, :].rearrange("p (h d) -> p h d", h=HEADS)
                    nc.gpsimd.tensor_tensor(
                        v, v, headmask[:, :].rearrange("p (h o) -> p h o", o=1).to_broadcast([ST, HEADS, D]),
                        ALU.mult).then_inc(s["v2bd"], 1)
                    pool.wait_ge(s["v2bd"], b + 1)

                spread_g(0, first=True)
                split_x(0, first=True)
                with pool.Fori(0, B - 1) as i:
                    encT_low(i + 1)
                    enc_low(i)
                    spread_v2(i)
                    spread_g(i + 1)
                    split_x(i + 1)
                enc_low(B - 1)
                spread_v2(B - 1)

            @block.tensor
            def _(pe):
                def scores(i, h):
                    if h == 0:
                        pe.wait_ge(s["qin"], 64 * i + 64)
                        pe.wait_ge(s["klo"], FT * i + 3)
                    if h == 1:
                        pe.wait_ge(s["klo"], FT * i + 2)
                    before = {2: 1, 4: 3, 6: 4, 7: 6}
                    if h in before:
                        pe.wait_ge(s["exp"], HEADS * i + before[h] + 1)
                    if h in (3, 5):
                        pe.wait_ge(s["klo"], FT * i + (4 if h == 3 else 5))
                    for f in range(FT):
                        if h in [q[0] for q in pieces(f)]:
                            pe.wait_ge(s_lift[f], 16 * LIFTS[f] * (i + 1))
                    for half in range(2):
                        k0 = half * (KEYS - HALF)
                        for p in range(2):
                            mm = pe.matmul(psS[score_slot[h]][0:S, half, 0:HALF], qst[p][:, h, :],
                                           kst[:, p, h % SLOTS, k0:k0 + HALF], start=(p == 0), stop=(p == 1))
                    mm.then_inc(s["scores"], 1)

                def keys(b, f, first=False):
                    if f == 0:
                        if not first:
                            pe.wait_ge(s["encT"], PARTS * b)
                            pe.wait_ge(s["exp"], HEADS * b - 2)
                    if f == 1:
                        pe.wait_ge(s["klo"], FT * b + 1)
                    if f == 2 and not first:
                        pe.wait_ge(s["exp"], HEADS * b)
                    if f == 3:
                        pe.wait_ge(s["exp"], HEADS * b + 1)
                    if f == 4:
                        pe.wait_ge(s["exp"], HEADS * b + 3)
                    for half in range(2):
                        k0 = half * (KEYS - HALF)
                        j = 0
                        for c in range(CT):
                            for w, e in products(Wk_s, eT):
                                mm = pe.matmul(psS[k_slot[f]][:, half, 0:HALF], w[:, c, f * 128:(f + 1) * 128],
                                               e[:, c, k0:k0 + HALF], start=(j == 0), stop=(j == 3 * CT - 1))
                                j += 1
                    mm.then_inc(s["kp"], 1)

                def turn(i, h, first=False):
                    pe.wait_ge(s["norm"], HEADS * i + h + 1)
                    if h:
                        pe.wait_ge(s["ptlo"], HEADS * i + h)
                    if h in (0, 4) and not first:
                        pe.wait_ge(s["hs"], 2 * i + (h == 4))
                    for k in range(KT):
                        mm = pe.transpose(psT[0:KP, k // 3, (k % 3) * S:(k % 3 + 1) * S],
                                          P[h % PRING][:, k * KP:(k + 1) * KP], ident[0:S, 0:S])
                    mm.then_inc(s["pt"], 1)

                def context(i, u, first=False):
                    half, c = divmod(u, CT)
                    if u == 0:
                        pe.wait_ge(s["encN"], PARTS * (i + 1))
                        pe.wait_ge(s["ptlo"], HEADS * i + 4)
                    if u == CT:
                        pe.wait_ge(s["ptlo"], HEADS * i + HEADS)
                    if u or not first:
                        pe.wait_ge(s["ulo"], 2 * CT * i + u)
                    j = 0
                    for k in range(KT):
                        for e, a in products(eN, PT):
                            mm = pe.matmul(psB[:, 1, 0:RH], e[:, k, c * 128:(c + 1) * 128],
                                           a[:, k, half * RH:(half + 1) * RH], start=(j == 0), stop=(j == 3 * KT - 1))
                            j += 1
                    mm.then_inc(s["u"], 1)

                def values(i, half, last=False):
                    pe.wait_ge(s["ulo"], 2 * CT * i + CT * (half + 1))
                    if half == 0:
                        pe.wait_ge(s["ptlo"], HEADS * i + HEADS)
                    elif not last:
                        pe.wait_ge(s["ptlo"], HEADS * i + HEADS + 4)
                    if half == 0:
                        pe.wait_ge(s["v2bd"], i + 1)
                    if half == 1:
                        pe.wait_ge(s["hs"], 2 * i + 2)
                    for h in range(4):
                        hh = slice((4 * half + h) * D, (4 * half + h + 1) * D)
                        both = psT[0:D, h // 2, (h % 2) * 2 * S:(h % 2 + 1) * 2 * S]
                        o = psT[0:D, h // 2, (h % 2) * 2 * S:(h % 2) * 2 * S + S]

                        def high(c):
                            return pe.matmul(both, Wv_s[0][:, c, hh], UT[:, c, h, :, :].rearrange("p a n -> p (a n)"),
                                             start=(c == 0), stop=(c == CT - 1))

                        for c in range(CT - 1):
                            high(c)
                        for c in range(CT):
                            pe.matmul(o, Wv_s[1][:, c, hh], UT[:, c, h, 0, :], start=False, stop=False)
                        pe.matmul(o, v2[:, hh], P2T[:, :], start=False, stop=False)
                        mm = high(CT - 1)
                    mm.then_inc(s["hsp"], 1)

                def b2_scores(i, half, first=False):
                    if half == 0:
                        pe.wait_ge(s["gbd"], i + 1)
                        pe.wait_ge(s["a"], i + 1)
                        if not first:
                            pe.wait_ge(s["p2lo"], i)
                    else:
                        pe.wait_ge(s["b2sub"], 2 * i + 1)
                    pe.matmul(psB[0:S, 0, 0:RH], As[:, :],
                              gbd[:, 4 * half:4 * half + 4, :].rearrange("p h j -> p (h j)"),
                              start=True, stop=True).then_inc(s["b2s"], 1)

                def b2_turn(i, half):
                    if half == 0:
                        pe.wait_ge(s["b2norm"], i + 1)
                    else:
                        pe.wait_ge(s["p1lo"], 2 * i + 1)
                    for h in range(4):
                        mm = pe.transpose(psB[0:S, 0, h * S:(h + 1) * S], P1[:, 4 * half + h, :], ident[0:S, 0:S])
                    mm.then_inc(s["b2t"], 1)

                def b2_values(i, half):
                    if half == 0:
                        pe.wait_ge(s["p1lo"], 2 * i + 2)
                        pe.wait_ge(s["xlo"], i + 1)
                    else:
                        pe.wait_ge(s["hs1lo"], 2 * i + 1)
                    for h in range(4):
                        hh = 4 * half + h
                        for j, (w, a) in enumerate(products(xs, P1T)):
                            mm = pe.matmul(psB[0:D, 0, h * S:(h + 1) * S],
                                           w[:, hh * D:(hh + 1) * D], a[:, hh, :], start=(j == 0), stop=(j == 2))
                    mm.then_inc(s["b2pv"], 1)

                def b2_scores2(i):
                    pe.wait_ge(s["hs1lo"], 2 * i + 2)
                    pe.wait_ge(s["min"], 32 * i + 32)
                    a = [[t[h // 4][:, h % 4, :] for h in range(HEADS)] for t in hs1T]

                    def high(h):
                        return pe.matmul(psB[0:S, 0, 0:2 * HT], a[0][h], Ms[:, :, :, h, :],
                                         start=(h == 0), stop=(h == HEADS - 1))

                    for h in range(HEADS - 1):
                        high(h)
                    for h in range(HEADS):
                        pe.matmul(psB[0:S, 0, 0:HT], a[1][h], Ms[:, 0, :, h, :], start=False, stop=False)
                    high(HEADS - 1).then_inc(s["b2c"], 1)

                def b2_turn2(i):
                    pe.wait_ge(s["c2norm"], i + 1)
                    pe.transpose(psB[0:ST, 0, 0:S], P2x3[:, :, :, :].rearrange("p k h t -> p (k h t)"),
                                 ident[0:S, 0:S]).then_inc(s["b2t2"], 1)

                def batch(i, first=False, last=False):
                    if not first:
                        context(i - 1, 2)
                    keys(i, 3)
                    if not first:
                        values(i - 1, 0)
                    scores(i, 2)
                    b2_turn(i, 0)
                    if not first:
                        context(i - 1, 3)
                    turn(i, 0, first)
                    scores(i, 3)
                    keys(i, 4)
                    turn(i, 1)
                    b2_turn(i, 1)
                    if not first:
                        context(i - 1, 4)
                    turn(i, 2)
                    scores(i, 4)
                    scores(i, 5)
                    turn(i, 3)
                    if not first:
                        context(i - 1, 5)
                    b2_values(i, 0)
                    scores(i, 6)
                    if not first:
                        values(i - 1, 1)
                    b2_values(i, 1)
                    if not last:
                        keys(i + 1, 0)
                    turn(i, 4, first)
                    scores(i, 7)
                    context(i, 0, first)
                    turn(i, 5)
                    b2_scores2(i)
                    if not last:
                        keys(i + 1, 1)
                    turn(i, 6)
                    b2_turn2(i)
                    if not last:
                        keys(i + 1, 2)
                    turn(i, 7)
                    if not last:
                        b2_scores(i + 1, 0)
                    context(i, 1)
                    if not last:
                        scores(i + 1, 0)
                        b2_scores(i + 1, 1)
                        scores(i + 1, 1)

                for f in range(3):
                    keys(0, f, first=True)
                b2_scores(0, 0, first=True)
                scores(0, 0)
                b2_scores(0, 1)
                scores(0, 1)
                batch(0, first=True)
                with pe.Fori(1, B - 1) as i:
                    batch(i)
                batch(B - 1, last=True)
                context(B - 1, 2)
                values(B - 1, 0)
                context(B - 1, 3)
                context(B - 1, 4)
                context(B - 1, 5)
                values(B - 1, 1, last=True)

            @block.scalar
            def _(act):
                def expo(i, h, first=False):
                    act.wait_ge(s["negmax"], HEADS * i + h + 1)
                    if h >= PRING:
                        act.wait_ge(s["pt"], HEADS * i + h + 1 - PRING)
                    elif h < 2 and not first:
                        act.wait_ge(s["pt"], HEADS * i - 1 + h)
                    nc.scalar.activation(halves(P[h % PRING][:, 0:KEYS]), without_overlap(psS[score_slot[h]], S),
                                         ACT.Exp, bias=negmax[:, h:h + 1],
                                         accum_out=total[:, h:h + 1]).then_inc(s["exp"], 1)

                def pt_high(i, h):
                    act.wait_ge(s["pt"], HEADS * i + h + 1)
                    nc.scalar.activation(
                        PT[0][:, :, h * S:(h + 1) * S].rearrange("p (a k) n -> p a k n", a=2),
                        psT[0:KP, :, 0:3 * S].rearrange("p a (k n) -> p a k n", k=3), ACT.Copy).then_inc(s["pthi"], 1)

                def k_high(b, f, first=False):
                    act.wait_ge(s["kp"], FT * b + f + 1)
                    if f >= 2:
                        act.wait_ge(s_lift[f - 2], 16 * LIFTS[f - 2] * (b + 1))
                    elif not first:
                        act.wait_ge(s_lift[4 - f], 16 * LIFTS[4 - f] * b)
                    nc.scalar.activation(halves(kT[f % 2][0][:, :]), without_overlap(psS[k_slot[f]], 128),
                                         ACT.Copy).then_inc(s["khi"], 1)

                def encT_high(b, c):
                    if c == 0:
                        act.wait_ge(s["rawT"], 16 * b)
                    nc.scalar.activation(eT[0][:, c, :], rawT[:, c, :], ACT.Copy).then_inc(s["encThi"], 1)

                def enc_high(b, c):
                    if c == 0:
                        act.wait_ge(s["rawN"], 16 * b + 16)
                    ks = slice(c * KQ, (c + 1) * KQ)
                    nc.scalar.activation(eN[0][:, ks, :], rawN[:, ks, :], ACT.Copy).then_inc(s["encNhi"], 1)

                def u_high(i, u):
                    act.wait_ge(s["u"], 2 * CT * i + u + 1)
                    if u == CT:
                        act.wait_ge(s["hsp"], 2 * i + 1)
                    nc.scalar.activation(UT[:, u % CT, :, 0, :], heads4(psB[:, 1, 0:RH]), ACT.Copy).then_inc(s["uhi"], 1)

                def hs_copy(i, half):
                    act.wait_ge(s["hsp"], 2 * i + half + 1)
                    act.wait_ge(s["hsout"], 32 * i + 16 * half + 1)
                    nc.scalar.activation(hs[:, :].rearrange("d (b h n) -> d b h n", b=2, h=2),
                                         hs_parts()[:, :, :, 1, :], ACT.Copy).then_inc(s["hscopy"], 1)

                def b2_exp(i):
                    act.wait_ge(s["b2sub"], 2 * i + 2)
                    nc.scalar.activation(P1[:, :, :], P1[:, :, :], ACT.Exp).then_inc(s["b2exp"], 1)

                def b2_pt_high(i, half):
                    act.wait_ge(s["b2t"], 2 * i + half + 1)
                    nc.scalar.activation(P1T[0][:, 4 * half:4 * half + 4, :].rearrange("p h j -> p (h j)"),
                                         psB[0:S, 0, 0:RH], ACT.Copy).then_inc(s["p1hi"], 1)

                def b2_hs_high(i, half):
                    act.wait_ge(s["b2pv"], 2 * i + half + 1)
                    nc.scalar.activation(hs1T[0][half], psB[0:D, 0, 0:RH].rearrange("d (h n) -> d h n", h=4), ACT.Copy).then_inc(s["hs1hi"], 1)

                def b2_exp2(i):
                    act.wait_ge(s["c2sub"], i + 1)
                    nc.scalar.activation(P2[:, :, :], P2[:, :, :], ACT.Exp).then_inc(s["b2exp2"], 1)

                def b2_pt2_high(i):
                    act.wait_ge(s["b2t2"], i + 1)
                    nc.scalar.activation(P2T[:, :], psB[0:ST, 0, 0:S], ACT.Copy).then_inc(s["p2hi"], 1)

                def wo_high(k):
                    act.wait_ge(s[f"woin{k}"], 16)
                    nc.scalar.activation(Wo_s[0][:, wo_part(k), :], wo_raw(k), ACT.Copy).then_inc(s["wohi"], 1)

                def batch(i, first=False, last=False):
                    if not first:
                        u_high(i - 1, 2)
                    k_high(i, 3)
                    if not first:
                        hs_copy(i - 1, 0)
                    expo(i, 2)
                    b2_pt_high(i, 0)
                    if not first:
                        u_high(i - 1, 3)
                    pt_high(i, 0)
                    expo(i, 3)
                    k_high(i, 4)
                    if not last:
                        encT_high(i + 1, 0)
                    pt_high(i, 1)
                    if not last:
                        encT_high(i + 1, 1)
                    b2_pt_high(i, 1)
                    if not last:
                        encT_high(i + 1, 2)
                    if not first:
                        u_high(i - 1, 4)
                    pt_high(i, 2)
                    expo(i, 4)
                    pt_high(i, 3)
                    expo(i, 5)
                    if not first:
                        u_high(i - 1, 5)
                    enc_high(i, 0)
                    b2_hs_high(i, 0)
                    enc_high(i, 1)
                    expo(i, 6)
                    if not first:
                        hs_copy(i - 1, 1)
                    enc_high(i, 2)
                    b2_hs_high(i, 1)
                    if not last:
                        k_high(i + 1, 0)
                    pt_high(i, 4)
                    expo(i, 7)
                    u_high(i, 0)
                    pt_high(i, 5)
                    b2_exp2(i)
                    if not last:
                        k_high(i + 1, 1)
                    pt_high(i, 6)
                    b2_pt2_high(i)
                    if not last:
                        k_high(i + 1, 2)
                    pt_high(i, 7)
                    u_high(i, 1)
                    if not last:
                        expo(i + 1, 0)
                        b2_exp(i + 1)
                        expo(i + 1, 1)

                nc.scalar.activation(st2[:, 2, :], ident[0:S, 0:HEADS], ACT.Copy).then_inc(s["hsout"], 1)
                for f in range(3):
                    k_high(0, f, first=True)
                expo(0, 0, first=True)
                b2_exp(0)
                expo(0, 1, first=True)
                batch(0, first=True)
                with act.Fori(1, B - 1) as i:
                    batch(i)
                batch(B - 1, last=True)
                wo_high(0)
                u_high(B - 1, 2)
                hs_copy(B - 1, 0)
                u_high(B - 1, 3)
                u_high(B - 1, 4)
                u_high(B - 1, 5)
                wo_high(1)
                hs_copy(B - 1, 1)

            @block.vector
            def _(dve):
                def rowmax(i, h):
                    dve.wait_ge(s["scores"], HEADS * i + h + 1)
                    nc.vector.tensor_reduce(negmax[:, h:h + 1], tile_in(h), AX.XY, ALU.max,
                                            negate=True).then_inc(s["negmax"], 1)

                def norm(i, h):
                    dve.wait_ge(s["exp"], HEADS * i + h + 1)
                    nc.vector.reciprocal(inv[:, h:h + 1], total[:, h:h + 1]).then_inc(s["inv"], 1)
                    dve.wait_ge(s["inv"], HEADS * i + h + 1)
                    nc.vector.tensor_scalar(P[h % PRING][:, 0:KEYS], P[h % PRING][:, 0:KEYS], inv[:, h:h + 1],
                                            None, ALU.mult).then_inc(s["norm"], 1)

                def pt_low(i, h):
                    dve.wait_ge(s["pthi"], HEADS * i + h + 1)
                    o = [PT[p][:, :, h * S:(h + 1) * S].rearrange("p (a k) n -> p a k n", a=2) for p in range(2)]
                    nc.vector.tensor_tensor(
                        o[1], psT[0:KP, :, 0:3 * S].rearrange("p a (k n) -> p a k n", k=3), o[0],
                        ALU.subtract).then_inc(s["ptlo"], 1)

                def hs_add(i, half):
                    dve.wait_ge(s["hscopy"], 2 * i + half + 1)
                    v = hs[:, :].rearrange("d (b h n) -> d b h n", b=2, h=2)
                    nc.vector.tensor_tensor(v, hs_parts()[:, :, :, 0, :], v, ALU.add).then_inc(s["hs"], 1)

                def k_low(b, f):
                    dve.wait_ge(s["khi"], FT * b + f + 1)
                    nc.vector.tensor_tensor(halves(kT[f % 2][1][:, :]), without_overlap(psS[k_slot[f]], 128),
                                            halves(kT[f % 2][0][:, :]), ALU.subtract).then_inc(s["klo"], 1)

                def u_low(i, u):
                    dve.wait_ge(s["uhi"], 2 * CT * i + u + 1)
                    nc.vector.tensor_tensor(UT[:, u % CT, :, 1, :], heads4(psB[:, 1, 0:RH]), UT[:, u % CT, :, 0, :],
                                            ALU.subtract).then_inc(s["ulo"], 1)

                def b2_less_max(i, half):
                    dve.wait_ge(s["b2s"], 2 * i + half + 1)
                    v = psB[0:S, 0, 0:RH].rearrange("p (h j) -> p h j", h=4)
                    hh = slice(4 * half, 4 * half + 4)
                    nc.vector.tensor_reduce(st1[:, 0, hh], v, AX.X, ALU.max, negate=True).then_inc(s["b2max"], 1)
                    dve.wait_ge(s["b2max"], 2 * i + half + 1)
                    nc.vector.tensor_tensor(
                        P1[:, hh, :], v, st1[:, 0, hh].rearrange("p (h o) -> p h o", o=1).to_broadcast([S, 4, S]),
                        ALU.add).then_inc(s["b2sub"], 1)

                def b2_norm(i):
                    dve.wait_ge(s["b2exp"], i + 1)
                    nc.vector.tensor_reduce(st1[:, 1, :], P1[:, :, :], AX.X, ALU.add).then_inc(s["b2sum"], 1)
                    dve.wait_ge(s["b2sum"], i + 1)
                    nc.vector.reciprocal(st1[:, 2, :], st1[:, 1, :]).then_inc(s["b2inv"], 1)
                    dve.wait_ge(s["b2inv"], i + 1)
                    nc.vector.tensor_tensor(
                        P1[:, :, :], P1[:, :, :],
                        st1[:, 2, :].rearrange("p (h o) -> p h o", o=1).to_broadcast([S, HEADS, S]),
                        ALU.mult).then_inc(s["b2norm"], 1)

                def b2_pt_low(i, half):
                    dve.wait_ge(s["p1hi"], 2 * i + half + 1)
                    o = [P1T[p][:, 4 * half:4 * half + 4, :].rearrange("p h j -> p (h j)") for p in range(2)]
                    nc.vector.tensor_tensor(o[1], psB[0:S, 0, 0:RH], o[0], ALU.subtract).then_inc(s["p1lo"], 1)

                def b2_hs_low(i, half):
                    dve.wait_ge(s["hs1hi"], 2 * i + half + 1)
                    nc.vector.tensor_tensor(hs1T[1][half], psB[0:D, 0, 0:RH].rearrange("d (h n) -> d h n", h=4), hs1T[0][half],
                                            ALU.subtract).then_inc(s["hs1lo"], 1)

                def b2_less_max2(i):
                    dve.wait_ge(s["b2c"], i + 1)
                    nc.vector.tensor_copy(P2[:, :, :], psB[0:S, 0, HT:2 * HT].rearrange("p (h t) -> p h t", h=HEADS))\
                      .then_inc(s["c2copy"], 1)
                    dve.wait_ge(s["c2copy"], i + 1)
                    nc.vector.tensor_tensor(P2[:, :, :], psB[0:S, 0, 0:HT].rearrange("p (h t) -> p h t", h=HEADS),
                                            P2[:, :, :], ALU.add).then_inc(s["c2add"], 1)
                    dve.wait_ge(s["c2add"], i + 1)
                    nc.vector.tensor_reduce(st2[:, 0, :], P2[:, :, :], AX.X, ALU.max, negate=True)\
                      .then_inc(s["c2max"], 1)
                    dve.wait_ge(s["c2max"], i + 1)
                    nc.vector.tensor_tensor(
                        P2[:, :, :], P2[:, :, :],
                        st2[:, 0, :].rearrange("p (h o) -> p h o", o=1).to_broadcast([S, HEADS, T]),
                        ALU.add).then_inc(s["c2sub"], 1)

                def b2_norm2(i):
                    dve.wait_ge(s["b2exp2"], i + 1)
                    nc.vector.tensor_reduce(st2[:, 1, :], P2[:, :, :], AX.X, ALU.add).then_inc(s["c2sum"], 1)
                    dve.wait_ge(s["c2sum"], i + 1)
                    nc.vector.reciprocal(st2[:, 2, :], st2[:, 1, :]).then_inc(s["c2inv"], 1)
                    dve.wait_ge(s["c2inv"], i + 1)
                    nc.vector.tensor_tensor(
                        P2x3[:, :, :, :], P2[:, :, :].rearrange("p (o h) t -> p o h t", o=1).to_broadcast([S, 3, HEADS, T]),
                        st2[:, 2, :].rearrange("p (o h u) -> p o h u", o=1, u=1).to_broadcast([S, 3, HEADS, T]),
                        ALU.mult).then_inc(s["c2norm"], 1)

                def b2_pt2_low(i):
                    dve.wait_ge(s["p2hi"], i + 1)
                    low = slice(HT, 2 * HT)
                    nc.vector.tensor_tensor(P2T[low, :], psB[low, 0, 0:S], P2T[low, :],
                                            ALU.subtract).then_inc(s["p2lo"], 1)

                def wo_low(k):
                    dve.wait_ge(s["wohi"], k + 1)
                    nc.vector.tensor_tensor(Wo_s[1][:, wo_part(k), :], wo_raw(k), Wo_s[0][:, wo_part(k), :],
                                            ALU.subtract).then_inc(s["wolo"], 1)

                def batch(i, first=False, last=False):
                    norm(i, 0)
                    b2_norm(i)
                    if not first:
                        u_low(i - 1, 2)
                    norm(i, 1)
                    k_low(i, 3)
                    if not first:
                        hs_add(i - 1, 0)
                    rowmax(i, 2)
                    b2_pt_low(i, 0)
                    if not first:
                        u_low(i - 1, 3)
                    pt_low(i, 0)
                    rowmax(i, 3)
                    norm(i, 2)
                    k_low(i, 4)
                    pt_low(i, 1)
                    b2_pt_low(i, 1)
                    norm(i, 3)
                    if not first:
                        u_low(i - 1, 4)
                    pt_low(i, 2)
                    rowmax(i, 4)
                    rowmax(i, 5)
                    pt_low(i, 3)
                    norm(i, 4)
                    if not first:
                        u_low(i - 1, 5)
                    b2_hs_low(i, 0)
                    norm(i, 5)
                    rowmax(i, 6)
                    if not first:
                        hs_add(i - 1, 1)
                    b2_hs_low(i, 1)
                    norm(i, 6)
                    if not last:
                        k_low(i + 1, 0)
                    pt_low(i, 4)
                    rowmax(i, 7)
                    u_low(i, 0)
                    pt_low(i, 5)
                    norm(i, 7)
                    b2_less_max2(i)
                    b2_norm2(i)
                    if not last:
                        k_low(i + 1, 1)
                    pt_low(i, 6)
                    b2_pt2_low(i)
                    if not last:
                        k_low(i + 1, 2)
                    pt_low(i, 7)
                    if not last:
                        b2_less_max(i + 1, 0)
                    u_low(i, 1)
                    if not last:
                        rowmax(i + 1, 0)
                        b2_less_max(i + 1, 1)
                        rowmax(i + 1, 1)

                for j in range(PRING):
                    nc.vector.memset(P[j][:, KEYS:KPAD], 0.0).then_inc(s["hs" if j == 0 else "ready"], 1)
                for f in range(3):
                    k_low(0, f)
                b2_less_max(0, 0)
                rowmax(0, 0)
                b2_less_max(0, 1)
                rowmax(0, 1)
                batch(0, first=True)
                with dve.Fori(1, B - 1) as i:
                    batch(i)
                batch(B - 1, last=True)
                wo_low(0)
                u_low(B - 1, 2)
                hs_add(B - 1, 0)
                u_low(B - 1, 3)
                u_low(B - 1, 4)
                u_low(B - 1, 5)
                wo_low(1)
                hs_add(B - 1, 1)


def project_out(nc, wo, x, bout, hs_d, out):
    with ExitStack() as ctx:
        def sb(name, shape, dt=F32):
            return ctx.enter_context(nc.sbuf_tensor(name, shape, dt))

        def sem(name):
            return ctx.enter_context(nc.semaphore(name))

        FULL, REST = divmod(NT, 128)
        HW = H // 2
        hsr = [sb(f"hsT_raw{j}", [128, FT, 128]) for j in range(2)]
        hsT = [[sb(f"hsT{j}_{p}", [128, FT, 128], F32R) for p in "hl"] for j in range(2)]
        xin = [sb(f"x_in{j}", [128, H]) for j in range(2)]
        res = [sb(f"res{j}", [128, H]) for j in range(2)]
        bias = sb("bias", [128, H])
        ps = [ctx.enter_context(nc.psum_tensor(f"pso{j}", [128, 2, 512], F32)) for j in range(2)]
        s_b, s_hi, s_lo, s_mm, s_sum, s_res, s_pass = (
            sem(n) for n in ("s_bias", "s_hs_hi", "s_hs_lo", "s_mm", "s_sum", "s_res", "s_passed_out"))
        s_in, s_x, s_st = ([sem(f"{n}{j}") for j in range(2)] for n in ("s_in", "s_x_in", "s_store"))
        x2, out2 = x.rearrange("b s n -> (b s) n"), out.rearrange("b s n -> (b s) n")

        with nc.Block() as block:
            @block.sync
            def _(sp):
                def load(r, j, n=128):
                    sp.dma_start(hsr[j][:, :, 0:n],
                                 hs_d.rearrange("(c p) n -> p c n", p=128)[:, :, bass.ds((2 * r + j) * 128, n)])\
                      .then_inc(s_in[j], 16)

                load(0, 0)
                load(0, 1)
                sp.dma_start(bias[:, :], bout.rearrange("(o n) -> o n", o=1).to_broadcast([128, H])).then_inc(s_b, 16)
                with sp.Fori(1, FULL // 2) as r:
                    for j in range(2):
                        wait_apart(sp, s_lo, 2 * r + j - 1, s_pass)
                        load(r, j)
                sp.wait_ge(s_lo, FULL - 1)
                load(FULL // 2, 0, REST)

            @block.scalar
            def _(act):
                def load_x(r, j, n=128):
                    act.dma_start(xin[j][0:n, :], x2[bass.ds((2 * r + j) * 128, n), :]).then_inc(s_x[j], 16)

                def high(r, j, n=128, first=False):
                    act.wait_ge(s_in[j], 16 * r + 16)
                    if not first:
                        act.wait_ge(s_mm, 2 * r + j - 1)
                    nc.scalar.activation(hsT[j][0][:, :, 0:n], hsr[j][:, :, 0:n], ACT.Copy).then_inc(s_hi, 1)

                def store(r, j, n=128):
                    act.wait_ge(s_res, 2 * r + j + 1)
                    act.dma_start(out2[bass.ds((2 * r + j) * 128, n), :], res[j][0:n, :]).then_inc(s_st[j], 16)

                load_x(0, 0)
                load_x(0, 1)
                high(0, 0, first=True)
                high(0, 1, first=True)
                with act.Fori(0, FULL // 2 - 1) as r:
                    for j in range(2):
                        store(r, j)
                        load_x(r + 1, j)
                        high(r + 1, j)
                store(FULL // 2 - 1, 0)
                load_x(FULL // 2, 0, REST)
                high(FULL // 2, 0, REST)
                store(FULL // 2 - 1, 1)
                store(FULL // 2, 0, REST)
                act.wait_ge(s_st[0], 16 * (FULL // 2 + 1))
                act.wait_ge(s_st[1], 16 * (FULL // 2))

            @block.tensor
            def _(pe):
                def tile(r, j, n=128, first=False):
                    pe.wait_ge(s_lo, 2 * r + j + 1)
                    if not first:
                        pe.wait_ge(s_sum, 2 * r + j - 1)
                    for half in range(2):
                        k = 0
                        for c in range(FT):
                            for a, w in products(hsT[j], wo):
                                mm = pe.matmul(ps[j][0:n, half, 0:HW], a[:, c, 0:n], w[:, c, half * HW:(half + 1) * HW],
                                               start=(k == 0), stop=(k == 3 * FT - 1))
                                k += 1
                    mm.then_inc(s_mm, 1)

                tile(0, 0, first=True)
                tile(0, 1, first=True)
                with pe.Fori(1, FULL // 2) as r:
                    tile(r, 0)
                    tile(r, 1)
                tile(FULL // 2, 0, REST)

            @block.vector
            def _(dve):
                def low(r, j, n=128):
                    dve.wait_ge(s_hi, 2 * r + j + 1)
                    nc.vector.tensor_tensor(hsT[j][1][:, :, 0:n], hsr[j][:, :, 0:n], hsT[j][0][:, :, 0:n],
                                            ALU.subtract).then_inc(s_lo, 1)

                def finish(r, j, n=128, first=False):
                    dve.wait_ge(s_mm, 2 * r + j + 1)
                    if not first:
                        dve.wait_ge(s_st[j], 16 * r)
                    v = [t[0:n, :].rearrange("p (a k) -> p a k", a=2) for t in (res[j], bias, xin[j])]
                    nc.vector.tensor_tensor(v[0], ps[j][0:n, :, 0:HW], v[1], ALU.add).then_inc(s_sum, 1)
                    dve.wait_ge(s_sum, 2 * r + j + 1)
                    dve.wait_ge(s_x[j], 16 * r + 16)
                    nc.vector.tensor_tensor(v[0], v[0], v[2], ALU.add).then_inc(s_res, 1)

                low(0, 0)
                low(0, 1)
                dve.wait_ge(s_b, 16)
                finish(0, 0, first=True)
                low(1, 0)
                finish(0, 1, first=True)
                low(1, 1)
                with dve.Fori(1, FULL // 2 - 1) as r:
                    for j in range(2):
                        finish(r, j)
                        low(r + 1, j)
                finish(FULL // 2 - 1, 0)
                low(FULL // 2, 0, REST)
                finish(FULL // 2 - 1, 1)
                finish(FULL // 2, 0, REST)


def kernel(x, ctx_768, L0_xattn_Wq, L0_xattn_Wk, L0_xattn_Wv, L0_xattn_Wq_ca, L0_xattn_Wk_ca, L0_xattn_Wv_ca,
           L0_xattn_Wout, L0_xattn_b_out):
    import numpy as _np
    import concourse.bacc as _bacc
    from concourse import mybir as _mybir
    from concourse.bass_utils import run_bass_kernel_spmd as _run

    x = _np.asarray(x)
    ctx = _np.asarray(ctx_768)
    Wq, Wk = _np.asarray(L0_xattn_Wq), _np.asarray(L0_xattn_Wk)
    Wq_ca = _np.asarray(L0_xattn_Wq_ca)
    enc, ca = ctx[:, :KEYS], ctx[:, KEYS:]
    encN = _np.zeros((B, KPAD, C), x.dtype)
    encN[:, :KEYS] = enc
    picked = _np.linspace(0, C - 1, S).astype(_np.int64)
    wg = _np.zeros((H, HT), x.dtype)
    for h in range(HEADS):
        wg[h * D:(h + 1) * D, h * T:(h + 1) * T] = Wq_ca[:, h * D:(h + 1) * D].T
    laid = {
        "x": x,
        "xT": x.reshape(NT, H).T,
        "encT": enc.transpose(0, 2, 1),
        "encN": encN,
        "caT": ca.reshape(B * T, C).T,
        "asel": _np.tile(ca[:, :, picked], (1, 3 * HEADS, 1)),
        "Wq": Wq,
        "WqT": Wq.T,
        "Wk": Wk,
        "Wv": L0_xattn_Wv,
        "WqcaBD": wg,
        "Wkca": L0_xattn_Wk_ca,
        "Wvca": L0_xattn_Wv_ca,
        "Wout": L0_xattn_Wout,
        "bout": L0_xattn_b_out,
    }
    nc = _bacc.Bacc("TRN2", target_bir_lowering=False, num_devices=1)
    arrays, args = {}, []
    for name, a in laid.items():
        a = _np.ascontiguousarray(a)
        arrays[f"in_{name}_dram"] = a
        args.append(nc.dram_tensor(f"in_{name}_dram", a.shape, _mybir.dt.from_np(a.dtype), kind="ExternalInput").ap())
    args.append(nc.dram_tensor("out_0_dram", (B, S, H), F32, kind="ExternalOutput").ap())
    build(nc, *args)
    r = _run(nc, [arrays], core_ids=[0])
    return r.results[0]["out_0_dram"]
```

```python
from contextlib import ExitStack

import concourse.bass as bass
from concourse import mybir

F32 = mybir.dt.float32
F32R = mybir.dt.float32r
ALU = mybir.AluOpType
ACT = mybir.ActivationFunctionType
AX = mybir.AxisListType

B, S, H = 16, 100, 640
HEADS = 8
D = H // HEADS
C = 384
T = 4
KEYS = 722 - T
NT = B * S
R = HEADS * S
HT = HEADS * T
ST = 3 * HT
SCALE = float(D) ** -0.5

CT = C // 128
FT = H // 128
KT = 6
KP = (KEYS + KT - 1) // KT
KPAD = KT * KP
HALF = KPAD // 2
RH = R // 2
GT = 4 * S
STK = 3 * D // 2
EX = STK - D
SLOTS = 4


def pieces(f):
    found = []
    for h in range(HEADS):
        lo, hi = max(128 * f, D * h), min(128 * (f + 1), D * (h + 1))
        if lo < hi:
            found.append((h, lo - D * h, lo - 128 * f, hi - lo))
    return found


def low_pieces(r0, n):
    found = []
    for p in range(2):
        lo, hi = max(r0, EX * p), min(r0 + n, EX * (p + 1))
        if lo < hi:
            found.append((p, lo, hi - lo))
    return found


LIFTS = {(f, h): 1 + len(low_pieces(r0, n)) for f in range(FT) for h, r0, _, n in pieces(f)}


def raw(ap):
    return ap.bitcast(F32)


def wait_apart(eng, sem, value, passed):
    eng.wait_ge(sem, value)
    eng.sem_inc(passed, 1)


def products(a, b):
    return ((a[0], b[0]), (a[0], b[1]), (a[1], b[0]))


def build(nc, x, xT, encT, encN, caT, asel, Wq, WqT, Wk, Wv, WqcaBD, Wkca, Wvca, Wout, bout, out):
    q_d = nc.dram_tensor("q_split", [2, H, NT], F32R).ap()
    g_d = nc.dram_tensor("g_split", [2, HT, NT], F32R).ap()
    v2_d = nc.dram_tensor("v2_split", [2, B, T, H], F32R).ap()
    m_d = nc.dram_tensor("m_split", [2, B, D, HEADS, HT], F32R).ap()
    hs_d = nc.dram_tensor("hs_all", [H, NT], F32).ap()
    with ExitStack() as keep:
        Wv_s = [keep.enter_context(nc.sbuf_tensor(f"Wv_{p}", [128, CT, H], F32R)) for p in "hl"]
        ident = keep.enter_context(nc.sbuf_tensor("ident", [128, 128], F32))
        headmask = keep.enter_context(nc.sbuf_tensor("headmask", [ST, HEADS], F32))
        wk_keep = keep.enter_context(nc.sbuf_tensor("Wk_keep", [128, 2 * CT * H], F32R))
        eT_keep = keep.enter_context(nc.sbuf_tensor("encT_keep", [128, 2 * CT * KEYS], F32R))
        Wk_s = [wk_keep[:, p * CT * H:(p + 1) * CT * H].rearrange("p (c n) -> p c n", c=CT) for p in range(2)]
        Wo_s = [t[:, 0:FT * H].rearrange("p (c n) -> p c n", c=FT) for t in (wk_keep, eT_keep)]
        eT_s = [eT_keep[:, p * CT * KEYS:(p + 1) * CT * KEYS].rearrange("p (c k) -> p c k", c=CT) for p in range(2)]
        prepare(nc, Wk_s, Wv_s, eT_s, ident, headmask, xT, encT, caT, Wq, WqT, Wk, Wv, WqcaBD, Wkca, Wvca,
                q_d, g_d, v2_d, m_d)
        attend(nc, Wk_s, Wv_s, Wo_s, eT_s, ident, headmask, x, encT, encN, asel, Wout, bout,
               q_d, g_d, v2_d, m_d, hs_d, out)


def prepare(nc, Wk_s, Wv_s, eT_s, ident, headmask, xT, encT, caT, Wq, WqT, Wk, Wv, WqcaBD, Wkca, Wvca,
            q_d, g_d, v2_d, m_d):
    with ExitStack() as ctx:
        def sb(name, shape, dt=F32):
            return ctx.enter_context(nc.sbuf_tensor(name, shape, dt))

        def pair(name, shape):
            return [sb(f"{name}_{p}", shape, F32R) for p in "hl"]

        def sem(name):
            return ctx.enter_context(nc.semaphore(name))

        GROUPS = NT // GT
        NP = FT + 1
        RING = 3
        wq, wg = pair("wq", [128, FT, H]), pair("wg", [128, FT, HT])
        ca_s, wkca, wvca = pair("caT", [128, CT, B * T]), pair("Wkca", [128, CT, H]), pair("Wvca", [128, CT, H])
        cuts = {"Wq0": slice(0, 3), "Wq1": slice(3, FT)}

        def tiled(w):
            return w.rearrange("(c p) n -> p c n", p=128)

        items = {
            "Wq0": (tiled(Wq)[:, cuts["Wq0"]], [w[:, cuts["Wq0"], :] for w in wq]),
            "Wq1": (tiled(Wq)[:, cuts["Wq1"]], [w[:, cuts["Wq1"], :] for w in wq]),
            "Wg": (tiled(WqcaBD), [w[:, :, :] for w in wg]),
            "caT": (tiled(caT), [w[:, :, :] for w in ca_s]),
            "Wkca": (tiled(Wkca), [w[:, :, :] for w in wkca]),
            "Wvca": (tiled(Wvca), [w[:, :, :] for w in wvca]),
            "Wk": (tiled(Wk), Wk_s),
            "Wv": (tiled(Wv), [w[:, :, :] for w in Wv_s]),
            "enc": (tiled(encT[0]), eT_s),
        }
        order = list(items)
        done = {n: k + 1 for k, n in enumerate(order)}
        raws = [sb(f"raw{j}", [128, CT * KEYS]) for j in range(RING)]
        xraw, xs = sb("xT_raw", [128, FT, GT]), pair("xT", [128, FT, GT])
        qs, gs = pair("q", [128, FT, GT]), pair("g", [HT, GT])
        hraw = [sb(f"WqT_raw{j}", [D, H]) for j in range(2)]
        wqT = [pair(f"WqT{j}", [D, H]) for j in range(2)]
        M = [pair(f"M{j}", [D, B, HEADS, T]) for j in range(2)]
        k2T, v2 = pair("k2T", [D, HEADS, B * T]), pair("v2", [B * T, H])
        credit = sb("credit", [1, 1])

        ps = [ctx.enter_context(nc.psum_tensor(f"psq{j}", [128, 512], F32)) for j in range(NP)]
        psw = [ctx.enter_context(nc.psum_tensor(f"psw{j}", [128, 512], F32)) for j in range(2)]
        s_raw = [sem(f"s_raw{j}") for j in range(RING)]
        s_hraw = [sem(f"s_WqT_raw{j}") for j in range(2)]
        s_const, s_pass = sem("s_const"), sem("s_pass")
        s_hi, s_lo = sem("s_hi"), sem("s_lo")
        s_hhi, s_hlo = sem("s_WqT_hi"), sem("s_WqT_lo")
        s_xr, s_xhi, s_xlo = sem("s_xr"), sem("s_xhi"), sem("s_xlo")
        s_q, s_qhi, s_qlo, s_qst = sem("s_q"), sem("s_qhi"), sem("s_qlo"), sem("s_qst")
        s_k2, s_k2hi, s_k2lo = sem("s_k2"), sem("s_k2hi"), sem("s_k2lo")
        s_v2, s_v2hi, s_v2lo, s_v2st = sem("s_v2"), sem("s_v2hi"), sem("s_v2lo"), sem("s_v2st")
        s_m, s_mhi, s_mlo, s_mst = sem("s_m"), sem("s_mhi"), sem("s_mlo"), sem("s_mst")
        STORES = 6
        x_view = tiled(xT)

        def rawview(n):
            dst = items[n][1][0]
            _, a, b = dst.shape
            return raws[order.index(n) % RING][:, 0:a * b].rearrange("p (a b) -> p a b", a=a)

        with nc.Block() as block:
            @block.sync
            def _(sp):
                def load(n):
                    k = order.index(n)
                    if k >= RING:
                        sp.wait_ge(s_lo, k - RING + 1)
                    sp.dma_start(rawview(n), items[n][0]).then_inc(s_raw[k % RING], 16)

                def load_x(g):
                    sp.dma_start(xraw[:, :, :], x_view[:, :, bass.ds(g * GT, GT)]).then_inc(s_xr, 16)

                def load_head(h, j):
                    sp.dma_start(hraw[j][:, :], WqT[bass.ds(h * D, D), :]).then_inc(s_hraw[j], 16)

                def store_q(g, c0, c1):
                    wait_apart(sp, s_qlo, NP * g + c1, s_pass)
                    for p in range(2):
                        sp.dma_start(raw(tiled(q_d[p])[:, c0:c1, bass.ds(g * GT, GT)]),
                                     raw(qs[p][:, c0:c1, :])).then_inc(s_qst, 16)

                def store_g(g):
                    wait_apart(sp, s_qlo, NP * g + NP, s_pass)
                    for p in range(2):
                        sp.dma_start(raw(g_d[p][:, bass.ds(g * GT, GT)]), raw(gs[p][:, :])).then_inc(s_qst, 16)

                def store_m(h, j):
                    wait_apart(sp, s_mlo, h + 1, s_pass)
                    for p in range(2):
                        dst = m_d[p][:, :, bass.ds(h, 1), :].rearrange("b d o n -> d b (o n)")
                        sp.dma_start(raw(dst), raw(M[j][p][:, :, :, :].rearrange("d b a t -> d b (a t)")))\
                          .then_inc(s_mst, 16)

                load("Wq0")
                load_x(0)
                load("Wq1")
                load("Wg")
                load_head(0, 0)
                load_head(1, 1)
                for n in ("caT", "Wkca", "Wvca"):
                    load(n)
                sp.wait_ge(s_xlo, FT)
                load_x(1)
                load("Wk")
                load("Wv")
                store_q(0, 0, 3)
                store_q(0, 3, FT)
                store_g(0)
                sp.wait_ge(s_v2lo, 2)
                for p in range(2):
                    sp.dma_start(raw(v2_d[p].rearrange("b t n -> (b t) n")), raw(v2[p][:, :])).then_inc(s_v2st, 16)
                load("enc")

                def load_heads(g):
                    for j in range(2):
                        wait_apart(sp, s_hlo, 2 * g - 1 + j, s_pass)
                        load_head(2 * g + j, j)

                with sp.Fori(1, GROUPS - 1) as g:
                    wait_apart(sp, s_xlo, FT * g + FT, s_pass)
                    load_x(g + 1)
                    load_heads(g)
                    store_q(g, 0, 3)
                    store_m(2 * g - 2, 0)
                    store_q(g, 3, FT)
                    store_g(g)
                    store_m(2 * g - 1, 1)
                g = GROUPS - 1
                load_heads(g)
                for j in range(2):
                    store_m(2 * g - 2 + j, j)
                store_q(g, 0, 3)
                store_m(2 * g, 0)
                store_q(g, 3, FT)
                store_g(g)
                store_m(2 * g + 1, 1)
                sp.wait_ge(s_qst, 16 * STORES * GROUPS)
                sp.wait_ge(s_v2st, 32)
                sp.wait_ge(s_mst, 1 + 32 * HEADS)

            @block.gpsimd
            def _(pool):
                nc.gpsimd.memset(credit[:, :], 0.0).then_inc(s_mst, 1)
                nc.gpsimd.memset(ident[:, :], 0.0).then_inc(s_const, 1)
                nc.gpsimd.memset(headmask[:, :], 1.0).then_inc(s_const, 1)
                pool.wait_ge(s_const, 2)
                nc.gpsimd.affine_select(out=ident[:, :], in_=ident[:, :], compare_op=ALU.not_equal, fill=1.0,
                                        base=0, pattern=[[-1, 128]], channel_multiplier=1).then_inc(s_const, 1)
                done = 3
                for k in range(3):
                    block = headmask[k * HT:(k + 1) * HT, :]
                    for op in (dict(base=0, pattern=[[-T, HEADS]], channel_multiplier=1),
                               dict(base=T - 1, pattern=[[T, HEADS]], channel_multiplier=-1)):
                        pool.wait_ge(s_const, done)
                        nc.gpsimd.affine_select(out=block, in_=block, compare_op=ALU.is_ge, fill=0.0,
                                                **op).then_inc(s_const, 1)
                        done += 1

            def m_view(j, p):
                return M[j][p][:, :, :, :].rearrange("d b a t -> d a b t")

            def ps_m(j):
                return psw[j][0:D, :].rearrange("d (a b t) -> d a b t", a=HEADS, b=B)

            def output(j, p):
                return qs[p][:, j, :] if j < FT else gs[p][:, :]

            def ps_output(j):
                return ps[j][0:(128 if j < FT else HT), 0:GT]

            @block.scalar
            def _(act):
                def high(n):
                    k = order.index(n)
                    act.wait_ge(s_raw[k % RING], 16 * (k // RING + 1))
                    nc.scalar.activation(items[n][1][0], rawview(n), ACT.Copy).then_inc(s_hi, 1)

                def x_high(g, cs=range(FT), first=False):
                    act.wait_ge(s_xr, 16 * g + 16)
                    if not first:
                        act.wait_ge(s_q, NP * g)
                    for c in cs:
                        nc.scalar.activation(xs[0][:, c, :], xraw[:, c, :], ACT.Copy).then_inc(s_xhi, 1)

                def q_high(g, js, first=False):
                    if not first:
                        act.wait_ge(s_qst, 16 * STORES * g)
                    for j in js:
                        act.wait_ge(s_q, NP * g + j + 1)
                        nc.scalar.activation(output(j, 0), ps_output(j), ACT.Copy, scale=SCALE).then_inc(s_qhi, 1)

                def head_high(h, g, j, first=False):
                    act.wait_ge(s_hraw[j], 16 * g + 16)
                    if not first:
                        act.wait_ge(s_m, h - 1)
                    nc.scalar.activation(wqT[j][0][:, :], hraw[j][:, :], ACT.Copy).then_inc(s_hhi, 1)

                def m_high(h, g, j):
                    act.wait_ge(s_m, h + 1)
                    act.wait_ge(s_mst, 1 + 64 * (g - 1))
                    nc.scalar.activation(m_view(j, 0), ps_m(j), ACT.Copy).then_inc(s_mhi, 1)

                high("Wq0")
                x_high(0, range(0, 3), first=True)
                high("Wq1")
                x_high(0, range(3, FT), first=True)
                for n in ("Wg", "caT", "Wkca", "Wvca"):
                    high(n)
                q_high(0, range(NP), first=True)
                x_high(1)
                act.wait_ge(s_k2, 1)
                nc.scalar.activation(k2T[0][:, :, :], psw[0][0:D, :].rearrange("d (h n) -> d h n", h=HEADS),
                                     ACT.Copy, scale=SCALE).then_inc(s_k2hi, 1)
                for j in range(2):
                    act.wait_ge(s_v2, j + 1)
                    nc.scalar.activation(v2[0][:, j * 320:(j + 1) * 320], psw[1 - j][0:B * T, 0:320],
                                         ACT.Copy).then_inc(s_v2hi, 1)
                high("Wk")
                high("Wv")
                head_high(0, 0, 0, first=True)
                head_high(1, 0, 1, first=True)

                with act.Fori(1, GROUPS - 1) as g:
                    q_high(g, range(0, 3))
                    m_high(2 * g - 2, g, 0)
                    head_high(2 * g, g, 0)
                    q_high(g, range(3, NP))
                    x_high(g + 1)
                    m_high(2 * g - 1, g, 1)
                    head_high(2 * g + 1, g, 1)
                g = GROUPS - 1
                high("enc")
                for j in range(2):
                    q_high(g, [j])
                    m_high(2 * g - 2 + j, g, j)
                    head_high(2 * g + j, g, j)
                q_high(g, [2, 3])
                m_high(2 * g, g + 1, 0)
                q_high(g, range(4, NP))
                m_high(2 * g + 1, g + 1, 1)

            @block.vector
            def _(dve):
                def low(n):
                    dve.wait_ge(s_hi, done[n])
                    nc.vector.tensor_tensor(items[n][1][1], rawview(n), items[n][1][0], ALU.subtract).then_inc(s_lo, 1)

                def x_low(g, cs=range(FT)):
                    for c in cs:
                        dve.wait_ge(s_xhi, FT * g + c + 1)
                        nc.vector.tensor_tensor(xs[1][:, c, :], xraw[:, c, :], xs[0][:, c, :],
                                                ALU.subtract).then_inc(s_xlo, 1)

                def q_low(g, js):
                    for j in js:
                        dve.wait_ge(s_qhi, NP * g + j + 1)
                        nc.vector.scalar_tensor_tensor(out=output(j, 1), in0=ps_output(j), scalar=SCALE,
                                                       in1=output(j, 0), op0=ALU.mult,
                                                       op1=ALU.subtract).then_inc(s_qlo, 1)

                def head_low(h, j):
                    dve.wait_ge(s_hhi, h + 1)
                    nc.vector.tensor_tensor(wqT[j][1][:, :], hraw[j][:, :], wqT[j][0][:, :],
                                            ALU.subtract).then_inc(s_hlo, 1)

                def m_low(h, j):
                    dve.wait_ge(s_mhi, h + 1)
                    nc.vector.tensor_tensor(m_view(j, 1), ps_m(j), m_view(j, 0), ALU.subtract).then_inc(s_mlo, 1)

                low("Wq0")
                x_low(0, range(0, 3))
                low("Wq1")
                x_low(0, range(3, FT))
                for n in ("Wg", "caT", "Wkca", "Wvca"):
                    low(n)
                q_low(0, range(NP))
                x_low(1)
                dve.wait_ge(s_k2hi, 1)
                nc.vector.scalar_tensor_tensor(out=k2T[1][:, :, :].rearrange("d h n -> d (h n)"), in0=psw[0][0:D, :],
                                               scalar=SCALE, in1=k2T[0][:, :, :].rearrange("d h n -> d (h n)"),
                                               op0=ALU.mult, op1=ALU.subtract).then_inc(s_k2lo, 1)
                for j in range(2):
                    cols = slice(j * 320, (j + 1) * 320)
                    dve.wait_ge(s_v2hi, j + 1)
                    nc.vector.tensor_tensor(v2[1][:, cols], psw[1 - j][0:B * T, 0:320], v2[0][:, cols],
                                            ALU.subtract).then_inc(s_v2lo, 1)
                low("Wk")
                low("Wv")
                head_low(0, 0)
                head_low(1, 1)

                with dve.Fori(1, GROUPS - 1) as g:
                    q_low(g, range(0, 3))
                    m_low(2 * g - 2, 0)
                    head_low(2 * g, 0)
                    q_low(g, range(3, NP))
                    x_low(g + 1)
                    m_low(2 * g - 1, 1)
                    head_low(2 * g + 1, 1)
                g = GROUPS - 1
                low("enc")
                for j in range(2):
                    q_low(g, [j])
                    m_low(2 * g - 2 + j, j)
                    head_low(2 * g + j, j)
                q_low(g, [2, 3])
                m_low(2 * g, 0)
                q_low(g, range(4, NP))
                m_low(2 * g + 1, 1)

            @block.tensor
            def _(pe):
                def queries(g, first=False, after={}):
                    for j in range(NP):
                        if not first:
                            pe.wait_ge(s_qlo, NP * g - NP + j + 1)
                        elif j == FT:
                            pe.wait_ge(s_lo, done["Wg"])
                        n = 0
                        for c in range(FT):
                            if j == 0:
                                if first:
                                    pe.wait_ge(s_lo, done["Wq0" if c < 3 else "Wq1"])
                                pe.wait_ge(s_xlo, FT * g + c + 1)
                            w = [wq[p][:, c, j * 128:(j + 1) * 128] if j < FT else wg[p][:, c, :] for p in range(2)]
                            for a, b in products(w, xs):
                                mm = pe.matmul(ps_output(j), a, b[:, c, :], start=(n == 0), stop=(n == 3 * FT - 1))
                                n += 1
                        mm.then_inc(s_q, 1)
                        if j in after:
                            m_head(*after[j])

                def m_head(h, j, first=False):
                    pe.wait_ge(s_hlo, h + 1)
                    if first:
                        pe.wait_ge(s_v2lo, 2)
                    else:
                        pe.wait_ge(s_mlo, h - 1)
                    for h1 in range(HEADS):
                        for n, (w, k) in enumerate(products(wqT[j], k2T)):
                            mm = pe.matmul(psw[j][0:D, h1 * B * T:(h1 + 1) * B * T], w[:, h1 * D:(h1 + 1) * D],
                                           k[:, bass.ds(h, 1), :].rearrange("d o n -> d (o n)"),
                                           start=(n == 0), stop=(n == 2))
                    mm.then_inc(s_m, 1)

                queries(0, first=True)
                pe.wait_ge(s_lo, done["Wkca"])
                for h in range(HEADS):
                    n = 0
                    for c in range(CT):
                        for w, a in products(wkca, ca_s):
                            mm = pe.matmul(psw[0][0:D, h * B * T:(h + 1) * B * T], w[:, c, h * D:(h + 1) * D],
                                           a[:, c, :], start=(n == 0), stop=(n == 3 * CT - 1))
                            n += 1
                mm.then_inc(s_k2, 1)
                pe.wait_ge(s_lo, done["Wvca"])
                for j in range(2):
                    if j == 1:
                        pe.wait_ge(s_k2lo, 1)
                    n = 0
                    for c in range(CT):
                        for a, w in products(ca_s, wvca):
                            mm = pe.matmul(psw[1 - j][0:B * T, 0:320], a[:, c, :], w[:, c, j * 320:(j + 1) * 320],
                                           start=(n == 0), stop=(n == 3 * CT - 1))
                            n += 1
                    mm.then_inc(s_v2, 1)
                queries(1, after={2: (0, 0, True), 5: (1, 1, True)})
                with pe.Fori(2, GROUPS - 1) as g:
                    queries(g, after={2: (2 * g - 2, 0), 5: (2 * g - 1, 1)})
                queries(GROUPS - 1, after={0: (4, 0), 1: (5, 1), 3: (6, 0), NP - 1: (7, 1)})


def attend(nc, Wk_s, Wv_s, Wo_s, eT_s, ident, headmask, x, encT, encN, asel, Wout, bout,
           q_d, g_d, v2_d, m_d, hs_d, out):
    with ExitStack() as ctx:
        def sb(name, shape, dt=F32):
            return ctx.enter_context(nc.sbuf_tensor(name, shape, dt))

        def pair(name, shape):
            return [sb(f"{name}_{p}", shape, F32R) for p in "hl"]

        def sem(name):
            return ctx.enter_context(nc.semaphore(name))

        PRING = 3
        PARTS = CT
        KQ = KT // PARTS
        encT_raw, enc_raw = sb("encT_raw", [128, CT * KEYS]), sb("enc_raw", [128, KT * C])
        rawT = encT_raw[:, :].rearrange("p (c k) -> p c k", c=CT)
        rawN = enc_raw[0:KP, :].rearrange("p (k c) -> p k c", k=KT)
        eT = eT_s
        eN = pair("encN", [KP, KT, C])
        kT = [pair(f"kT{j}", [128, KEYS]) for j in range(2)]
        kst = sb("kstack", [STK, 2, SLOTS, KEYS], F32R)
        P = [sb(f"probs{j}", [128, KPAD]) for j in range(PRING)]
        PT = pair("PT", [KP, KT, R])
        UT = sb("UT", [128, CT, 4, 2, S], F32R)
        qst = pair("qstack", [STK, HEADS, S])
        hs = sb("hs", [D, RH])
        negmax, total, inv = sb("negmax", [S, HEADS]), sb("total", [S, HEADS]), sb("inv", [S, HEADS])
        xr, xs = sb("x_raw", [S, H]), pair("x", [S, H])
        ar, As = sb("a_raw", [ST, S]), sb("a", [ST, S], F32R)
        g = sb("g_in", [ST, S], F32R)
        gbd = sb("gbd", [ST, HEADS, S], F32R)
        v2 = sb("v2bd", [ST, H], F32R)
        Ms = sb("Min", [D, 2, HEADS, HEADS, T], F32R)
        P1 = sb("P1", [S, HEADS, S])
        P1T = pair("P1T", [S, HEADS, S])
        P2 = sb("P2", [S, HEADS, T])
        P2x3 = sb("P2x3", [S, 3, HEADS, T])
        P2T = sb("P2T", [ST, S], F32R)
        st1 = sb("st1", [S, 3, HEADS])
        st2 = sb("st2", [S, 3, HEADS])
        hs1T = [[PT[p][0:D, 0:4, (7 - half) * S:(8 - half) * S] for half in range(2)] for p in range(2)]

        psS = [ctx.enter_context(nc.psum_tensor(f"psS{j}", [128, 2, 512], F32)) for j in range(2)]
        psT = ctx.enter_context(nc.psum_tensor("psT", [128, 2, 512], F32))
        psB = ctx.enter_context(nc.psum_tensor("psB", [128, 2, 512], F32))

        loads = "rawT rawN qin gin ain xin v2in min woin0 woin1 bias hsout"
        products_done = "scores pt u kp hsp b2s b2t b2pv b2c b2t2 cmm"
        exps_and_highs = "exp pthi uhi khi hscopy b2exp p1hi hs1hi b2exp2 p2hi encThi encNhi wohi chi"
        steps_and_lows = """negmax inv norm ptlo ulo klo hs b2max b2sub b2sum b2inv b2norm p1lo hs1lo
            c2copy c2add c2max c2sub c2sum c2inv c2norm p2lo clo csum cres ready"""
        splits = "encT encN gbd ahi a xhi xlo v2bd wolo passed_sp passed_pool"
        names = " ".join((loads, products_done, exps_and_highs, steps_and_lows, splits)).split()
        s = {n: sem("s_" + n) for n in names}
        s_lift = {(f, h): sem(f"s_lift{f}_{h}") for f, h in LIFTS}

        def wait_lifted(eng, batches, f=None, h=None):
            for key in LIFTS:
                if key[0] == f or key[1] == h:
                    eng.wait_ge(s_lift[key], 16 * LIFTS[key] * batches)

        score_slot = [0, 1, 1, 0, 0, 1, 0, 0]
        k_slot = [1, 1, 0, 0, 1]

        def keys_in(f, first=False):
            return psS[0 if first and f == 0 else k_slot[f]]

        def tile_in(h):
            return psS[score_slot[h]][0:S, :, 0:HALF]

        def without_overlap(t, n):
            whole = t[0:n, :, :]
            w = KEYS // 2
            step = list(list(d) for d in whole.ap)
            return bass.AP(whole.tensor, whole.offset, [step[0], [512 + HALF - w, 2], [1, w]])

        def slot(t, k, n=1):
            return t[:, k * H:(k + n) * H]

        HW = H // 2
        FULL, REST = divmod(NT, 128)
        hsr = [slot(enc_raw, j).rearrange("p (c n) -> p c n", c=FT) for j in range(2)]
        hsT = [[slot(kT[j][p], 0).rearrange("p (c n) -> p c n", c=FT) for p in range(2)] for j in range(2)]
        bias = slot(enc_raw, 2)
        xin = [slot(encT_raw, j) for j in range(2)]
        res = [slot(encT_raw, 2), slot(P[2], 0)]
        s_in, s_x, s_st = ([sem(f"{n}{j}") for j in range(2)] for n in ("s_in", "s_x_in", "s_store"))
        x2, out2 = x.rearrange("b s n -> (b s) n"), out.rearrange("b s n -> (b s) n")

        def wo_raw(c):
            return slot(encT_raw, c % 3)

        def hs_parts():
            return psT[0:D, :, 0:4 * S].rearrange("d b (h a n) -> d b h a n", h=2, a=2)

        def heads4(ap):
            return ap.rearrange("p (h n) -> p h n", h=4)

        def halves(ap):
            return ap.rearrange("p (a k) -> p a k", a=2)

        with nc.Block() as block:
            @block.sync
            def _(sp):
                def free(name, n, first):
                    if not first:
                        wait_apart(sp, s[name], n, s["passed_sp"])

                def load_q(b, first=False):
                    free("scores", HEADS * b, first)
                    for p in range(2):
                        q3 = q_d[p].rearrange("(h d) n -> d h n", d=D)[:, :, bass.ds(b * S, S)]
                        sp.dma_start(raw(qst[p][0:D, :, :]), raw(q3)).then_inc(s["qin"], 16)
                        qh = q_d[0].rearrange("(h d) n -> d h n", d=D)[p * EX:(p + 1) * EX, :, bass.ds(b * S, S)]
                        sp.dma_start(raw(qst[p][D:STK, :, :]), raw(qh)).then_inc(s["qin"], 16)

                def load_encT(b, first=False):
                    free("encT", PARTS * (b - 1), first)
                    sp.dma_start(rawT[:, :, :], encT[bass.ds(b, 1)].rearrange("o (c p) k -> p (o c) k", p=128))\
                      .then_inc(s["rawT"], 16)

                def load_ga(b, first=False):
                    free("gbd", b, first)
                    for k, p in enumerate((0, 1, 0)):
                        sp.dma_start(raw(g[k * HT:(k + 1) * HT, :]), raw(g_d[p][:, bass.ds(b * S, S)]))\
                          .then_inc(s["gin"], 16)
                    free("a", b, first)
                    sp.dma_start(ar[:, :], asel[bass.ds(b, 1)].rearrange("o p j -> (o p) j")).then_inc(s["ain"], 16)

                def load_x(b, first=False):
                    free("xlo", b, first)
                    sp.dma_start(xr[:, :], x[bass.ds(b, 1)].rearrange("o p j -> (o p) j")).then_inc(s["xin"], 16)

                def load_m(b, first=False):
                    free("b2c", b, first)
                    for p in range(2):
                        sp.dma_start(raw(Ms[:, p, :, :, :].rearrange("d h a t -> d h (a t)")),
                                     raw(m_d[p][bass.ds(b, 1)].rearrange("o d h n -> (o d) h n"))).then_inc(s["min"], 16)

                def load_enc(b, first=False):
                    free("encN", PARTS * b, first)
                    sp.dma_start(rawN[:, :, :], encN[bass.ds(b, 1)].rearrange("o (k p) c -> p (o k) c", p=KP))\
                      .then_inc(s["rawN"], 16)

                def lift(b, f, heads=range(HEADS), first=False):
                    wait_apart(sp, s["klo"], FT * b + f + 1, s["passed_sp"])
                    for h, r0, a0, n in pieces(f):
                        if h not in heads:
                            continue
                        if h >= SLOTS or not first:
                            wait_apart(sp, s["scores"], HEADS * b + h + 1 - SLOTS, s["passed_sp"])
                        j = h % SLOTS
                        high = kT[f % 2][0][a0:a0 + n, :].rearrange("p (o k) -> p o k", o=1)
                        sp.dma_start(raw(kst[r0:r0 + n, :, j, :]), raw(high.to_broadcast([n, 2, KEYS])))\
                          .then_inc(s_lift[f, h], 16)
                        for p, r, m in low_pieces(r0, n):
                            sp.dma_start(raw(kst[D + r - EX * p:D + r - EX * p + m, p, j, :]),
                                         raw(kT[f % 2][1][a0 + r - r0:a0 + r - r0 + m, :])).then_inc(s_lift[f, h], 16)

                def load_v2(b):
                    for k, p in enumerate((0, 0, 1)):
                        src = v2_d[p][bass.ds(b, 1)].to_broadcast([HEADS, T, H])
                        sp.dma_start(raw(v2[k * HT:(k + 1) * HT, :]), raw(src)).then_inc(s["v2in"], 16)

                def store_hs(b, half):
                    wait_apart(sp, s["hs"], 2 * b + half + 2, s["passed_sp"])
                    dst = hs_d.rearrange("(a h d) n -> a d h n", a=2, d=D)[half][:, :, bass.ds(b * S, S)]
                    sp.dma_start(dst, hs[:, :].rearrange("d (h n) -> d h n", h=4)).then_inc(s["hsout"], 16)

                load_ga(0, first=True)
                load_q(0, first=True)
                lift(0, 0, first=True)
                load_x(0, first=True)
                lift(0, 1, first=True)
                load_m(0, first=True)
                lift(0, 2, heads=(3,), first=True)

                def load_wo(k):
                    cs = slice(0, 3) if k == 0 else slice(3, FT)
                    n = cs.stop - cs.start
                    sp.dma_start(slot(encT_raw, 0, n).rearrange("p (c n) -> p c n", c=n),
                                 Wout.rearrange("(c p) n -> p c n", p=128)[:, cs, :]).then_inc(s[f"woin{k}"], 16)

                def load_tile(r, j, n=128):
                    sp.dma_start(hsr[j][:, :, 0:n],
                                 hs_d.rearrange("(c p) n -> p c n", p=128)[:, :, bass.ds((2 * r + j) * 128, n)])\
                      .then_inc(s_in[j], 16)

                def batch(i, first=False, last=False):
                    if last:
                        sp.wait_ge(s["encT"], PARTS * (B - 1))
                        load_wo(0)
                    if not last:
                        load_encT(i + 1, first)
                    lift(i, 2, heads=(4,))
                    if not first:
                        store_hs(i - 1, 0)
                    lift(i, 3)
                    load_enc(i, first)
                    lift(i, 4)
                    if last:
                        sp.wait_ge(s["wolo"], 2)
                        load_wo(1)
                    if not last:
                        load_ga(i + 1)
                    if not first:
                        wait_apart(sp, s["hsp"], 2 * i, s["passed_sp"])
                    load_v2(i)
                    if not first:
                        store_hs(i - 1, 1)
                    if not last:
                        lift(i + 1, 0)
                        load_q(i + 1)
                        lift(i + 1, 1)
                        load_x(i + 1)
                        load_m(i + 1)
                        lift(i + 1, 2, heads=(3,))

                batch(0, first=True)
                with sp.Fori(1, B - 1) as i:
                    batch(i)
                batch(B - 1, last=True)
                sp.wait_ge(s["encN"], PARTS * B)
                sp.wait_ge(s["hsout"], 1 + 32 * (B - 1))
                load_tile(0, 0)
                load_tile(0, 1)
                sp.dma_start(bias, bout.rearrange("(o n) -> o n", o=1).to_broadcast([128, H])).then_inc(s["bias"], 16)
                sp.wait_ge(s["wolo"], FT)
                for j in range(2):
                    sp.dma_start(xin[j], x2[j * 128:(j + 1) * 128, :]).then_inc(s_x[j], 16)
                for j in range(2):
                    sp.wait_ge(s["clo"], j + 1)
                    load_tile(1, j)
                store_hs(B - 1, 0)
                for t in range(4, 8):
                    sp.wait_ge(s["clo"], t - 1)
                    load_tile(t // 2, t % 2)
                store_hs(B - 1, 1)
                with sp.Fori(4, FULL // 2 - 1) as r:
                    for j in range(2):
                        wait_apart(sp, s["clo"], 2 * r + j - 1, s["passed_sp"])
                        load_tile(r, j)
                sp.wait_ge(s["clo"], FULL - 3)
                load_tile(FULL // 2 - 1, 0)
                sp.wait_ge(s["hsout"], 1 + 16 * 2 * B)
                sp.wait_ge(s["clo"], FULL - 2)
                load_tile(FULL // 2 - 1, 1)
                sp.wait_ge(s["clo"], FULL - 1)
                load_tile(FULL // 2, 0, REST)

            @block.gpsimd
            def _(pool):
                def spread_g(b, first=False):
                    pool.wait_ge(s["gin"], 48 * b + 48)
                    if not first:
                        pool.wait_ge(s["b2s"], 2 * b)
                    nc.gpsimd.tensor_tensor(
                        gbd[:, :, :], g[:, :].rearrange("p (o j) -> p o j", o=1).to_broadcast([ST, HEADS, S]),
                        headmask[:, :].rearrange("p (h o) -> p h o", o=1).to_broadcast([ST, HEADS, S]),
                        ALU.mult).then_inc(s["gbd"], 1)
                    pool.wait_ge(s["gbd"], b + 1)
                    wait_apart(pool, s["ain"], 16 * b + 16, s["passed_pool"])
                    nc.gpsimd.tensor_copy(As[:, :], ar[:, :]).then_inc(s["ahi"], 1)
                    pool.wait_ge(s["ahi"], b + 1)
                    low = slice(2 * HT, ST)
                    nc.gpsimd.tensor_tensor(As[low, :], ar[low, :], As[low, :], ALU.subtract).then_inc(s["a"], 1)
                    pool.wait_ge(s["a"], b + 1)

                def split_x(b, first=False):
                    wait_apart(pool, s["xin"], 16 * b + 16, s["passed_pool"])
                    if not first:
                        wait_apart(pool, s["b2pv"], 2 * b, s["passed_pool"])
                    nc.gpsimd.tensor_copy(xs[0][:, :], xr[:, :]).then_inc(s["xhi"], 1)
                    pool.wait_ge(s["xhi"], b + 1)
                    nc.gpsimd.tensor_tensor(xs[1][:, :], xr[:, :], xs[0][:, :], ALU.subtract).then_inc(s["xlo"], 1)
                    pool.wait_ge(s["xlo"], b + 1)

                def encT_low(b):
                    for c in range(PARTS):
                        pool.wait_ge(s["encThi"], PARTS * (b - 1) + c + 1)
                        nc.gpsimd.tensor_tensor(eT[1][:, c, :], rawT[:, c, :], eT[0][:, c, :],
                                                ALU.subtract).then_inc(s["encT"], 1)
                        pool.wait_ge(s["encT"], PARTS * (b - 1) + c + 1)

                def enc_low(b):
                    for c in range(PARTS):
                        ks = slice(c * KQ, (c + 1) * KQ)
                        pool.wait_ge(s["encNhi"], PARTS * b + c + 1)
                        nc.gpsimd.tensor_tensor(eN[1][:, ks, :], rawN[:, ks, :], eN[0][:, ks, :],
                                                ALU.subtract).then_inc(s["encN"], 1)
                        pool.wait_ge(s["encN"], PARTS * b + c + 1)

                def spread_v2(b):
                    pool.wait_ge(s["v2in"], 48 * b + 48)
                    v = v2[:, :].rearrange("p (h d) -> p h d", h=HEADS)
                    nc.gpsimd.tensor_tensor(
                        v, v, headmask[:, :].rearrange("p (h o) -> p h o", o=1).to_broadcast([ST, HEADS, D]),
                        ALU.mult).then_inc(s["v2bd"], 1)
                    pool.wait_ge(s["v2bd"], b + 1)

                spread_g(0, first=True)
                split_x(0, first=True)
                with pool.Fori(0, B - 1) as i:
                    encT_low(i + 1)
                    enc_low(i)
                    spread_v2(i)
                    spread_g(i + 1)
                    split_x(i + 1)

                def wo_low(c):
                    pool.wait_ge(s["wohi"], c + 1)
                    nc.gpsimd.tensor_tensor(Wo_s[1][:, c, :], wo_raw(c), Wo_s[0][:, c, :],
                                            ALU.subtract).then_inc(s["wolo"], 1)
                    pool.wait_ge(s["wolo"], c + 1)

                for c in range(3):
                    wo_low(c)
                enc_low(B - 1)
                for c in range(3, FT):
                    wo_low(c)
                spread_v2(B - 1)

            @block.tensor
            def _(pe):
                def scores(i, h):
                    if h == 0:
                        pe.wait_ge(s["qin"], 64 * i + 64)
                        pe.wait_ge(s["klo"], FT * i + 3)
                    if h == 1:
                        pe.wait_ge(s["klo"], FT * i + 2)
                    before = {2: 1, 4: 3, 6: 4, 7: 6}
                    if h in before:
                        pe.wait_ge(s["exp"], HEADS * i + before[h] + 1)
                    if h in (3, 5):
                        pe.wait_ge(s["klo"], FT * i + (4 if h == 3 else 5))
                    wait_lifted(pe, i + 1, h=h)
                    for half in range(2):
                        k0 = half * (KEYS - HALF)
                        for p in range(2):
                            mm = pe.matmul(psS[score_slot[h]][0:S, half, 0:HALF], qst[p][:, h, :],
                                           kst[:, p, h % SLOTS, k0:k0 + HALF], start=(p == 0), stop=(p == 1))
                    mm.then_inc(s["scores"], 1)

                def keys(b, f, first=False):
                    if f == 0:
                        if not first:
                            pe.wait_ge(s["encT"], PARTS * b)
                            pe.wait_ge(s["exp"], HEADS * b - 2)
                    if f == (2 if first else 1):
                        pe.wait_ge(s["klo"], FT * b + 1)
                    if f == 2 and not first:
                        pe.wait_ge(s["exp"], HEADS * b)
                    if f == 3:
                        pe.wait_ge(s["exp"], HEADS * b + 1)
                    if f == 4:
                        pe.wait_ge(s["exp"], HEADS * b + 3)
                    for half in range(2):
                        k0 = half * (KEYS - HALF)
                        j = 0
                        for c in range(CT):
                            for w, e in products(Wk_s, eT):
                                mm = pe.matmul(keys_in(f, first)[:, half, 0:HALF], w[:, c, f * 128:(f + 1) * 128],
                                               e[:, c, k0:k0 + HALF], start=(j == 0), stop=(j == 3 * CT - 1))
                                j += 1
                    mm.then_inc(s["kp"], 1)

                def turn(i, h, first=False):
                    pe.wait_ge(s["norm"], HEADS * i + h + 1)
                    if h:
                        pe.wait_ge(s["ptlo"], HEADS * i + h)
                    if h in (0, 4) and not first:
                        pe.wait_ge(s["hs"], 2 * i + (h == 4))
                    for k in range(KT):
                        mm = pe.transpose(psT[0:KP, k // 3, (k % 3) * S:(k % 3 + 1) * S],
                                          P[h % PRING][0:S, k * KP:(k + 1) * KP], ident[0:S, 0:S])
                    mm.then_inc(s["pt"], 1)

                def context(i, u, first=False):
                    half, c = divmod(u, CT)
                    if u == 0:
                        pe.wait_ge(s["encN"], PARTS * (i + 1))
                        pe.wait_ge(s["ptlo"], HEADS * i + 4)
                    if u == CT:
                        pe.wait_ge(s["ptlo"], HEADS * i + HEADS)
                    if u or not first:
                        pe.wait_ge(s["ulo"], 2 * CT * i + u)
                    j = 0
                    for k in range(KT):
                        for e, a in products(eN, PT):
                            mm = pe.matmul(psB[:, 1, 0:RH], e[:, k, c * 128:(c + 1) * 128],
                                           a[:, k, half * RH:(half + 1) * RH], start=(j == 0), stop=(j == 3 * KT - 1))
                            j += 1
                    mm.then_inc(s["u"], 1)

                def values(i, half, last=False):
                    pe.wait_ge(s["ulo"], 2 * CT * i + CT * (half + 1))
                    if half == 0:
                        pe.wait_ge(s["ptlo"], HEADS * i + HEADS)
                    elif not last:
                        pe.wait_ge(s["ptlo"], HEADS * i + HEADS + 4)
                    if half == 0:
                        pe.wait_ge(s["v2bd"], i + 1)
                    if half == 1:
                        pe.wait_ge(s["hs"], 2 * i + 2)
                    for h in range(4):
                        hh = slice((4 * half + h) * D, (4 * half + h + 1) * D)
                        both = psT[0:D, h // 2, (h % 2) * 2 * S:(h % 2 + 1) * 2 * S]
                        o = psT[0:D, h // 2, (h % 2) * 2 * S:(h % 2) * 2 * S + S]

                        def high(c):
                            return pe.matmul(both, Wv_s[0][:, c, hh], UT[:, c, h, :, :].rearrange("p a n -> p (a n)"),
                                             start=(c == 0), stop=(c == CT - 1))

                        for c in range(CT - 1):
                            high(c)
                        for c in range(CT):
                            pe.matmul(o, Wv_s[1][:, c, hh], UT[:, c, h, 0, :], start=False, stop=False)
                        pe.matmul(o, v2[:, hh], P2T[:, :], start=False, stop=False)
                        mm = high(CT - 1)
                    mm.then_inc(s["hsp"], 1)

                def b2_scores(i, half, first=False):
                    if half == 0:
                        pe.wait_ge(s["gbd"], i + 1)
                        pe.wait_ge(s["a"], i + 1)
                        if not first:
                            pe.wait_ge(s["p2lo"], i)
                    else:
                        pe.wait_ge(s["b2sub"], 2 * i + 1)
                    pe.matmul(psB[0:S, 0, 0:RH], As[:, :],
                              gbd[:, 4 * half:4 * half + 4, :].rearrange("p h j -> p (h j)"),
                              start=True, stop=True).then_inc(s["b2s"], 1)

                def b2_turn(i, half):
                    if half == 0:
                        pe.wait_ge(s["b2norm"], i + 1)
                    else:
                        pe.wait_ge(s["p1lo"], 2 * i + 1)
                    for h in range(4):
                        mm = pe.transpose(psB[0:S, 0, h * S:(h + 1) * S], P1[:, 4 * half + h, :], ident[0:S, 0:S])
                    mm.then_inc(s["b2t"], 1)

                def b2_values(i, half):
                    if half == 0:
                        pe.wait_ge(s["p1lo"], 2 * i + 2)
                        pe.wait_ge(s["xlo"], i + 1)
                    else:
                        pe.wait_ge(s["hs1lo"], 2 * i + 1)
                    for h in range(4):
                        hh = 4 * half + h
                        for j, (w, a) in enumerate(products(xs, P1T)):
                            mm = pe.matmul(psB[0:D, 0, h * S:(h + 1) * S],
                                           w[:, hh * D:(hh + 1) * D], a[:, hh, :], start=(j == 0), stop=(j == 2))
                    mm.then_inc(s["b2pv"], 1)

                def b2_scores2(i):
                    pe.wait_ge(s["hs1lo"], 2 * i + 2)
                    pe.wait_ge(s["min"], 32 * i + 32)
                    a = [[t[h // 4][:, h % 4, :] for h in range(HEADS)] for t in hs1T]

                    def high(h):
                        return pe.matmul(psB[0:S, 0, 0:2 * HT], a[0][h], Ms[:, :, :, h, :],
                                         start=(h == 0), stop=(h == HEADS - 1))

                    for h in range(HEADS - 1):
                        high(h)
                    for h in range(HEADS):
                        pe.matmul(psB[0:S, 0, 0:HT], a[1][h], Ms[:, 0, :, h, :], start=False, stop=False)
                    high(HEADS - 1).then_inc(s["b2c"], 1)

                def b2_turn2(i):
                    pe.wait_ge(s["c2norm"], i + 1)
                    pe.transpose(psB[0:ST, 0, 0:S], P2x3[:, :, :, :].rearrange("p k h t -> p (k h t)"),
                                 ident[0:S, 0:S]).then_inc(s["b2t2"], 1)

                def tile(r, j, n=128, first=False):
                    pe.wait_ge(s["clo"], 2 * r + j + 1)
                    if first:
                        pe.wait_ge(s["wolo"], FT)
                        pe.wait_ge(s["exp"], HEADS * B)
                    else:
                        pe.wait_ge(s["csum"], 2 * r + j - 1)
                    for half in range(2):
                        k = 0
                        for c in range(FT):
                            for a, w in products(hsT[j], Wo_s):
                                mm = pe.matmul(psS[j][0:n, half, 0:HW], a[:, c, 0:n], w[:, c, half * HW:(half + 1) * HW],
                                               start=(k == 0), stop=(k == 3 * FT - 1))
                                k += 1
                    mm.then_inc(s["cmm"], 1)

                def batch(i, first=False, last=False):
                    if not first:
                        context(i - 1, 2)
                    keys(i, 3)
                    if not first:
                        values(i - 1, 0)
                    scores(i, 2)
                    b2_turn(i, 0)
                    if not first:
                        context(i - 1, 3)
                    turn(i, 0, first)
                    scores(i, 3)
                    keys(i, 4)
                    turn(i, 1)
                    if not first:
                        context(i - 1, 4)
                    turn(i, 2)
                    scores(i, 4)
                    scores(i, 5)
                    b2_turn(i, 1)
                    turn(i, 3)
                    if not first:
                        context(i - 1, 5)
                    b2_values(i, 0)
                    scores(i, 6)
                    if not first:
                        values(i - 1, 1)
                    b2_values(i, 1)
                    if not last:
                        keys(i + 1, 0)
                    turn(i, 4, first)
                    scores(i, 7)
                    context(i, 0, first)
                    turn(i, 5)
                    b2_scores2(i)
                    if last:
                        tile(0, 0, first=True)
                    if not last:
                        keys(i + 1, 1)
                    turn(i, 6)
                    b2_turn2(i)
                    if not last:
                        keys(i + 1, 2)
                    turn(i, 7)
                    if not last:
                        b2_scores(i + 1, 0)
                    context(i, 1)
                    if not last:
                        scores(i + 1, 0)
                        b2_scores(i + 1, 1)
                        scores(i + 1, 1)

                for f in range(3):
                    keys(0, f, first=True)
                b2_scores(0, 0, first=True)
                scores(0, 0)
                b2_scores(0, 1)
                scores(0, 1)
                batch(0, first=True)
                with pe.Fori(1, B - 1) as i:
                    batch(i)
                batch(B - 1, last=True)
                tile(0, 1, first=True)
                context(B - 1, 2)
                tile(1, 0)
                values(B - 1, 0)
                context(B - 1, 3)
                tile(1, 1)
                context(B - 1, 4)
                tile(2, 0)
                context(B - 1, 5)
                tile(2, 1)
                values(B - 1, 1, last=True)
                with pe.Fori(3, FULL // 2) as r:
                    tile(r, 0)
                    tile(r, 1)
                tile(FULL // 2, 0, REST)

            @block.scalar
            def _(act):
                def expo(i, h, first=False):
                    act.wait_ge(s["negmax"], HEADS * i + h + 1)
                    if h >= PRING:
                        act.wait_ge(s["pt"], HEADS * i + h + 1 - PRING)
                    elif h < 2 and not first:
                        act.wait_ge(s["pt"], HEADS * i - 1 + h)
                    nc.scalar.activation(halves(P[h % PRING][0:S, 0:KEYS]), without_overlap(psS[score_slot[h]], S),
                                         ACT.Exp, bias=negmax[:, h:h + 1],
                                         accum_out=total[:, h:h + 1]).then_inc(s["exp"], 1)

                def pt_high(i, h):
                    act.wait_ge(s["pt"], HEADS * i + h + 1)
                    nc.scalar.activation(
                        PT[0][:, :, h * S:(h + 1) * S].rearrange("p (a k) n -> p a k n", a=2),
                        psT[0:KP, :, 0:3 * S].rearrange("p a (k n) -> p a k n", k=3), ACT.Copy).then_inc(s["pthi"], 1)

                def k_high(b, f, first=False):
                    act.wait_ge(s["kp"], FT * b + f + 1)
                    if f >= 2:
                        wait_lifted(act, b + 1, f=f - 2)
                    elif not first:
                        wait_lifted(act, b, f=4 - f)
                    nc.scalar.activation(halves(kT[f % 2][0][:, :]), without_overlap(keys_in(f, first), 128),
                                         ACT.Copy).then_inc(s["khi"], 1)

                def encT_high(b, c):
                    if c == 0:
                        act.wait_ge(s["rawT"], 16 * b)
                    nc.scalar.activation(eT[0][:, c, :], rawT[:, c, :], ACT.Copy).then_inc(s["encThi"], 1)

                def enc_high(b, c):
                    if c == 0:
                        act.wait_ge(s["rawN"], 16 * b + 16)
                    ks = slice(c * KQ, (c + 1) * KQ)
                    nc.scalar.activation(eN[0][:, ks, :], rawN[:, ks, :], ACT.Copy).then_inc(s["encNhi"], 1)

                def u_high(i, u):
                    act.wait_ge(s["u"], 2 * CT * i + u + 1)
                    if u == CT:
                        act.wait_ge(s["hsp"], 2 * i + 1)
                    nc.scalar.activation(UT[:, u % CT, :, 0, :], heads4(psB[:, 1, 0:RH]), ACT.Copy).then_inc(s["uhi"], 1)

                def hs_copy(i, half):
                    act.wait_ge(s["hsp"], 2 * i + half + 1)
                    act.wait_ge(s["hsout"], 32 * i + 16 * half + 1)
                    nc.scalar.activation(hs[:, :].rearrange("d (b h n) -> d b h n", b=2, h=2),
                                         hs_parts()[:, :, :, 1, :], ACT.Copy).then_inc(s["hscopy"], 1)

                def b2_exp(i):
                    act.wait_ge(s["b2sub"], 2 * i + 2)
                    nc.scalar.activation(P1[:, :, :], P1[:, :, :], ACT.Exp).then_inc(s["b2exp"], 1)

                def b2_pt_high(i, half):
                    act.wait_ge(s["b2t"], 2 * i + half + 1)
                    nc.scalar.activation(P1T[0][:, 4 * half:4 * half + 4, :].rearrange("p h j -> p (h j)"),
                                         psB[0:S, 0, 0:RH], ACT.Copy).then_inc(s["p1hi"], 1)

                def b2_hs_high(i, half):
                    act.wait_ge(s["b2pv"], 2 * i + half + 1)
                    nc.scalar.activation(hs1T[0][half], psB[0:D, 0, 0:RH].rearrange("d (h n) -> d h n", h=4), ACT.Copy).then_inc(s["hs1hi"], 1)

                def b2_exp2(i):
                    act.wait_ge(s["c2sub"], i + 1)
                    nc.scalar.activation(P2[:, :, :], P2[:, :, :], ACT.Exp).then_inc(s["b2exp2"], 1)

                def b2_pt2_high(i):
                    act.wait_ge(s["b2t2"], i + 1)
                    nc.scalar.activation(P2T[:, :], psB[0:ST, 0, 0:S], ACT.Copy).then_inc(s["p2hi"], 1)

                def wo_high(c):
                    act.wait_ge(s["woin0" if c < 3 else "woin1"], 16)
                    nc.scalar.activation(Wo_s[0][:, c, :], wo_raw(c), ACT.Copy).then_inc(s["wohi"], 1)

                def load_x(r, j, n=128):
                    act.dma_start(xin[j][0:n, :], x2[bass.ds((2 * r + j) * 128, n), :]).then_inc(s_x[j], 16)

                def high(r, j, n=128, first=False):
                    act.wait_ge(s_in[j], 16 * r + 16)
                    if first:
                        wait_lifted(act, B, f=4 - j)
                    else:
                        act.wait_ge(s["cmm"], 2 * r + j - 1)
                    nc.scalar.activation(hsT[j][0][:, :, 0:n], hsr[j][:, :, 0:n], ACT.Copy).then_inc(s["chi"], 1)

                def store(r, j, n=128):
                    act.wait_ge(s["cres"], 2 * r + j + 1)
                    act.dma_start(out2[bass.ds((2 * r + j) * 128, n), :], res[j][0:n, :]).then_inc(s_st[j], 16)

                def batch(i, first=False, last=False):
                    if not first:
                        u_high(i - 1, 2)
                    k_high(i, 3)
                    if not first:
                        hs_copy(i - 1, 0)
                    expo(i, 2)
                    b2_pt_high(i, 0)
                    if not first:
                        u_high(i - 1, 3)
                    pt_high(i, 0)
                    expo(i, 3)
                    k_high(i, 4)
                    if not last:
                        encT_high(i + 1, 0)
                    if last:
                        wo_high(0)
                    pt_high(i, 1)
                    if not last:
                        encT_high(i + 1, 1)
                    if last:
                        wo_high(1)
                    if not last:
                        encT_high(i + 1, 2)
                    if last:
                        wo_high(2)
                    if not first:
                        u_high(i - 1, 4)
                    pt_high(i, 2)
                    expo(i, 4)
                    b2_pt_high(i, 1)
                    pt_high(i, 3)
                    expo(i, 5)
                    if not first:
                        u_high(i - 1, 5)
                    enc_high(i, 0)
                    b2_hs_high(i, 0)
                    enc_high(i, 1)
                    expo(i, 6)
                    if not first:
                        hs_copy(i - 1, 1)
                    enc_high(i, 2)
                    b2_hs_high(i, 1)
                    if not last:
                        k_high(i + 1, 0)
                    if last:
                        wo_high(3)
                        wo_high(4)
                    pt_high(i, 4)
                    expo(i, 7)
                    u_high(i, 0)
                    pt_high(i, 5)
                    if last:
                        high(0, 0, first=True)
                    b2_exp2(i)
                    if not last:
                        k_high(i + 1, 1)
                    if last:
                        high(0, 1, first=True)
                    pt_high(i, 6)
                    b2_pt2_high(i)
                    if not last:
                        k_high(i + 1, 2)
                    pt_high(i, 7)
                    u_high(i, 1)
                    if not last:
                        expo(i + 1, 0)
                        b2_exp(i + 1)
                        expo(i + 1, 1)

                nc.scalar.activation(st2[:, 2, :], ident[0:S, 0:HEADS], ACT.Copy).then_inc(s["hsout"], 1)
                for f in range(3):
                    k_high(0, f, first=True)
                expo(0, 0, first=True)
                b2_exp(0)
                expo(0, 1, first=True)
                batch(0, first=True)
                with act.Fori(1, B - 1) as i:
                    batch(i)
                batch(B - 1, last=True)
                high(1, 0)
                u_high(B - 1, 2)
                high(1, 1)
                store(0, 0)
                load_x(1, 0)
                hs_copy(B - 1, 0)
                u_high(B - 1, 3)
                high(2, 0)
                store(0, 1)
                load_x(1, 1)
                u_high(B - 1, 4)
                high(2, 1)
                store(1, 0)
                load_x(2, 0)
                u_high(B - 1, 5)
                high(3, 0)
                store(1, 1)
                load_x(2, 1)
                hs_copy(B - 1, 1)
                store(2, 0)
                load_x(3, 0)
                high(3, 1)
                store(2, 1)
                load_x(3, 1)
                with act.Fori(3, FULL // 2 - 1) as r:
                    for j in range(2):
                        high(r + 1, j)
                        store(r, j)
                        load_x(r + 1, j)
                high(FULL // 2, 0, REST)
                store(FULL // 2 - 1, 0)
                load_x(FULL // 2, 0, REST)
                store(FULL // 2 - 1, 1)
                store(FULL // 2, 0, REST)
                act.wait_ge(s_st[0], 16 * (FULL // 2 + 1))
                act.wait_ge(s_st[1], 16 * (FULL // 2))

            @block.vector
            def _(dve):
                def rowmax(i, h):
                    dve.wait_ge(s["scores"], HEADS * i + h + 1)
                    nc.vector.tensor_reduce(negmax[:, h:h + 1], tile_in(h), AX.XY, ALU.max,
                                            negate=True).then_inc(s["negmax"], 1)

                def norm(i, h):
                    dve.wait_ge(s["exp"], HEADS * i + h + 1)
                    nc.vector.reciprocal(inv[:, h:h + 1], total[:, h:h + 1]).then_inc(s["inv"], 1)
                    dve.wait_ge(s["inv"], HEADS * i + h + 1)
                    nc.vector.tensor_scalar(P[h % PRING][0:S, 0:KEYS], P[h % PRING][0:S, 0:KEYS], inv[:, h:h + 1],
                                            None, ALU.mult).then_inc(s["norm"], 1)

                def pt_low(i, h):
                    dve.wait_ge(s["pthi"], HEADS * i + h + 1)
                    o = [PT[p][:, :, h * S:(h + 1) * S].rearrange("p (a k) n -> p a k n", a=2) for p in range(2)]
                    nc.vector.tensor_tensor(
                        o[1], psT[0:KP, :, 0:3 * S].rearrange("p a (k n) -> p a k n", k=3), o[0],
                        ALU.subtract).then_inc(s["ptlo"], 1)

                def hs_add(i, half):
                    dve.wait_ge(s["hscopy"], 2 * i + half + 1)
                    v = hs[:, :].rearrange("d (b h n) -> d b h n", b=2, h=2)
                    nc.vector.tensor_tensor(v, hs_parts()[:, :, :, 0, :], v, ALU.add).then_inc(s["hs"], 1)

                def k_low(b, f, first=False):
                    dve.wait_ge(s["khi"], FT * b + f + 1)
                    nc.vector.tensor_tensor(halves(kT[f % 2][1][:, :]), without_overlap(keys_in(f, first), 128),
                                            halves(kT[f % 2][0][:, :]), ALU.subtract).then_inc(s["klo"], 1)

                def u_low(i, u):
                    dve.wait_ge(s["uhi"], 2 * CT * i + u + 1)
                    nc.vector.tensor_tensor(UT[:, u % CT, :, 1, :], heads4(psB[:, 1, 0:RH]), UT[:, u % CT, :, 0, :],
                                            ALU.subtract).then_inc(s["ulo"], 1)

                def b2_less_max(i, half):
                    dve.wait_ge(s["b2s"], 2 * i + half + 1)
                    v = psB[0:S, 0, 0:RH].rearrange("p (h j) -> p h j", h=4)
                    hh = slice(4 * half, 4 * half + 4)
                    nc.vector.tensor_reduce(st1[:, 0, hh], v, AX.X, ALU.max, negate=True).then_inc(s["b2max"], 1)
                    dve.wait_ge(s["b2max"], 2 * i + half + 1)
                    nc.vector.tensor_tensor(
                        P1[:, hh, :], v, st1[:, 0, hh].rearrange("p (h o) -> p h o", o=1).to_broadcast([S, 4, S]),
                        ALU.add).then_inc(s["b2sub"], 1)

                def b2_norm(i):
                    dve.wait_ge(s["b2exp"], i + 1)
                    nc.vector.tensor_reduce(st1[:, 1, :], P1[:, :, :], AX.X, ALU.add).then_inc(s["b2sum"], 1)
                    dve.wait_ge(s["b2sum"], i + 1)
                    nc.vector.reciprocal(st1[:, 2, :], st1[:, 1, :]).then_inc(s["b2inv"], 1)
                    dve.wait_ge(s["b2inv"], i + 1)
                    nc.vector.tensor_tensor(
                        P1[:, :, :], P1[:, :, :],
                        st1[:, 2, :].rearrange("p (h o) -> p h o", o=1).to_broadcast([S, HEADS, S]),
                        ALU.mult).then_inc(s["b2norm"], 1)

                def b2_pt_low(i, half):
                    dve.wait_ge(s["p1hi"], 2 * i + half + 1)
                    o = [P1T[p][:, 4 * half:4 * half + 4, :].rearrange("p h j -> p (h j)") for p in range(2)]
                    nc.vector.tensor_tensor(o[1], psB[0:S, 0, 0:RH], o[0], ALU.subtract).then_inc(s["p1lo"], 1)

                def b2_hs_low(i, half):
                    dve.wait_ge(s["hs1hi"], 2 * i + half + 1)
                    nc.vector.tensor_tensor(hs1T[1][half], psB[0:D, 0, 0:RH].rearrange("d (h n) -> d h n", h=4), hs1T[0][half],
                                            ALU.subtract).then_inc(s["hs1lo"], 1)

                def b2_less_max2(i):
                    dve.wait_ge(s["b2c"], i + 1)
                    nc.vector.tensor_copy(P2[:, :, :], psB[0:S, 0, HT:2 * HT].rearrange("p (h t) -> p h t", h=HEADS))\
                      .then_inc(s["c2copy"], 1)
                    dve.wait_ge(s["c2copy"], i + 1)
                    nc.vector.tensor_tensor(P2[:, :, :], psB[0:S, 0, 0:HT].rearrange("p (h t) -> p h t", h=HEADS),
                                            P2[:, :, :], ALU.add).then_inc(s["c2add"], 1)
                    dve.wait_ge(s["c2add"], i + 1)
                    nc.vector.tensor_reduce(st2[:, 0, :], P2[:, :, :], AX.X, ALU.max, negate=True)\
                      .then_inc(s["c2max"], 1)
                    dve.wait_ge(s["c2max"], i + 1)
                    nc.vector.tensor_tensor(
                        P2[:, :, :], P2[:, :, :],
                        st2[:, 0, :].rearrange("p (h o) -> p h o", o=1).to_broadcast([S, HEADS, T]),
                        ALU.add).then_inc(s["c2sub"], 1)

                def b2_norm2(i):
                    dve.wait_ge(s["b2exp2"], i + 1)
                    nc.vector.tensor_reduce(st2[:, 1, :], P2[:, :, :], AX.X, ALU.add).then_inc(s["c2sum"], 1)
                    dve.wait_ge(s["c2sum"], i + 1)
                    nc.vector.reciprocal(st2[:, 2, :], st2[:, 1, :]).then_inc(s["c2inv"], 1)
                    dve.wait_ge(s["c2inv"], i + 1)
                    nc.vector.tensor_tensor(
                        P2x3[:, :, :, :], P2[:, :, :].rearrange("p (o h) t -> p o h t", o=1).to_broadcast([S, 3, HEADS, T]),
                        st2[:, 2, :].rearrange("p (o h u) -> p o h u", o=1, u=1).to_broadcast([S, 3, HEADS, T]),
                        ALU.mult).then_inc(s["c2norm"], 1)

                def b2_pt2_low(i):
                    dve.wait_ge(s["p2hi"], i + 1)
                    low = slice(HT, 2 * HT)
                    nc.vector.tensor_tensor(P2T[low, :], psB[low, 0, 0:S], P2T[low, :],
                                            ALU.subtract).then_inc(s["p2lo"], 1)

                def low(r, j, n=128):
                    dve.wait_ge(s["chi"], 2 * r + j + 1)
                    nc.vector.tensor_tensor(hsT[j][1][:, :, 0:n], hsr[j][:, :, 0:n], hsT[j][0][:, :, 0:n],
                                            ALU.subtract).then_inc(s["clo"], 1)

                def finish(r, j, n=128, first=False):
                    dve.wait_ge(s["cmm"], 2 * r + j + 1)
                    if not first:
                        dve.wait_ge(s_st[j], 16 * r)
                    v = [halves(t[0:n, 0:H]) for t in (res[j], bias, xin[j])]
                    nc.vector.tensor_tensor(v[0], psS[j][0:n, :, 0:HW], v[1], ALU.add).then_inc(s["csum"], 1)
                    dve.wait_ge(s["csum"], 2 * r + j + 1)
                    dve.wait_ge(s_x[j], 16 * r + 16)
                    nc.vector.tensor_tensor(v[0], v[0], v[2], ALU.add).then_inc(s["cres"], 1)

                def batch(i, first=False, last=False):
                    norm(i, 0)
                    b2_norm(i)
                    if not first:
                        u_low(i - 1, 2)
                    norm(i, 1)
                    k_low(i, 3)
                    if not first:
                        hs_add(i - 1, 0)
                    rowmax(i, 2)
                    b2_pt_low(i, 0)
                    if not first:
                        u_low(i - 1, 3)
                    pt_low(i, 0)
                    rowmax(i, 3)
                    norm(i, 2)
                    k_low(i, 4)
                    pt_low(i, 1)
                    norm(i, 3)
                    if not first:
                        u_low(i - 1, 4)
                    pt_low(i, 2)
                    rowmax(i, 4)
                    rowmax(i, 5)
                    b2_pt_low(i, 1)
                    pt_low(i, 3)
                    norm(i, 4)
                    if not first:
                        u_low(i - 1, 5)
                    b2_hs_low(i, 0)
                    norm(i, 5)
                    rowmax(i, 6)
                    if not first:
                        hs_add(i - 1, 1)
                    b2_hs_low(i, 1)
                    norm(i, 6)
                    if not last:
                        k_low(i + 1, 0)
                    pt_low(i, 4)
                    rowmax(i, 7)
                    u_low(i, 0)
                    pt_low(i, 5)
                    if last:
                        low(0, 0)
                    norm(i, 7)
                    b2_less_max2(i)
                    b2_norm2(i)
                    if last:
                        low(0, 1)
                    if not last:
                        k_low(i + 1, 1)
                    pt_low(i, 6)
                    b2_pt2_low(i)
                    if not last:
                        k_low(i + 1, 2)
                    pt_low(i, 7)
                    if last:
                        dve.wait_ge(s["bias"], 16)
                    if last:
                        finish(0, 0, first=True)
                    if not last:
                        b2_less_max(i + 1, 0)
                    u_low(i, 1)
                    if not last:
                        rowmax(i + 1, 0)
                        b2_less_max(i + 1, 1)
                        rowmax(i + 1, 1)

                for j in range(PRING):
                    nc.vector.memset(P[j][0:S, KEYS:KPAD], 0.0).then_inc(s["hs" if j == 0 else "ready"], 1)
                for f in range(3):
                    k_low(0, f, first=True)
                b2_less_max(0, 0)
                rowmax(0, 0)
                b2_less_max(0, 1)
                rowmax(0, 1)
                batch(0, first=True)
                with dve.Fori(1, B - 1) as i:
                    batch(i)
                batch(B - 1, last=True)
                low(1, 0)
                finish(0, 1, first=True)
                u_low(B - 1, 2)
                low(1, 1)
                finish(1, 0)
                hs_add(B - 1, 0)
                u_low(B - 1, 3)
                low(2, 0)
                finish(1, 1)
                u_low(B - 1, 4)
                low(2, 1)
                finish(2, 0)
                u_low(B - 1, 5)
                low(3, 0)
                finish(2, 1)
                hs_add(B - 1, 1)
                low(3, 1)
                with dve.Fori(3, FULL // 2 - 1) as r:
                    for j in range(2):
                        finish(r, j)
                        low(r + 1, j)
                finish(FULL // 2 - 1, 0)
                low(FULL // 2, 0, REST)
                finish(FULL // 2 - 1, 1)
                finish(FULL // 2, 0, REST)


def kernel(x, ctx_768, L0_xattn_Wq, L0_xattn_Wk, L0_xattn_Wv, L0_xattn_Wq_ca, L0_xattn_Wk_ca, L0_xattn_Wv_ca,
           L0_xattn_Wout, L0_xattn_b_out):
    import numpy as _np
    import concourse.bacc as _bacc
    from concourse import mybir as _mybir
    from concourse.bass_utils import run_bass_kernel_spmd as _run

    x = _np.asarray(x)
    ctx = _np.asarray(ctx_768)
    Wq, Wk = _np.asarray(L0_xattn_Wq), _np.asarray(L0_xattn_Wk)
    Wq_ca = _np.asarray(L0_xattn_Wq_ca)
    enc, ca = ctx[:, :KEYS], ctx[:, KEYS:]
    encN = _np.zeros((B, KPAD, C), x.dtype)
    encN[:, :KEYS] = enc
    picked = _np.linspace(0, C - 1, S).astype(_np.int64)
    wg = _np.zeros((H, HT), x.dtype)
    for h in range(HEADS):
        wg[h * D:(h + 1) * D, h * T:(h + 1) * T] = Wq_ca[:, h * D:(h + 1) * D].T
    laid = {
        "x": x,
        "xT": x.reshape(NT, H).T,
        "encT": enc.transpose(0, 2, 1),
        "encN": encN,
        "caT": ca.reshape(B * T, C).T,
        "asel": _np.tile(ca[:, :, picked], (1, 3 * HEADS, 1)),
        "Wq": Wq,
        "WqT": Wq.T,
        "Wk": Wk,
        "Wv": L0_xattn_Wv,
        "WqcaBD": wg,
        "Wkca": L0_xattn_Wk_ca,
        "Wvca": L0_xattn_Wv_ca,
        "Wout": L0_xattn_Wout,
        "bout": L0_xattn_b_out,
    }
    nc = _bacc.Bacc("TRN2", target_bir_lowering=False, num_devices=1)
    arrays, args = {}, []
    for name, a in laid.items():
        a = _np.ascontiguousarray(a)
        arrays[f"in_{name}_dram"] = a
        args.append(nc.dram_tensor(f"in_{name}_dram", a.shape, _mybir.dt.from_np(a.dtype), kind="ExternalInput").ap())
    args.append(nc.dram_tensor("out_0_dram", (B, S, H), F32, kind="ExternalOutput").ap())
    build(nc, *args)
    r = _run(nc, [arrays], core_ids=[0])
    return r.results[0]["out_0_dram"]
```
